# Optimizing a Trainium2 kernel written in Bass

```python
import numpy as np
import jax
import jax.numpy as jnp

def _softmax(x, axis=-1):
    return jax.nn.softmax(x, axis=axis)

def _gelu(x):
    return jax.nn.gelu(x, approximate=True)

def _silu(x):
    return jax.nn.silu(x)

def _sigmoid(x):
    return jax.nn.sigmoid(x)

def _layernorm(x, axis=-1, eps=1e-05):
    m = jnp.mean(x, axis=axis, keepdims=True)
    v = jnp.var(x, axis=axis, keepdims=True)
    return (x - m) / jnp.sqrt(v + eps)

def _scatter_add(tgt, idx, src, axis=0):
    return tgt.at[idx].add(src)

def _segment_sum(src, seg, n):
    return jax.ops.segment_sum(src, seg, n)
kernel_name = 'mk_adaln_attn_ffn_d2_seqx_r8_064b02'

def setup_inputs(seed: int=0):
    np.random.seed(seed)
    _w = jnp.asarray

    def _rec_inputs():
        import jax
        import jax.numpy as jnp
        _rk = jax.random.key(seed)
        x = -0.0001538 + 1 * jax.random.normal(jax.random.fold_in(_rk, 1), (64, 32, 128), jnp.float32)
        _lenS = 32 - jax.random.randint(jax.random.fold_in(_rk, 7), (64,), 0, max(1, 32 // 4) + 1, jnp.int32)
        _lenS2 = 32 - jax.random.randint(jax.random.fold_in(_rk, 8), (64,), 0, max(1, 32 // 4) + 1, jnp.int32)
        cond_1024 = 0.00782532 + 1.00527 * jax.random.normal(jax.random.fold_in(_rk, 11), (64, 128), jnp.float32)
        return (x, cond_1024)
    x, cond_1024 = _rec_inputs()

    def _L0_cond_setup():
        import jax, jax.numpy as jnp
        import numpy as np
        NUM_EXPERTS = 4
        TOP_K = 2
        key = jax.random.key(seed)
        ks = jax.random.split(key, 16)
        B, L, D, E, H = (8, 96, 128, NUM_EXPERTS, 512)
        s = 0.02
        return {'context_c': jax.random.normal(ks[0], (B, L, D), jnp.float32), 'time_cond': jax.random.normal(ks[1], (B, D), jnp.float32), 'gate_w': jax.random.normal(ks[2], (3 * D, E), jnp.float32) * s, 'gate_b': jnp.zeros((E,), jnp.float32), 'time_w': jax.random.normal(ks[3], (D, 2 * E), jnp.float32) * s, 'time_b': jnp.zeros((2 * E,), jnp.float32), 'ew1': jax.random.normal(ks[4], (E, D, H), jnp.float32) * s, 'eb1': jnp.zeros((E, H), jnp.float32), 'ew2': jax.random.normal(ks[5], (E, H, D), jnp.float32) * s, 'eb2': jnp.zeros((E, D), jnp.float32), 'sw1': jax.random.normal(ks[6], (D, H), jnp.float32) * s, 'sb1': jnp.zeros((H,), jnp.float32), 'sw2': jax.random.normal(ks[7], (H, D), jnp.float32) * s, 'sb2': jnp.zeros((D,), jnp.float32)}
    _L0_cond_all = _L0_cond_setup()
    _L0_cond_in = {k: v for k, v in _L0_cond_all.items() if k in ('gate_w', 'gate_b', 'time_w', 'time_b', 'ew1', 'eb1', 'ew2', 'eb2', 'sw1', 'sb1', 'sw2', 'sb2')}
    del _L0_cond_all

    def _L0_attn_setup():
        import jax, jax.numpy as jnp
        import numpy as np
        H, D = (8, 128)
        HID = 128
        K = 4
        EPS_QK = 1e-06
        EPS_NORM = 1e-05

        def short_conv(x, w):
            k = w.shape[-1]
            xp = jnp.pad(x, ((0, 0), (k - 1, 0), (0, 0)))
            xc = jnp.transpose(xp, (0, 2, 1))
            y = jax.lax.conv_general_dilated(xc, w, window_strides=(1,), padding='VALID', feature_group_count=w.shape[0])
            return jax.nn.silu(jnp.transpose(y, (0, 2, 1)))

        def _rmsn(t, eps):
            return t * jax.lax.rsqrt(jnp.mean(t * t, axis=-1, keepdims=True) + eps)
        key = jax.random.key(seed)
        ks = jax.random.split(key, 16)
        s = 0.02
        inp = {'x': jax.random.normal(ks[0], (2, 128, HID), dtype=jnp.float32), 'Wq': jax.random.normal(ks[1], (H * D, HID), dtype=jnp.float32) * s, 'Wk': jax.random.normal(ks[2], (H * D, HID), dtype=jnp.float32) * s, 'Wv': jax.random.normal(ks[3], (H * D, HID), dtype=jnp.float32) * s, 'wq_conv': jax.random.normal(ks[4], (H * D, 1, K), dtype=jnp.float32) * 0.3, 'wk_conv': jax.random.normal(ks[5], (H * D, 1, K), dtype=jnp.float32) * 0.3, 'wv_conv': jax.random.normal(ks[6], (H * D, 1, K), dtype=jnp.float32) * 0.3, 'Wfa': jax.random.normal(ks[7], (D, HID), dtype=jnp.float32) * s, 'Wfb': jax.random.normal(ks[8], (H * D, D), dtype=jnp.float32) * s, 'Wb': jax.random.normal(ks[9], (H, HID), dtype=jnp.float32) * s, 'Wga': jax.random.normal(ks[10], (D, HID), dtype=jnp.float32) * s, 'Wgb': jax.random.normal(ks[11], (H * D, D), dtype=jnp.float32) * s, 'A_log': jnp.log(jax.random.uniform(ks[12], (H,), minval=1.0, maxval=16.0, dtype=jnp.float32)), 'dt_bias': jnp.zeros((H, D), dtype=jnp.float32), 'o_norm_w': jnp.ones((D,), dtype=jnp.float32), 'Wo': jax.random.normal(ks[13], (HID, H * D), dtype=jnp.float32) * s}
        return inp
    _L0_attn_all = _L0_attn_setup()
    _L0_attn_in = {k: v for k, v in _L0_attn_all.items() if k in ('Wq', 'Wk', 'Wv', 'wq_conv', 'wk_conv', 'wv_conv', 'Wfa', 'Wfb', 'Wb', 'Wga', 'Wgb', 'A_log', 'dt_bias', 'o_norm_w', 'Wo')}
    del _L0_attn_all

    def _L0_cond2_setup():
        import jax, jax.numpy as jnp
        import numpy as np
        import math
        N, T, D, H = (64, 64, 128, 128)

        def lstm_forward(x, h0, Wx, Wh, b):
            Hd = h0.shape[1]
            xW = jnp.einsum('ntd,dg->ntg', x, Wx) + b
            c0 = jnp.zeros_like(h0)

            def step(carry, xw_t):
                prev_h, prev_c = carry
                a = xw_t + prev_h @ Wh
                i = jax.nn.sigmoid(a[:, :Hd])
                f = jax.nn.sigmoid(a[:, Hd:2 * Hd])
                o = jax.nn.sigmoid(a[:, 2 * Hd:3 * Hd])
                g = jnp.tanh(a[:, 3 * Hd:])
                next_c = f * prev_c + i * g
                next_h = o * jnp.tanh(next_c)
                return ((next_h, next_c), next_h)
            (_, _), hs = jax.lax.scan(step, (h0, c0), jnp.swapaxes(xW, 0, 1))
            return jnp.swapaxes(hs, 0, 1)
        key = jax.random.key(seed)
        k1, k2, k3, k4 = jax.random.split(key, 4)
        x = jax.random.normal(k1, (N, T, D), dtype=jnp.float32)
        h0 = jax.random.normal(k2, (N, H), dtype=jnp.float32)
        Wx = jax.random.normal(k3, (D, 4 * H), dtype=jnp.float32) / math.sqrt(D)
        Wh = jax.random.normal(k4, (H, 4 * H), dtype=jnp.float32) / math.sqrt(H)
        b = jnp.zeros((4 * H,), dtype=jnp.float32)
        return {'x': x, 'h0': h0, 'Wx': Wx, 'Wh': Wh, 'b': b}
    _L0_cond2_all = _L0_cond2_setup()
    _L0_cond2_in = {k: v for k, v in _L0_cond2_all.items() if k in ('Wx', 'Wh', 'b')}
    del _L0_cond2_all

    def _L0_ffn_setup():
        import jax, jax.numpy as jnp
        import numpy as np
        B, T, D, F, E = (2, 128, 128, 512, 8)
        EPS = 1e-06
        key = jax.random.key(seed)
        k = jax.random.split(key, 5)
        scale = 0.02
        return {'x': jax.random.normal(k[0], (B, T, D), dtype=jnp.float32), 'rms_w': jnp.ones((D,), dtype=jnp.float32), 'gate_w': jax.random.normal(k[1], (E, D), dtype=jnp.float32) * scale, 'W1': jax.random.normal(k[2], (E, D, F), dtype=jnp.float32) * scale, 'b1': jnp.zeros((E, F), dtype=jnp.float32), 'W2': jax.random.normal(k[3], (E, F, D), dtype=jnp.float32) * scale, 'b2': jnp.zeros((E, D), dtype=jnp.float32)}
    _L0_ffn_all = _L0_ffn_setup()
    _L0_ffn_in = {k: v for k, v in _L0_ffn_all.items() if k in ('rms_w', 'gate_w', 'W1', 'b1', 'W2', 'b2')}
    del _L0_ffn_all

    def _L1_cond_setup():
        import jax, jax.numpy as jnp
        import numpy as np
        B, T, C = (64, 64, 128)
        key = jax.random.key(seed)
        ks = jax.random.split(key, 17)
        s_in = 1.0 / np.sqrt(C)

        def lin(kw, kb, fan_in):
            s = 1.0 / np.sqrt(fan_in)
            W = jax.random.uniform(kw, (C, fan_in), jnp.float32, -s, s)
            b = jax.random.uniform(kb, (C,), jnp.float32, -s, s)
            return (W, b)
        Wxz, bxz = lin(ks[0], ks[1], C)
        Whz, bhz = lin(ks[2], ks[3], C)
        Wxr, bxr = lin(ks[4], ks[5], C)
        Whr, bhr = lin(ks[6], ks[7], C)
        Wxh, bxh = lin(ks[8], ks[9], C)
        Whh, bhh = lin(ks[10], ks[11], C)
        Whq, bhq = lin(ks[12], ks[13], C)
        X = jax.random.normal(ks[14], (B, T, C), jnp.float32)
        h0 = jax.random.normal(ks[15], (B, C), jnp.float32)
        return {'X': X, 'h0': h0, 'Wxz': Wxz, 'bxz': bxz, 'Whz': Whz, 'bhz': bhz, 'Wxr': Wxr, 'bxr': bxr, 'Whr': Whr, 'bhr': bhr, 'Wxh': Wxh, 'bxh': bxh, 'Whh': Whh, 'bhh': bhh, 'Whq': Whq, 'bhq': bhq}
    _L1_cond_all = _L1_cond_setup()
    _L1_cond_in = {k: v for k, v in _L1_cond_all.items() if k in ('Wxz', 'bxz', 'Whz', 'bhz', 'Wxr', 'bxr', 'Whr', 'bhr', 'Wxh', 'bxh', 'Whh', 'bhh', 'Whq', 'bhq')}
    del _L1_cond_all

    def _L1_attn_setup():
        import jax, jax.numpy as jnp
        import numpy as np
        B, M, D, H, K, V = (4, 256, 128, 16, 64, 64)
        key = jax.random.key(seed)
        ks = jax.random.split(key, 5)
        return {'x': jax.random.normal(ks[0], (B, M, D), dtype=jnp.float32), 'P_q': jax.random.normal(ks[1], (H, D, K), dtype=jnp.float32) * 0.02, 'P_k': jax.random.normal(ks[2], (H, D, K), dtype=jnp.float32) * 0.02, 'P_v': jax.random.normal(ks[3], (H, D, V), dtype=jnp.float32) * 0.02, 'P_o': jax.random.normal(ks[4], (H, D, V), dtype=jnp.float32) * 0.02}
    _L1_attn_all = _L1_attn_setup()
    _L1_attn_in = {k: v for k, v in _L1_attn_all.items() if k in ('P_q', 'P_k', 'P_v', 'P_o')}
    del _L1_attn_all

    def _L1_cond2_setup():
        import jax, jax.numpy as jnp
        import numpy as np
        import math
        N, T, D, H = (64, 64, 128, 128)
        key = jax.random.key(seed)
        k1, k2, k3, k4 = jax.random.split(key, 4)
        x = jax.random.normal(k1, (N, T, D), dtype=jnp.float32)
        h0 = jax.random.normal(k2, (N, H), dtype=jnp.float32)
        Wx = jax.random.normal(k3, (D, 4 * H), dtype=jnp.float32) / math.sqrt(D)
        Wh = jax.random.normal(k4, (H, 4 * H), dtype=jnp.float32) / math.sqrt(H)
        b = jnp.zeros((4 * H,), dtype=jnp.float32)
        return {'x': x, 'h0': h0, 'Wx': Wx, 'Wh': Wh, 'b': b}
    _L1_cond2_all = _L1_cond2_setup()
    _L1_cond2_in = {k: v for k, v in _L1_cond2_all.items() if k in ('Wx', 'Wh', 'b')}
    del _L1_cond2_all

    def _L1_ffn_setup():
        import jax, jax.numpy as jnp
        import numpy as np
        TOP_K = 2
        key = jax.random.key(seed)
        k0, k1, k2, k3 = jax.random.split(key, 4)
        B, T, C, E, D = (4, 256, 128, 8, 128)
        x = jax.random.normal(k0, (B, T, C), dtype=jnp.float32)
        s = 1.0 / np.sqrt(C)
        w_router = jax.random.normal(k1, (C, E), dtype=jnp.float32) * s
        w1 = jax.random.normal(k2, (E, C, D), dtype=jnp.float32) * s
        w2 = jax.random.normal(k3, (E, D, C), dtype=jnp.float32) * (1.0 / np.sqrt(D))
        return {'x': x, 'w_router': w_router, 'w1': w1, 'w2': w2}
    _L1_ffn_all = _L1_ffn_setup()
    _L1_ffn_in = {k: v for k, v in _L1_ffn_all.items() if k in ('w_router', 'w1', 'w2')}
    del _L1_ffn_all
    return {'x': x, 'cond_1024': cond_1024, 'L0_cond_gate_w': _L0_cond_in['gate_w'], 'L0_cond_gate_b': _L0_cond_in['gate_b'], 'L0_cond_time_w': _L0_cond_in['time_w'], 'L0_cond_time_b': _L0_cond_in['time_b'], 'L0_cond_ew1': _L0_cond_in['ew1'], 'L0_cond_eb1': _L0_cond_in['eb1'], 'L0_cond_ew2': _L0_cond_in['ew2'], 'L0_cond_eb2': _L0_cond_in['eb2'], 'L0_cond_sw1': _L0_cond_in['sw1'], 'L0_cond_sb1': _L0_cond_in['sb1'], 'L0_cond_sw2': _L0_cond_in['sw2'], 'L0_cond_sb2': _L0_cond_in['sb2'], 'L0_attn_Wq': _L0_attn_in['Wq'], 'L0_attn_Wk': _L0_attn_in['Wk'], 'L0_attn_Wv': _L0_attn_in['Wv'], 'L0_attn_wq_conv': _L0_attn_in['wq_conv'], 'L0_attn_wk_conv': _L0_attn_in['wk_conv'], 'L0_attn_wv_conv': _L0_attn_in['wv_conv'], 'L0_attn_Wfa': _L0_attn_in['Wfa'], 'L0_attn_Wfb': _L0_attn_in['Wfb'], 'L0_attn_Wb': _L0_attn_in['Wb'], 'L0_attn_Wga': _L0_attn_in['Wga'], 'L0_attn_Wgb': _L0_attn_in['Wgb'], 'L0_attn_A_log': _L0_attn_in['A_log'], 'L0_attn_dt_bias': _L0_attn_in['dt_bias'], 'L0_attn_o_norm_w': _L0_attn_in['o_norm_w'], 'L0_attn_Wo': _L0_attn_in['Wo'], 'L0_cond2_Wx': _L0_cond2_in['Wx'], 'L0_cond2_Wh': _L0_cond2_in['Wh'], 'L0_cond2_b': _L0_cond2_in['b'], 'L0_ffn_rms_w': _L0_ffn_in['rms_w'], 'L0_ffn_gate_w': _L0_ffn_in['gate_w'], 'L0_ffn_W1': _L0_ffn_in['W1'], 'L0_ffn_b1': _L0_ffn_in['b1'], 'L0_ffn_W2': _L0_ffn_in['W2'], 'L0_ffn_b2': _L0_ffn_in['b2'], 'L1_cond_Wxz': _L1_cond_in['Wxz'], 'L1_cond_bxz': _L1_cond_in['bxz'], 'L1_cond_Whz': _L1_cond_in['Whz'], 'L1_cond_bhz': _L1_cond_in['bhz'], 'L1_cond_Wxr': _L1_cond_in['Wxr'], 'L1_cond_bxr': _L1_cond_in['bxr'], 'L1_cond_Whr': _L1_cond_in['Whr'], 'L1_cond_bhr': _L1_cond_in['bhr'], 'L1_cond_Wxh': _L1_cond_in['Wxh'], 'L1_cond_bxh': _L1_cond_in['bxh'], 'L1_cond_Whh': _L1_cond_in['Whh'], 'L1_cond_bhh': _L1_cond_in['bhh'], 'L1_cond_Whq': _L1_cond_in['Whq'], 'L1_cond_bhq': _L1_cond_in['bhq'], 'L1_attn_P_q': _L1_attn_in['P_q'], 'L1_attn_P_k': _L1_attn_in['P_k'], 'L1_attn_P_v': _L1_attn_in['P_v'], 'L1_attn_P_o': _L1_attn_in['P_o'], 'L1_cond2_Wx': _L1_cond2_in['Wx'], 'L1_cond2_Wh': _L1_cond2_in['Wh'], 'L1_cond2_b': _L1_cond2_in['b'], 'L1_ffn_w_router': _L1_ffn_in['w_router'], 'L1_ffn_w1': _L1_ffn_in['w1'], 'L1_ffn_w2': _L1_ffn_in['w2']}

def reference(x, cond_1024, L0_cond_gate_w, L0_cond_gate_b, L0_cond_time_w, L0_cond_time_b, L0_cond_ew1, L0_cond_eb1, L0_cond_ew2, L0_cond_eb2, L0_cond_sw1, L0_cond_sb1, L0_cond_sw2, L0_cond_sb2, L0_attn_Wq, L0_attn_Wk, L0_attn_Wv, L0_attn_wq_conv, L0_attn_wk_conv, L0_attn_wv_conv, L0_attn_Wfa, L0_attn_Wfb, L0_attn_Wb, L0_attn_Wga, L0_attn_Wgb, L0_attn_A_log, L0_attn_dt_bias, L0_attn_o_norm_w, L0_attn_Wo, L0_cond2_Wx, L0_cond2_Wh, L0_cond2_b, L0_ffn_rms_w, L0_ffn_gate_w, L0_ffn_W1, L0_ffn_b1, L0_ffn_W2, L0_ffn_b2, L1_cond_Wxz, L1_cond_bxz, L1_cond_Whz, L1_cond_bhz, L1_cond_Wxr, L1_cond_bxr, L1_cond_Whr, L1_cond_bhr, L1_cond_Wxh, L1_cond_bxh, L1_cond_Whh, L1_cond_bhh, L1_cond_Whq, L1_cond_bhq, L1_attn_P_q, L1_attn_P_k, L1_attn_P_v, L1_attn_P_o, L1_cond2_Wx, L1_cond2_Wh, L1_cond2_b, L1_ffn_w_router, L1_ffn_w1, L1_ffn_w2):
    import jax
    import jax.numpy as jnp

    def _L0_cond_ref(context_c, time_cond, gate_w, gate_b, time_w, time_b, ew1, eb1, ew2, eb2, sw1, sb1, sw2, sb2):
        import jax, jax.numpy as jnp
        import numpy as np
        NUM_EXPERTS = 4
        TOP_K = 2
        B, L, D = context_c.shape
        E, K = (NUM_EXPERTS, TOP_K)
        L_head = L_wrist = L // 3
        head = context_c[:, :L_head]
        wrist = context_c[:, L_head:L_head + L_wrist]
        proprio = context_c[:, L_head + L_wrist:]
        full_agg = context_c.mean(axis=1)
        hp_agg = jnp.concatenate([head, proprio], axis=1).mean(axis=1)
        wp_agg = jnp.concatenate([wrist, proprio], axis=1).mean(axis=1)
        gate_in = jnp.concatenate([full_agg, hp_agg, wp_agg], axis=-1)
        gate_logits = gate_in @ gate_w + gate_b
        mod = jax.nn.silu(time_cond) @ time_w + time_b
        scale, shift = jnp.split(mod, 2, axis=-1)
        gate_logits = gate_logits * (1.0 + scale) + shift
        gate_scores = jax.nn.softmax(gate_logits, axis=-1)
        topk_w, topk_i = jax.lax.top_k(gate_scores, K)
        topk_w = topk_w / (topk_w.sum(axis=-1, keepdims=True) + 1e-08)
        onehot = (topk_i[..., None] == jnp.arange(E)[None, None, :]).astype(context_c.dtype)
        w_be = jnp.sum(topk_w[..., None] * onehot, axis=1)
        mask = np.ones((E, L), dtype=np.float32)
        mask[1, L_head:L_head + L_wrist] = 0.0
        mask[2, :L_head] = 0.0
        mask = jnp.asarray(mask)
        out = jnp.zeros_like(context_c)
        for e in range(E):
            h = jax.nn.gelu(context_c @ ew1[e] + eb1[e], approximate=True)
            y = h @ ew2[e] + eb2[e]
            out = out + w_be[:, e][:, None, None] * mask[e][None, :, None] * y
        shared = jax.nn.gelu(context_c @ sw1 + sb1, approximate=True) @ sw2 + sb2
        return out + shared

    def _L0_attn_ref(x, Wq, Wk, Wv, wq_conv, wk_conv, wv_conv, Wfa, Wfb, Wb, Wga, Wgb, A_log, dt_bias, o_norm_w, Wo):
        import jax, jax.numpy as jnp
        import numpy as np
        H, D = (8, 128)
        HID = 128
        K = 4
        EPS_QK = 1e-06
        EPS_NORM = 1e-05

        def short_conv(x, w):
            k = w.shape[-1]
            xp = jnp.pad(x, ((0, 0), (k - 1, 0), (0, 0)))
            xc = jnp.transpose(xp, (0, 2, 1))
            y = jax.lax.conv_general_dilated(xc, w, window_strides=(1,), padding='VALID', feature_group_count=w.shape[0])
            return jax.nn.silu(jnp.transpose(y, (0, 2, 1)))

        def _rmsn(t, eps):
            return t * jax.lax.rsqrt(jnp.mean(t * t, axis=-1, keepdims=True) + eps)
        B, T, _ = x.shape
        scale = float(D) ** (-0.5)
        q = short_conv(x @ Wq.T, wq_conv).reshape(B, T, H, D)
        k = short_conv(x @ Wk.T, wk_conv).reshape(B, T, H, D)
        v = short_conv(x @ Wv.T, wv_conv).reshape(B, T, H, D)
        q = scale ** 2 * _rmsn(q, EPS_QK)
        k = scale * _rmsn(k, EPS_QK)
        a_logits = (x @ Wfa.T @ Wfb.T).reshape(B, T, H, D)
        g = -jnp.exp(A_log)[None, None, :, None] * jax.nn.softplus(a_logits + dt_bias)
        beta = jax.nn.sigmoid(x @ Wb.T)

        def step(S, inputs):
            q_t, k_t, v_t, g_t, b_t = inputs
            S = S * jnp.exp(g_t)[..., None]
            kv = jnp.einsum('bhd,bhdv->bhv', k_t, S)
            delta = b_t[..., None] * (v_t - kv)
            S = S + k_t[..., None] * delta[:, :, None, :]
            o = jnp.einsum('bhd,bhdv->bhv', q_t, S)
            return (S, o)
        tb = lambda t: jnp.moveaxis(t, 1, 0)
        S0 = jnp.zeros((B, H, D, D), dtype=x.dtype)
        _, o_t = jax.lax.scan(step, S0, (tb(q), tb(k), tb(v), tb(g), tb(beta)))
        out = jnp.moveaxis(o_t, 0, 1)
        gate = (x @ Wga.T @ Wgb.T).reshape(B, T, H, D)
        out = _rmsn(out, EPS_NORM) * o_norm_w * jax.nn.sigmoid(gate)
        return out.reshape(B, T, H * D) @ Wo.T

    def _L0_cond2_ref(x, h0, Wx, Wh, b):
        import jax, jax.numpy as jnp
        import numpy as np
        import math
        N, T, D, H = (64, 64, 128, 128)

        def lstm_forward(x, h0, Wx, Wh, b):
            Hd = h0.shape[1]
            xW = jnp.einsum('ntd,dg->ntg', x, Wx) + b
            c0 = jnp.zeros_like(h0)

            def step(carry, xw_t):
                prev_h, prev_c = carry
                a = xw_t + prev_h @ Wh
                i = jax.nn.sigmoid(a[:, :Hd])
                f = jax.nn.sigmoid(a[:, Hd:2 * Hd])
                o = jax.nn.sigmoid(a[:, 2 * Hd:3 * Hd])
                g = jnp.tanh(a[:, 3 * Hd:])
                next_c = f * prev_c + i * g
                next_h = o * jnp.tanh(next_c)
                return ((next_h, next_c), next_h)
            (_, _), hs = jax.lax.scan(step, (h0, c0), jnp.swapaxes(xW, 0, 1))
            return jnp.swapaxes(hs, 0, 1)
        return lstm_forward(x, h0, Wx, Wh, b)

    def _L0_ffn_ref(x, rms_w, gate_w, W1, b1, W2, b2):
        import jax, jax.numpy as jnp
        import numpy as np
        B, T, D, F, E = (2, 128, 128, 512, 8)
        EPS = 1e-06
        ms = jnp.mean(x * x, axis=-1, keepdims=True)
        xn = x * jax.lax.rsqrt(ms + EPS) * rms_w
        logits = jnp.einsum('btd,ed->bte', xn, gate_w)
        scores = jax.nn.softmax(logits, axis=-1)
        top1_idx = jnp.argmax(scores, axis=-1)
        top1_score = jnp.max(scores, axis=-1)
        out = jnp.zeros_like(xn)
        for e in range(E):
            h = jax.nn.silu(jnp.einsum('btd,df->btf', xn, W1[e]) + b1[e])
            ye = jnp.einsum('btf,fd->btd', h, W2[e]) + b2[e]
            out = jnp.where((top1_idx == e)[..., None], ye, out)
        return out * top1_score[..., None]

    def _L1_cond_ref(X, h0, Wxz, bxz, Whz, bhz, Wxr, bxr, Whr, bhr, Wxh, bxh, Whh, bhh, Whq, bhq):
        import jax, jax.numpy as jnp
        import numpy as np
        B, T, C = (64, 64, 128)
        Xz = jnp.einsum('btc,hc->tbh', X, Wxz) + bxz
        Xr = jnp.einsum('btc,hc->tbh', X, Wxr) + bxr
        Xh = jnp.einsum('btc,hc->tbh', X, Wxh) + bxh

        def step(H, xs):
            xz, xr, xh = xs
            Z = jax.nn.sigmoid(xz + H @ Whz.T + bhz)
            R = jax.nn.sigmoid(xr + H @ Whr.T + bhr)
            H_tilda = jnp.tanh(xh + R * H @ Whh.T + bhh)
            H_new = Z * H + (1.0 - Z) * H_tilda
            Y = H_new @ Whq.T + bhq
            return (H_new, Y)
        _, Ys = jax.lax.scan(step, h0, (Xz, Xr, Xh))
        return jnp.transpose(Ys, (1, 0, 2))

    def _L1_attn_ref(x, P_q, P_k, P_v, P_o):
        import jax, jax.numpy as jnp
        import numpy as np
        B, M, D, H, K, V = (4, 256, 128, 16, 64, 64)
        Q = jnp.einsum('bmd,hdk->bhmk', x, P_q)
        Kt = jnp.einsum('bmd,hdk->bhmk', x, P_k)
        Vt = jnp.einsum('bmd,hdv->bhmv', x, P_v)
        scale = 1.0 / jnp.sqrt(jnp.asarray(K, dtype=x.dtype))
        logits = jnp.einsum('bhmk,bhnk->bhmn', Q, Kt) * scale
        m = logits.shape[-1]
        causal = jnp.tril(jnp.ones((m, m), dtype=bool))
        logits = jnp.where(causal[None, None], logits, jnp.asarray(-jnp.inf, dtype=logits.dtype))
        weights = jax.nn.softmax(logits, axis=-1)
        o = jnp.einsum('bhmn,bhnv->bhmv', weights, Vt)
        y = jnp.einsum('bhmv,hdv->bmd', o, P_o)
        return y

    def _L1_cond2_ref(x, h0, Wx, Wh, b):
        import jax, jax.numpy as jnp
        import numpy as np
        import math
        N, T, D, H = (64, 64, 128, 128)
        Hdim = h0.shape[1]
        xW = jnp.einsum('ntd,dg->ntg', x, Wx) + b

        def step(carry, xw_t):
            prev_h, prev_c = carry
            a = xw_t + prev_h @ Wh
            i = jax.nn.sigmoid(a[:, :Hdim])
            f = jax.nn.sigmoid(a[:, Hdim:2 * Hdim])
            o = jax.nn.sigmoid(a[:, 2 * Hdim:3 * Hdim])
            g = jnp.tanh(a[:, 3 * Hdim:])
            next_c = f * prev_c + i * g
            next_h = o * jnp.tanh(next_c)
            return ((next_h, next_c), next_h)
        c0 = jnp.zeros_like(h0)
        _, hs = jax.lax.scan(step, (h0, c0), jnp.swapaxes(xW, 0, 1))
        return jnp.swapaxes(hs, 0, 1)

    def _L1_ffn_ref(x, w_router, w1, w2):
        import jax, jax.numpy as jnp
        import numpy as np
        TOP_K = 2
        B, T, C = x.shape
        xf = x.reshape(-1, C)
        logits = xf @ w_router
        top_vals, top_idx = jax.lax.top_k(logits, TOP_K)
        probs = jax.nn.softmax(top_vals, axis=-1)
        h = jnp.square(jax.nn.relu(jnp.einsum('nc,ecd->ned', xf, w1)))
        y_all = jnp.einsum('ned,edc->nec', h, w2)
        y_sel = jnp.take_along_axis(y_all, top_idx[:, :, None], axis=1)
        out = jnp.sum(y_sel * probs[:, :, None], axis=1)
        return out.reshape(B, T, C)
    x = x + _L0_attn_ref(_L0_cond_ref(x, cond_1024, L0_cond_gate_w, L0_cond_gate_b, L0_cond_time_w, L0_cond_time_b, L0_cond_ew1, L0_cond_eb1, L0_cond_ew2, L0_cond_eb2, L0_cond_sw1, L0_cond_sb1, L0_cond_sw2, L0_cond_sb2), L0_attn_Wq, L0_attn_Wk, L0_attn_Wv, L0_attn_wq_conv, L0_attn_wk_conv, L0_attn_wv_conv, L0_attn_Wfa, L0_attn_Wfb, L0_attn_Wb, L0_attn_Wga, L0_attn_Wgb, L0_attn_A_log, L0_attn_dt_bias, L0_attn_o_norm_w, L0_attn_Wo)
    x = x + _L0_ffn_ref(_L0_cond2_ref(x, cond_1024, L0_cond2_Wx, L0_cond2_Wh, L0_cond2_b), L0_ffn_rms_w, L0_ffn_gate_w, L0_ffn_W1, L0_ffn_b1, L0_ffn_W2, L0_ffn_b2)
    x = x + _L1_attn_ref(_L1_cond_ref(x, cond_1024, L1_cond_Wxz, L1_cond_bxz, L1_cond_Whz, L1_cond_bhz, L1_cond_Wxr, L1_cond_bxr, L1_cond_Whr, L1_cond_bhr, L1_cond_Wxh, L1_cond_bxh, L1_cond_Whh, L1_cond_bhh, L1_cond_Whq, L1_cond_bhq), L1_attn_P_q, L1_attn_P_k, L1_attn_P_v, L1_attn_P_o)
    x = x + _L1_ffn_ref(_L1_cond2_ref(x, cond_1024, L1_cond2_Wx, L1_cond2_Wh, L1_cond2_b), L1_ffn_w_router, L1_ffn_w1, L1_ffn_w2)
    return x

_drawn_inputs = setup_inputs


def setup_inputs(seed=0):
    import zlib

    import numpy as np

    out = dict(_drawn_inputs(seed))
    spreads = {'L0_cond_gate_b': (0.0, 0.8),
     'L0_cond_time_b': (0.0, 0.8),
     'L0_cond_eb1': (0.0, 0.8),
     'L0_cond_eb2': (0.0, 0.8),
     'L0_cond_sb1': (0.0, 0.8),
     'L0_cond_sb2': (0.0, 0.8),
     'L0_attn_dt_bias': (0.0, 0.8),
     'L0_attn_o_norm_w': (1.0, 0.6),
     'L0_cond2_b': (0.0, 0.72),
     'L0_ffn_rms_w': (1.0, 0.6),
     'L0_ffn_b1': (0.0, 0.8),
     'L0_ffn_b2': (0.0, 0.439),
     'L1_cond2_b': (0.0, 2.0)}
    factors = {'cond_1024': 3.234,
     'L0_cond_gate_w': 8.0,
     'L0_cond_time_w': 8.0,
     'L0_cond_ew1': 8.0,
     'L0_cond_ew2': 8.0,
     'L0_cond_sw1': 8.0,
     'L0_cond_sw2': 8.0,
     'L0_attn_Wq': 8.0,
     'L0_attn_Wk': 8.0,
     'L0_attn_Wv': 8.0,
     'L0_attn_wq_conv': 8.0,
     'L0_attn_wk_conv': 8.0,
     'L0_attn_wv_conv': 8.0,
     'L0_attn_Wfa': 8.0,
     'L0_attn_Wfb': 8.0,
     'L0_attn_Wb': 8.0,
     'L0_attn_Wga': 8.0,
     'L0_attn_Wgb': 8.0,
     'L0_attn_A_log': 8.0,
     'L0_attn_Wo': 8.0,
     'L0_cond2_Wx': 2.863,
     'L0_cond2_Wh': 5.01,
     'L0_ffn_gate_w': 2.892,
     'L0_ffn_W1': 5.557,
     'L0_ffn_W2': 5.137,
     'L1_cond_Wxz': 8.0,
     'L1_cond_bxz': 8.0,
     'L1_cond_Whz': 8.0,
     'L1_cond_bhz': 8.0,
     'L1_cond_Wxr': 8.0,
     'L1_cond_bxr': 8.0,
     'L1_cond_Whr': 8.0,
     'L1_cond_bhr': 8.0,
     'L1_cond_Wxh': 4.729,
     'L1_cond_bxh': 8.0,
     'L1_cond_Whh': 8.0,
     'L1_cond_bhh': 8.0,
     'L1_cond_Whq': 2.895,
     'L1_cond_bhq': 6.339,
     'L1_attn_P_q': 8.0,
     'L1_attn_P_k': 8.0,
     'L1_attn_P_v': 2.698,
     'L1_attn_P_o': 2.73,
     'L1_cond2_Wh': 8.949}
    for name, (base, spread) in spreads.items():
        noise = np.random.default_rng([zlib.crc32(name.encode()), seed]).standard_normal(out[name].shape)
        drawn = base * np.exp(spread * noise) if base else spread * noise
        out[name] = jnp.asarray(drawn.astype(out[name].dtype))
    for name, factor in factors.items():
        out[name] = (out[name] * factor).astype(out[name].dtype)
    return out
```

```python
from contextlib import ExitStack

import numpy as np

import concourse.bass as bass
from concourse import mybir

F32 = mybir.dt.float32
U8 = mybir.dt.uint8
ALU = mybir.AluOpType
ACT = mybir.ActivationFunctionType
AX = mybir.AxisListType

B, T, D = 64, 32, 128
N = B * T
P = 128
TILE = 512
TILES = N // TILE
GROUPS = N // P
HEADS = 8
ds = bass.ds


class Moe:

    def __init__(self, name, experts, chunks, biases, plain_first, before=None):
        self.name, self.E, self.C = name, experts, chunks
        self.biases, self.plain_first = biases, plain_first
        self.w2 = chunks * P
        self.b1 = 2 * chunks * P
        self.b2 = self.b1 + chunks
        self.width = 2 * chunks * P + (chunks + 1 if biases else 0)
        self.peeled = 1 if plain_first else 0
        self.pairs = (experts - self.peeled) // 2
        self.units0 = 4 * before.E + before.units0 if before else 0
        self.chunks0 = 4 * before.E * before.C + before.chunks0 if before else 0
        self.loads0 = [before.loads0[k] + 16 * before.loads(k) if before else 0 for k in range(2)]
        self.gates0 = [before.gates0[k] + 16 * (before.loads(k) - (before.plain_first and k == 0)) if before else 0
                       for k in range(2)]

    def loads(self, slot):
        return len(range(slot, self.E, 2))


MIX = Moe("mix", 5, 4, True, True)
MOE_A = Moe("moe_a", 8, 4, True, False, MIX)
MOE_B = Moe("moe_b", 8, 1, False, False, MOE_A)


def wait(engine, semaphore, value):
    if not isinstance(value, int) or value > 0:
        engine.wait_ge(semaphore, value)


def build(nc, a, out):
    scratch = {
        "mix_gate": nc.dram_tensor("mix_gate", [4, N], F32, kind="Internal").ap(),
        "moe_a_gate": nc.dram_tensor("moe_a_gate", [GROUPS, 8, P], F32, kind="Internal").ap(),
        "moe_b_gate": nc.dram_tensor("moe_b_gate", [GROUPS, 8, P], F32, kind="Internal").ap(),
        "values": nc.dram_tensor("values", [HEADS, P, N], F32, kind="Internal").ap(),
        "reads": nc.dram_tensor("reads", [HEADS, P, N], F32, kind="Internal").ap(),
        "systems": nc.dram_tensor("systems", [HEADS, B, T * T], F32, kind="Internal").ap(),
        "inverses": nc.dram_tensor("inverses", [HEADS, B, T * T], F32, kind="Internal").ap(),
        "row_scales": nc.dram_tensor("row_scales", [2, HEADS * B, T], F32, kind="Internal").ap(),
    }
    with ExitStack() as ctx:
        def sbuf(name, shape, dtype=F32):
            return ctx.enter_context(nc.sbuf_tensor(name, shape, dtype))

        def sem(name):
            return ctx.enter_context(nc.semaphore(name))

        arena = sbuf("arena", [P, 24, N])
        bank = [ctx.enter_context(nc.psum_tensor(f"bank{i}", [P, TILE], F32)) for i in range(8)]

        def tok(i):
            return arena[:, i, :]

        residual = tok(0)

        ident = sbuf("ident", [P, P])
        ones = sbuf("ones", [P, P])
        earlier = sbuf("earlier", [P, 8, 8])
        ident_mask = sbuf("ident_mask", [P, P], U8)
        level_mask = sbuf("level_mask", [P, 5, 64], U8)
        mask_work = tok(23)[:, 0:6 * P].rearrange("p (m n) -> p m n", n=P)
        s_carrier = sem("wait_carrier")
        s_const = sem("constants_made")
        s_const_copy = sem("constants_cast")
        CONST = 2 + 3 + 10

        cond = sbuf("cond", [P, B])
        gate_in = sbuf("gate_in", [P, 20])
        gate_rows = sbuf("gate_rows", [1, 12])
        s_x = sem("x_loaded")
        s_gate_in = sem("gate_inputs_loaded")

        block = ctx.enter_context(nc.Block())
        programs = {"sync": [], "tensor": [], "scalar": [], "vector": [], "gpsimd": []}

        def settled(engine):
            engine.sem_inc(s_carrier, 1)

        def stage(engine):
            def add(f):
                programs[engine].append(f)
                return f
            return add

        @stage("gpsimd")
        def _(pool):
            pool.memset(ones[:, :], 1.0).then_inc(s_const, 1)
            pool.memset(mask_work[:, :, :], 1.0).then_inc(s_const, 1)
            pool.wait_ge(s_const, 2)
            pool.affine_select(out=ident[:, :], in_=ones[:, :], compare_op=ALU.is_equal, fill=0.0,
                               base=0, pattern=[[-1, P]], channel_multiplier=1).then_inc(s_const, 1)
            pool.affine_select(out=earlier[:, :, :], in_=ones[:, 0:64].rearrange("p (e j) -> p e j", j=8),
                               compare_op=ALU.is_gt, fill=0.0, base=0, pattern=[[1, 8], [-1, 8]],
                               channel_multiplier=0).then_inc(s_const, 1)
            pool.affine_select(out=mask_work[:, 5, :], in_=ones[:, :], compare_op=ALU.is_equal, fill=0.0,
                               base=0, pattern=[[-1, P]], channel_multiplier=1).then_inc(s_const, 1)
            for level in range(5):
                half = 1 << level
                work = mask_work[:, level, 0:64].rearrange("p (c r) -> p c r", r=half)
                src = ones[:, 0:64].rearrange("p (c r) -> p c r", r=half)
                pool.affine_select(out=work, in_=src, compare_op=ALU.is_ge, fill=0.0, base=0,
                                   pattern=[[-2 * half, 64 // half], [0, half]],
                                   channel_multiplier=1).then_inc(s_const, 1)
                pool.wait_ge(s_const, 2 + 3 + 2 * level + 1)
                pool.affine_select(out=work, in_=work, compare_op=ALU.is_ge, fill=0.0, base=half - 1,
                                   pattern=[[2 * half, 64 // half], [0, half]],
                                   channel_multiplier=-1).then_inc(s_const, 1)

        @stage("vector")
        def _(dve):
            dve.wait_ge(s_const, CONST)
            dve.tensor_copy(ident_mask[:, :], mask_work[:, 5, :]).then_inc(s_const_copy, 1)
            dve.tensor_copy(level_mask[:, :, :], mask_work[:, 0:5, 0:64]).then_inc(s_const_copy, 1)

        @stage("sync")
        def _(sp):
            sp.dma_start(residual, a["x"]).then_inc(s_x, 16)
            sp.dma_start(cond[:, :], a["cond"]).then_inc(s_gate_in, 16)
            sp.dma_start(gate_in[:, :], a["gate_in"]).then_inc(s_gate_in, 16)
            sp.dma_start(gate_rows[:, :], a["gate_rows"]).then_inc(s_gate_in, 16)

        mixture_semaphores = (
            [sem(f"mixture_weights_loaded{k}") for k in range(2)],
            [sem(f"mixture_gate_spread{k}") for k in range(2)],
            sem("mixture_hidden_ready"),
            sem("mixture_relu_done"),
            sem("mixture_activated"),
            sem("mixture_expert_out_ready"),
            sem("mixture_gated"),
            sem("mixture_added"),
        )

        def moe(m, src, acc, hidden, spread, weights, work, hidden_act, w_dram, spread_src,
                src_ready, gates_ready, gate_hooks=None):
            C = m.C
            (s_w, s_g, s_h, s_r, s_a, s_y, s_c, s_acc) = mixture_semaphores
            U0, Q0 = m.units0, m.chunks0
            hid = [tok(i).rearrange("p (c n) -> p c n", n=TILE) for i in hidden]
            spr = [tok(i) for i in spread]
            wgt = [tok(i) for i in weights]
            tmp = [tok(work)[:, k * TILE:(k + 1) * TILE] for k in range(2)]
            squared = hidden_act == "relu2"
            rel = [tok(work)[:, (2 + k) * TILE:(3 + k) * TILE] for k in range(2)]
            loops = m.pairs

            def tile_of(array, n):
                return array[:, n * TILE:(n + 1) * TILE]

            @stage("sync")
            def _(sp):
                ready_waited = False
                for e in range(m.E):
                    if e >= 2:
                        sp.wait_ge(s_c, U0 + 4 * (e - 1))
                    if e == 0:
                        sp.wait_ge(*src_ready)
                    sp.dma_start(wgt[e % 2][:, 0:m.width], w_dram[e]).then_inc(s_w[e % 2], 16)
                    if not (m.plain_first and e == 0):
                        if not ready_waited:
                            sp.wait_ge(*gates_ready)
                            ready_waited = True
                        rows = spread_src(e - m.peeled)
                        dst = spr[e % 2] if len(rows.shape) == 2 else spr[e % 2].rearrange("p (g n) -> p g n", n=P)
                        sp.dma_start(dst, rows).then_inc(s_g[e % 2], 16)

            def body_units(i, count):
                if count == 1:
                    return [(0, 0, 0, n) for n in range(4)]
                return [(i, i * 2 + m.peeled + k, m.peeled + k, n) for k in range(2) for n in range(4)]

            def run(engine, body, after_peeled=None):
                if m.peeled:
                    body(0, 1)
                    if after_peeled:
                        after_peeled(engine)
                    first = 0
                else:
                    body(0, 2)
                    first = 1
                with engine.Fori(first, loops) as i:
                    body(i, 2)

            @stage("tensor")
            def _(pe):
                pe.wait_ge(*src_ready)

                def up(i, e, k, n):
                    s, u = k % 2, e * 4 + (n + U0)
                    if n == 0:
                        pe.wait_ge(s_w[s], i * 16 + ((k // 2 + 1) * 16 + m.loads0[s]))
                    for c in range(C):
                        q = e * 4 * C + (n * C + c + Q0)
                        wait(pe, s_a, q - 3)
                        pe.matmul(bank[(k * 4 * C + n * C + c) % 4][:, :], wgt[s][:, c * P:(c + 1) * P],
                                  tile_of(src, n), start=True, stop=True).then_inc(s_h, 1)

                def down(i, e, k, n):
                    s, u = k % 2, e * 4 + (n + U0)
                    wait(pe, s_c, u - 1)
                    for c in range(C):
                        pe.wait_ge(s_a, e * 4 * C + (n * C + c + Q0 + 1))
                        mm = pe.matmul(bank[4 + n % 2][:, :], wgt[s][:, m.w2 + c * P:m.w2 + (c + 1) * P],
                                       hid[n % 2][:, c, :], start=(c == 0), stop=(c == C - 1))
                    mm.then_inc(s_y, 1)

                def body(i, count):
                    units = body_units(i, count)
                    up(*units[0])
                    for j, unit in enumerate(units):
                        if j + 1 < len(units):
                            up(*units[j + 1])
                        down(*unit)

                run(pe, body, gate_hooks and gate_hooks["tensor"])

            @stage("scalar")
            def _(act):
                def body(i, count):
                    for i, e, k, n in body_units(i, count):
                        s, u = k % 2, e * 4 + (n + U0)
                        wait(act, s_y, u - 1)
                        for c in range(C):
                            q = e * 4 * C + (n * C + c + Q0)
                            act.wait_ge(s_h, q + 1)
                            src_bank = bank[(k * 4 * C + n * C + c) % 4][:, :]
                            dst = hid[n % 2][:, c, :]
                            if squared:
                                act.activation(rel[n % 2], src_bank, ACT.Relu).then_inc(s_r, 1)
                                act.wait_ge(s_r, q + (1 - Q0))
                                act.activation(dst, rel[n % 2], ACT.Square).then_inc(s_a, 1)
                            else:
                                act.activation(dst, src_bank, hidden_act,
                                               bias=wgt[s][:, m.b1 + c:m.b1 + c + 1]).then_inc(s_a, 1)

                run(act, body, gate_hooks and gate_hooks["scalar"])

            @stage("vector")
            def _(dve):
                def body(i, count):
                    for i, e, k, n in body_units(i, count):
                        s, u = k % 2, e * 4 + (n + U0)
                        b2 = wgt[s][:, m.b2:m.b2 + 1] if m.biases else 0.0
                        dve.wait_ge(s_y, u + 1)
                        if m.plain_first and count == 1:
                            dve.tensor_scalar(tile_of(acc, n), bank[4 + n % 2][:, :], b2, None,
                                              ALU.add).then_inc(s_c, 1)
                            dve.wait_ge(s_c, u + 1)
                            dve.sem_inc(s_acc, 1)
                            continue
                        if n == 0:
                            dve.wait_ge(s_g[s], i * 16 + (16 + m.gates0[s]))
                        wait(dve, s_acc, u - 1)
                        dve.scalar_tensor_tensor(out=tmp[n % 2], in0=bank[4 + n % 2][:, :], scalar=b2,
                                                 in1=tile_of(spr[s], n), op0=ALU.add,
                                                 op1=ALU.mult).then_inc(s_c, 1)
                        dve.wait_ge(s_c, u + 1)
                        dve.tensor_tensor(tile_of(acc, n), tile_of(acc, n), tmp[n % 2],
                                          ALU.add).then_inc(s_acc, 1)

                run(dve, body, gate_hooks and gate_hooks["vector"])

            return s_acc, U0 + 4 * m.E

        def ranks(dve, sem_steps, base, scores, wide_a, wide_b, rank, G, E):
            shape = [scores.shape[0], G, E, E]
            mine = scores.unsqueeze(3).to_broadcast(shape)
            other = scores.unsqueeze(2).to_broadcast(shape)
            tri = earlier[0:scores.shape[0], 0:E, 0:E].unsqueeze(1).to_broadcast(shape)
            dve.tensor_tensor(wide_a, other, mine, ALU.is_gt).then_inc(sem_steps, 1)
            dve.tensor_tensor(wide_b, other, mine, ALU.is_equal).then_inc(sem_steps, 1)
            dve.wait_ge(sem_steps, base + 2)
            dve.tensor_tensor(wide_b, wide_b, tri, ALU.mult).then_inc(sem_steps, 1)
            dve.wait_ge(sem_steps, base + 3)
            dve.tensor_tensor(wide_a, wide_a, wide_b, ALU.add).then_inc(sem_steps, 1)
            dve.wait_ge(sem_steps, base + 4)
            dve.tensor_reduce(rank, wide_a, AX.X, ALU.add).then_inc(sem_steps, 1)
            return base + 5

        E4 = 4
        seg = sbuf("segment_sums", [P, 3, B])
        agg = sbuf("aggregates", [P, 3, B])
        silu_cond = sbuf("silu_cond", [P, B])
        gsm = sbuf("gate_small", [B, 64])
        gwide = sbuf("gate_wide", [B, 2, 16])
        gmask = sbuf("gate_by_token", [B, E4, T])
        s_seg = sem("mix_segments_summed")
        s_agg = sem("mix_aggregates_ready")
        s_silu = sem("mix_condition_silu")
        s_glog = sem("mix_gate_logits")
        s_gst = sem("mix_gate_steps")
        s_gexp = sem("mix_gate_exp")
        s_gtok = sem("mix_gate_by_token")
        s_gdram = sem("mix_gate_stored")
        H3 = T // 3

        @stage("vector")
        def _(dve):
            dve.wait_ge(s_x, 16)
            x3 = residual.rearrange("p (b t) -> p b t", t=T)
            for k, (lo, hi) in enumerate([(0, H3), (H3, 2 * H3), (2 * H3, T)]):
                dve.tensor_reduce(seg[:, k, :], x3[:, :, lo:hi], AX.X, ALU.add).then_inc(s_seg, 1)
            dve.wait_ge(s_seg, 3)
            head, wrist, proprio = (seg[:, k, :] for k in range(3))
            dve.tensor_tensor(agg[:, 1, :], head, proprio, ALU.add).then_inc(s_seg, 1)
            dve.tensor_tensor(agg[:, 2, :], wrist, proprio, ALU.add).then_inc(s_seg, 1)
            dve.wait_ge(s_seg, 5)
            dve.tensor_tensor(agg[:, 0, :], agg[:, 1, :], wrist, ALU.add).then_inc(s_seg, 1)
            dve.wait_ge(s_seg, 6)
            for k, size in enumerate([T, T - H3, T - H3]):
                dve.tensor_scalar(agg[:, k, :], agg[:, k, :], 1.0 / size, None, ALU.mult).then_inc(s_agg, 1)

        @stage("scalar")
        def _(act):
            act.wait_ge(s_gate_in, 48)
            act.activation(silu_cond[:, :], cond[:, :], ACT.Silu).then_inc(s_silu, 1)

        def mix_gate_tensor(pe):
            pe.wait_ge(s_agg, 3)
            pe.wait_ge(s_silu, 1)
            pe.wait_ge(s_const, CONST)
            pe.wait_ge(s_gate_in, 48)
            for k in range(3):
                pe.matmul(bank[6][0:B, 0:4], agg[:, k, :], gate_in[:, 4 * k:4 * k + 4],
                          start=(k == 0), stop=False)
            pe.matmul(bank[6][0:B, 0:4], ones[0:1, 0:B], gate_rows[:, 0:4], start=False, stop=True)
            pe.matmul(bank[7][0:B, 0:8], silu_cond[:, :], gate_in[:, 12:20], start=True, stop=False)
            pe.matmul(bank[7][0:B, 0:8], ones[0:1, 0:B], gate_rows[:, 4:12], start=False,
                      stop=True).then_inc(s_glog, 1)

        def mix_gate_scalar(act):
            act.wait_ge(s_gst, 4)
            act.activation(gsm[:, 24:28], gsm[:, 16:20], ACT.Exp, bias=gsm[:, 20:21],
                           accum_out=gsm[:, 28:29]).then_inc(s_gexp, 1)

        def mix_gate_vector(dve):
            mod, scaled, logits, neg_max = gsm[:, 0:8], gsm[:, 8:12], gsm[:, 16:20], gsm[:, 20:21]
            exps, total, inverse = gsm[:, 24:28], gsm[:, 28:29], gsm[:, 29:30]
            scores, rank, kept = gsm[:, 32:36], gsm[:, 36:40], gsm[:, 40:44]
            kept_sum, kept_inverse, gate = gsm[:, 44:45], gsm[:, 45:46], gsm[:, 48:52]
            n = 0

            def step(instruction):
                nonlocal n
                instruction.then_inc(s_gst, 1)
                n += 1
                dve.wait_ge(s_gst, n)

            dve.wait_ge(s_glog, 1)
            step(dve.tensor_copy(mod, bank[7][0:B, 0:8]))
            step(dve.scalar_tensor_tensor(out=scaled, in0=mod[:, 0:4], scalar=1.0, in1=bank[6][0:B, 0:4],
                                          op0=ALU.add, op1=ALU.mult))
            step(dve.tensor_tensor(logits, scaled, mod[:, 4:8], ALU.add))
            step(dve.tensor_reduce(neg_max, logits, AX.X, ALU.max, negate=True))
            dve.wait_ge(s_gexp, 1)
            step(dve.reciprocal(inverse, total))
            step(dve.tensor_scalar(scores, exps, inverse, None, ALU.mult))
            n = ranks(dve, s_gst, n, scores.unsqueeze(1),
                      gwide[:, 0, :].rearrange("p (g e j) -> p g e j", g=1, e=4),
                      gwide[:, 1, :].rearrange("p (g e j) -> p g e j", g=1, e=4),
                      rank.unsqueeze(1), 1, E4)
            dve.wait_ge(s_gst, n)
            step(dve.scalar_tensor_tensor(out=kept, in0=rank, scalar=1.5, in1=scores, op0=ALU.is_lt, op1=ALU.mult))
            step(dve.tensor_reduce(kept_sum, kept, AX.X, ALU.add))
            step(dve.tensor_scalar(kept_sum, kept_sum, 1e-8, None, ALU.add))
            step(dve.reciprocal(kept_inverse, kept_sum))
            step(dve.tensor_scalar(gate, kept, kept_inverse, None, ALU.mult))
            step(dve.tensor_copy(gmask[:, :, :], gate.unsqueeze(2).to_broadcast([B, E4, T])))
            dve.memset(gmask[:, 1, H3:2 * H3], 0.0).then_inc(s_gtok, 1)
            dve.memset(gmask[:, 2, 0:H3], 0.0).then_inc(s_gtok, 1)

        mixed = tok(1)

        @stage("gpsimd")
        def _(pool):
            pool.wait_ge(s_gtok, 2)
            pool.dma_start(scratch["mix_gate"].rearrange("e (b t) -> b e t", t=T),
                           gmask[:, :, :]).then_inc(s_gdram, 16)
            pool.wait_ge(s_gdram, 16)

        s_mix, MIX_ADDS = moe(
            MIX, residual, mixed, hidden=(2, 3), spread=(4, 5), weights=(6, 7), work=8,
            hidden_act=ACT.Gelu_apprx_tanh, w_dram=a["mix_w"],
            spread_src=lambda e: scratch["mix_gate"][e, :].partition_broadcast(P),
            src_ready=(s_x, 16), gates_ready=(s_gdram, 16),
            gate_hooks={"tensor": mix_gate_tensor, "scalar": mix_gate_scalar, "vector": mix_gate_vector})

        s_out = sem("result_stored")

        def finish(array, semaphore, value):
            @stage("sync")
            def _(sp):
                sp.wait_ge(semaphore, value)
                sp.dma_start(out, array).then_inc(s_out, 16)
                sp.wait_ge(s_out, 16)

        decay_low, gate_low = tok(2), tok(3)
        decay = arena[:, 4:12, :]
        low_w = tok(22)[:, 0:2 * P + HEADS]
        head_cols = sbuf("head_columns", [P, 2 * HEADS])
        neg_rate = sbuf("negative_rate", [P, HEADS])
        beta = sbuf("beta", [P, GROUPS, HEADS])
        fb_w = [tok(22)[:, (3 + k) * P:(4 + k) * P] for k in range(2)]
        s_low_w = sem("low_rank_weights_loaded")
        s_low = sem("low_rank_ready")
        s_low_copied = sem("low_rank_copied")
        s_rate = sem("rate_ready")
        s_fb = [sem(f"decay_weights_loaded{k}") for k in range(2)]
        s_dl = sem("decay_logits_ready")
        s_abs = sem("decay_abs_done")
        s_relu = sem("decay_relu_done")
        s_expu = sem("decay_exp_done")
        s_ln = sem("decay_log_done")
        s_poly = sem("decay_series_steps")
        s_sp = sem("softplus_ready")
        s_decay = sem("decay_ready")
        POLY = 6

        def dtile(array, n):
            return array[:, n * TILE:(n + 1) * TILE]

        @stage("sync")
        def _(sp):
            sp.dma_start(low_w, a["low_w"]).then_inc(s_low_w, 16)
            sp.dma_start(head_cols[:, :], a["head_cols"]).then_inc(s_low_w, 16)
            for k in range(2):
                sp.dma_start(fb_w[k], a["fb_w"][k]).then_inc(s_fb[k], 16)
            with sp.Fori(1, HEADS // 2) as i:
                for k in range(2):
                    sp.wait_ge(s_dl, i * 8 + (4 * k - 4))
                    sp.dma_start(fb_w[k], a["fb_w"][ds(i * 2 + k, 1)].rearrange("a p n -> p (a n)")).then_inc(s_fb[k], 16)

        @stage("tensor")
        def _(pe):
            pe.wait_ge(s_mix, MIX_ADDS)
            pe.wait_ge(s_low_w, 32)
            for half in range(2):
                for n in range(TILES):
                    pe.matmul(bank[half * 4 + n][:, :], low_w[:, half * P:(half + 1) * P], dtile(mixed, n),
                              start=True, stop=True).then_inc(s_low, 1)
            pe.wait_ge(s_low_copied, 5)
            for g in range(GROUPS):
                mm = pe.matmul(bank[4][:, g * HEADS:(g + 1) * HEADS], mixed[:, g * P:(g + 1) * P],
                               low_w[:, 2 * P:2 * P + HEADS], start=(g == 0), stop=(g == GROUPS - 1), skip_group_check=True)
            mm.then_inc(s_low, 1)
            pe.wait_ge(s_low_copied, 9)

            def body(i):
                for k in range(2):
                    pe.wait_ge(s_fb[k], (i + 1) * 16)
                    for n in range(TILES):
                        wait(pe, s_relu, i * 8 + (4 * k + n + 1 - 8))
                        pe.matmul(bank[4 * k + n][:, :], fb_w[k], dtile(decay_low, n),
                                  start=True, stop=True).then_inc(s_dl, 1)
            body(0)
            with pe.Fori(1, HEADS // 2) as i:
                body(i)

        @stage("scalar")
        def _(act):
            for q in range(8):
                act.wait_ge(s_low, q + 1)
                act.activation(dtile(decay_low if q < 4 else gate_low, q % 4), bank[q][:, :],
                               ACT.Copy).then_inc(s_low_copied, 1)
            act.wait_ge(s_low, 9)
            act.activation(beta[:, :, :], bank[4][:, 0:GROUPS * HEADS].rearrange("p (g h) -> p g h", h=HEADS),
                           ACT.Sigmoid).then_inc(s_low_copied, 1)
            act.wait_ge(s_low_w, 32)
            act.activation(neg_rate[:, :], head_cols[:, HEADS:2 * HEADS], ACT.Exp).then_inc(s_rate, 1)

            def body(i):
                for k in range(2):
                    U, R, L = tok(12 + k), tok(14 + k), tok(16 + k)
                    wait(act, s_decay, i * 2 + (k - 1))
                    dt = head_cols[:, ds(i * 2 + k, 1)] if not isinstance(i, int) else head_cols[:, 2 * i + k:2 * i + k + 1]
                    for n in range(TILES):
                        act.wait_ge(s_dl, i * 8 + (4 * k + n + 1))
                        settled(act)
                        act.activation(dtile(U, n), bank[4 * k + n][:, :], ACT.Abs, bias=dt).then_inc(s_abs, 1)
                        act.activation(dtile(R, n), bank[4 * k + n][:, :], ACT.Relu, bias=dt).then_inc(s_relu, 1)
                    act.wait_ge(s_abs, i * 8 + (4 * k + 4))
                    act.activation(U, U, ACT.Exp, scale=-1.0).then_inc(s_expu, 1)
                for k in range(2):
                    U, L = tok(12 + k), tok(16 + k)
                    act.wait_ge(s_expu, i * 2 + (k + 1))
                    act.activation(L, U, ACT.Ln, bias=1.0).then_inc(s_ln, 1)
                for k in range(2):
                    R = tok(14 + k)
                    act.wait_ge(s_sp, i * 2 + (k + 1))
                    rate = neg_rate[:, ds(i * 2 + k, 1)] if not isinstance(i, int) else neg_rate[:, 2 * i + k:2 * i + k + 1]
                    dst = decay[:, ds(i * 2 + k, 1), :].rearrange("p a n -> p (a n)") if not isinstance(i, int) else decay[:, 2 * i + k, :]
                    settled(act)
                    act.activation(dst, R, ACT.Exp, scale=rate).then_inc(s_decay, 1)
            act.preload_act_table_set("natural_log_exp_and_others")
            act.wait_ge(s_rate, 2)
            body(0)
            with act.Fori(1, HEADS // 2) as i:
                body(i)

        @stage("vector")
        def _(dve):
            dve.wait_ge(s_rate, 1)
            dve.tensor_scalar(neg_rate[:, :], neg_rate[:, :], -1.0, None, ALU.mult).then_inc(s_rate, 1)

            def body(i):
                for k in range(2):
                    U, R, L, Q = tok(12 + k), tok(14 + k), tok(16 + k), tok(18 + k)
                    small = tok(20 + k)[:, 0:N // 4].bitcast(U8)
                    at = i * (2 * POLY) + k * POLY
                    dve.wait_ge(s_expu, i * 2 + (k + 1))
                    dve.tensor_scalar(Q, U, -0.25, 1.0 / 3.0, ALU.mult, ALU.add).then_inc(s_poly, 1)
                    dve.tensor_scalar(small, U, 2.0 ** -5, None, ALU.is_lt).then_inc(s_poly, 1)
                    dve.wait_ge(s_poly, at + 1)
                    dve.tensor_tensor(Q, Q, U, ALU.mult).then_inc(s_poly, 1)
                    dve.wait_ge(s_poly, at + 3)
                    dve.scalar_tensor_tensor(out=Q, in0=Q, scalar=-0.5, in1=U, op0=ALU.add,
                                             op1=ALU.mult).then_inc(s_poly, 1)
                    dve.wait_ge(s_poly, at + 4)
                    dve.scalar_tensor_tensor(out=Q, in0=Q, scalar=1.0, in1=U, op0=ALU.add,
                                             op1=ALU.mult).then_inc(s_poly, 1)
                    dve.wait_ge(s_ln, i * 2 + (k + 1))
                    dve.wait_ge(s_poly, at + 5)
                    settled(dve)
                    dve.copy_predicated(L, small, Q).then_inc(s_poly, 1)
                    dve.wait_ge(s_poly, at + 6)
                    dve.wait_ge(s_relu, i * 8 + (4 * k + 4))
                    dve.tensor_tensor(R, R, L, ALU.add).then_inc(s_sp, 1)
            body(0)
            with dve.Fori(1, HEADS // 2) as i:
                body(i)

        q_tok, k_tok, v_tok = tok(12), tok(13), tok(14)
        in_left = tok(15)
        right_qk = [tok(16), tok(17)]
        left_k = [tok(18), tok(19)]
        kk_gram, qk_gram = tok(20), tok(21)
        v_rows, squares = tok(22), tok(23)
        qkv_w = sbuf("qkv_weights", [P, 3 * P + 12])
        dots = sbuf("square_sums", [P, HEADS, 2 * GROUPS])
        s_gz = sem("gram_arrays_cleared")
        s_qw = sem("qkv_weights_loaded")
        s_pj = sem("projection_ready")
        s_tap = sem("conv_current_tap_done")
        s_cstep = sem("conv_inner_taps_done")
        s_conv = sem("conv_done")
        s_silu_h = sem("qkv_activated")
        s_vt = sem("value_rows_transposed")
        s_vev = sem("value_rows_copied")
        s_sq = sem("squares_ready")
        s_dot = sem("square_sums_ready")
        s_dotc = sem("square_sums_copied")
        s_prod = sem("decayed_operands_ready")
        s_left = sem("left_products_steps")
        s_right = sem("right_products_updated")
        s_gm = sem("gram_products_ready")
        s_pq = sem("qk_blocks_kept")
        s_pk = sem("gram_banks_kept")
        s_vout = sem("values_stored")
        s_aout = sem("reads_stored")
        s_nout = sem("systems_stored")
        HALVES = [1, 2, 4, 8, 16]

        def at_head(array, h):
            return array[h] if isinstance(h, int) else array[ds(h, 1)].squeeze(0)

        def decay_of(h):
            return decay[:, h, :] if isinstance(h, int) else decay[:, ds(h, 1), :].squeeze(1)

        def halves(array, half):
            v = array.rearrange("p (c w) -> p c w", w=2 * half)
            return v[:, :, 0:half], v[:, :, half:2 * half]

        def compact(array, part, half):
            v = array.rearrange("p (g x m) -> p g x m", g=GROUPS, x=2)[:, :, part, :]
            return v.rearrange("p g (c r) -> p g c r", r=half)

        def grouped(view):
            return view.rearrange("p (g c) r -> p g c r", g=GROUPS)

        def heads_loop(engine, body):
            body(0)
            with engine.Fori(1, HEADS) as h:
                body(h)

        @stage("sync")
        def _(sp):
            sp.dma_start(qkv_w[:, :], a["qkv_w"][0]).then_inc(s_qw, 16)

            def store(h, last):
                if not last:
                    sp.wait_ge(s_conv, h * 12 + 12)
                    nxt = a["qkv_w"][h + 1] if isinstance(h, int) else a["qkv_w"][ds(h + 1, 1)].squeeze(0)
                    sp.dma_start(qkv_w[:, :], nxt).then_inc(s_qw, 16)
                sp.wait_ge(s_vev, h * 4 + 4)
                sp.dma_start(at_head(scratch["values"], h), v_rows).then_inc(s_vout, 16)
                sp.wait_ge(s_pq, h * 20 + 20)
                sp.wait_ge(s_pk, h * 24 + 24)
                sp.dma_start(at_head(scratch["reads"], h), qk_gram).then_inc(s_aout, 16)
                for q in range(4):
                    rows = slice(T * q, T * q + T)
                    src = kk_gram.rearrange("p (g i) -> p g i", i=P)[rows, :, rows]
                    dst = at_head(scratch["systems"], h).rearrange("(g q) (j i) -> q j g i", q=4, i=T)[q]
                    sp.dma_start(dst, src).then_inc(s_nout, 16)
            with sp.Fori(0, HEADS - 1) as h:
                store(h, False)
            store(HEADS - 1, True)

        @stage("tensor")
        def _(pe):
            def body(h):
                pe.wait_ge(s_qw, h * 16 + 16)
                if isinstance(h, int):
                    pe.wait_ge(s_decay, HEADS)
                for u in range(12):
                    m, n = u // 4, u % 4
                    if u < 4:
                        wait(pe, s_vev, h * 4)
                        wait(pe, s_dotc, h * 2)
                    else:
                        pe.wait_ge(s_conv, h * 12 + (u - 3))
                    pe.matmul(bank[u % 4][:, :], qkv_w[:, m * P:(m + 1) * P], dtile(mixed, n), start=True,
                              stop=True).then_inc(s_pj, 1)

                def gram(level):
                    half = HALVES[level - 1] if level else 0
                    if level == 0:
                        pe.wait_ge(s_silu_h, h * 3 + 2)
                    else:
                        pe.wait_ge(s_prod, h * 14 + (3 * level - 1))
                    for b in range(4):
                        prior = h * 24 + (4 * (level - 1) + b + 1)
                        wait(pe, s_pk, prior)
                        for g in range(4 * b, 4 * b + 4):
                            cols = slice(g * P, (g + 1) * P)
                            left = (k_tok if level < 2 else left_k[level % 2])[:, cols]
                            moving = (q_tok if level == 0 else right_qk[level % 2])[:, cols]
                            mm = pe.matmul(bank[4 + b][:, (g % 4) * P:(g % 4 + 1) * P], left, moving,
                                           start=True, stop=True, skip_group_check=True)
                        mm.then_inc(s_gm, 1)

                def sums(which):
                    pe.wait_ge(s_vev, h * 4 + (which + 1))
                    pe.wait_ge(s_sq, h * 2 + (which + 1))
                    for g in range(GROUPS):
                        mm = pe.matmul(bank[which][:, g:g + 1], squares[:, g * P:(g + 1) * P], ones[:, 0:1],
                                       start=True, stop=True, skip_group_check=True)
                    mm.then_inc(s_dot, 1)

                gram(0)
                gram(1)
                pe.wait_ge(s_silu_h, h * 3 + 3)
                for n in range(TILES):
                    for j in range(4):
                        g = 4 * n + j
                        mm = pe.transpose(bank[n][:, j * P:(j + 1) * P], v_tok[:, g * P:(g + 1) * P], ident[:, :])
                    mm.then_inc(s_vt, 1)
                sums(0)
                gram(2)
                sums(1)
                gram(3)
                gram(4)
                gram(5)
            heads_loop(pe, body)

        @stage("scalar")
        def _(act):
            act.preload_act_table(ACT.Silu)

            def body(h):
                def taps(m):
                    for n in range(TILES):
                        act.wait_ge(s_pj, h * 12 + (4 * m + n + 1))
                        if m == 0 and n == 0:
                            wait(act, s_prod, h * 14)
                        act.activation(dtile((q_tok, k_tok, v_tok)[m], n), bank[n][:, :], ACT.Copy,
                                       scale=qkv_w[:, 3 * P + 4 * m + 3:3 * P + 4 * m + 4]).then_inc(s_tap, 1)

                def silu(m):
                    act.wait_ge(s_conv, h * 12 + (4 * m + 4))
                    x = (q_tok, k_tok, v_tok)[m]
                    act.activation(x, x, ACT.Silu).then_inc(s_silu_h, 1)

                taps(0)
                taps(1)
                silu(0)
                taps(2)
                silu(1)
                silu(2)
                act.wait_ge(s_silu_h, h * 3 + 3)
                wait(act, s_dot, h * 2)
                act.activation(squares, k_tok, ACT.Square).then_inc(s_sq, 1)
                wait(act, s_vout, h * 16)
                for n in range(TILES):
                    act.wait_ge(s_vt, h * 4 + (n + 1))
                    act.activation(dtile(v_rows, n), bank[n][:, :], ACT.Copy).then_inc(s_vev, 1)
                for which in range(2):
                    act.wait_ge(s_dot, h * 2 + (which + 1))
                    if which == 0:
                        act.activation(squares, q_tok, ACT.Square).then_inc(s_sq, 1)
                    dst = dots[:, h, which * 16:which * 16 + 16] if isinstance(h, int) \
                        else dots[:, ds(h, 1), which * 16:which * 16 + 16].squeeze(1)
                    settled(act)
                    act.activation(dst, bank[which][:, 0:GROUPS], ACT.Copy).then_inc(s_dotc, 1)
            heads_loop(act, body)

        @stage("gpsimd")
        def _(pool):
            pool.wait_ge(s_decay, HEADS)
            pool.memset(kk_gram, 0.0).then_inc(s_gz, 1)
            pool.memset(qk_gram, 0.0).then_inc(s_gz, 1)
            pool.memset(left_k[0], 0.0).then_inc(s_gz, 1)
            pool.memset(left_k[1], 0.0).then_inc(s_gz, 1)

            def body(h):
                right = decay_of(h)
                wait(pool, s_prod, h * 14)
                settled(pool)
                pool.memset(in_left, 1.0).then_inc(s_left, 1)
                pool.wait_ge(s_left, h * 5 + 1)
                settled(pool)
                pool.tensor_copy(halves(in_left, 1)[0], halves(right, 1)[1]).then_inc(s_left, 1)
                for level in range(1, 5):
                    half = HALVES[level - 1]
                    left_end = halves(right, half)[0][:, :, half - 1:half]
                    right_end = halves(right, half)[1][:, :, half - 1:half]
                    shape = [P, N // (2 * half), half]
                    if level >= 2:
                        pool.wait_ge(s_prod, h * 14 + (3 * level - 3))
                        pool.wait_ge(s_left, h * 5 + level)
                        settled(pool)
                        lo = halves(in_left, half)[0]
                        pool.tensor_tensor(lo, lo, right_end.to_broadcast(shape), ALU.mult).then_inc(s_left, 1)
                    pool.wait_ge(s_prod, h * 14 + (3 * level - 1))
                    pool.wait_ge(s_left, h * 5 + level + 1)
                    settled(pool)
                    hi = halves(right, half)[1]
                    pool.tensor_tensor(hi, hi, left_end.to_broadcast(shape), ALU.mult).then_inc(s_right, 1)
                    pool.wait_ge(s_right, h * 4 + level)
            heads_loop(pool, body)

        @stage("vector")
        def _(dve):
            dve.wait_ge(s_gz, 4)

            def body(h):
                right = decay_of(h)
                for u in range(12):
                    m, n = u // 4, u % 4
                    dst = dtile((q_tok, k_tok, v_tok)[m], n).rearrange("p (b t) -> p b t", t=T)
                    src = bank[u % 4][:, :].rearrange("p (b t) -> p b t", t=T)
                    dve.wait_ge(s_tap, h * 12 + (u + 1))
                    for back in range(1, 4):
                        tap = qkv_w[:, 3 * P + 4 * m + 3 - back:3 * P + 4 * m + 4 - back]
                        if back > 1:
                            dve.wait_ge(s_cstep, h * 24 + (2 * u + back - 1))
                        ins = dve.scalar_tensor_tensor(out=dst[:, :, back:T], in0=src[:, :, 0:T - back], scalar=tap,
                                                       in1=dst[:, :, back:T], op0=ALU.mult, op1=ALU.add)
                        ins.then_inc(s_conv if back == 3 else s_cstep, 1)

                def products(level):
                    half = HALVES[level - 1]
                    ring = level % 2
                    if level == 1:
                        dve.wait_ge(s_silu_h, h * 3 + 2)
                        wait(dve, s_gm, h * 24)
                    else:
                        dve.wait_ge(s_gm, h * 24 + (4 * (level - 1)))
                        dve.wait_ge(s_left, h * 5 + level)
                        dve.tensor_tensor(halves(left_k[ring], half)[0], halves(k_tok, half)[0],
                                          halves(in_left, half)[0], ALU.mult).then_inc(s_prod, 1)
                        dve.wait_ge(s_right, h * 4 + (level - 1))
                    settled(dve)
                    factor = grouped(halves(right, half)[1])
                    for part, x in enumerate((q_tok, k_tok)):
                        dve.tensor_tensor(compact(right_qk[ring], part, half), grouped(halves(x, half)[1]), factor,
                                          ALU.mult).then_inc(s_prod, 1)

                def keep(level):
                    for b in range(4):
                        dve.wait_ge(s_gm, h * 24 + (4 * level + b + 1))
                        if b == 0 and level == 0:
                            wait(dve, s_aout, h * 16)
                            settled(dve)
                        if b == 0 and level == 1:
                            wait(dve, s_nout, h * 64)
                        settled(dve)
                        if level == 0:
                            out_v = qk_gram.rearrange("p (g i) -> p g i", i=P)[:, 4 * b:4 * b + 4, :]
                            data = bank[4 + b][:, :].rearrange("p (g i) -> p g i", i=P)
                            mask = ident_mask[:, :].unsqueeze(1).to_broadcast([P, 4, P])
                            dve.copy_predicated(out_v, mask, data).then_inc(s_pk, 1)
                            continue
                        half = HALVES[level - 1]
                        c = 64 // half
                        data = bank[4 + b][:, :].rearrange("p (g x c r) -> p g x c r", g=4, x=2, r=half)
                        mask = level_mask[:, level - 1, :].rearrange("p (c r) -> p c r", r=half).unsqueeze(1) \
                            .to_broadcast([P, 4, c, half])
                        for part, dst in enumerate((qk_gram, kk_gram)):
                            out_v = dst.rearrange("p (g c w) -> p g c w", g=GROUPS, w=2 * half)[
                                :, 4 * b:4 * b + 4, :, half:2 * half]
                            dve.copy_predicated(out_v, mask, data[:, :, part]).then_inc((s_pq, s_pk)[part], 1)

                products(1)
                keep(0)
                for level in range(2, 6):
                    products(level)
                    keep(level - 1)
                keep(5)
            heads_loop(dve, body)

        SEQ_TILES = HEADS * B // P
        PAD = T * (T + 1)
        flat = arena.rearrange("p a n -> p (a n)")
        system = flat[:, 4 * N:4 * N + SEQ_TILES * PAD].rearrange("p (s m) -> p s m", m=PAD)
        inverse = flat[:, 7 * N:7 * N + SEQ_TILES * PAD].rearrange("p (s m) -> p s m", m=PAD)
        products = flat[:, 10 * N:12 * N]
        half_out = flat[:, 4 * N + SEQ_TILES * PAD:4 * N + SEQ_TILES * PAD + 256]
        norm_work = sbuf("norm_work", [P, HEADS, 2 * GROUPS])
        gamma_kappa = sbuf("gamma_kappa", [P, 2, HEADS, GROUPS])
        q_norm2 = sbuf("q_norm_squared", [P, HEADS, GROUPS])
        gk_rows = sbuf("gamma_kappa_rows", [P, 2, P])
        row_scale = sbuf("row_scales_by_sequence", [P, 2, SEQ_TILES, T])
        s_nw = sem("norms_steps")
        s_kn = sem("k_norm_root")
        s_gkt = sem("gamma_kappa_transposed")
        s_gkc = sem("gamma_kappa_copied")
        s_rsd = sem("row_scales_stored")
        s_rs = sem("row_scales_loaded")
        s_sys = [sem(f"system_loaded{s}") for s in range(SEQ_TILES)]
        s_inv0 = sem("inverse_cleared")
        s_solve = sem("solve_steps")
        s_inv = sem("inverse_ready")
        s_invd = sem("inverses_stored")
        EPS_QK = 1e-6

        @stage("vector")
        def _(dve):
            dve.wait_ge(s_dotc, 2 * HEADS)
            dve.tensor_scalar(norm_work[:, :, :], dots[:, :, :], D * EPS_QK, None, ALU.add).then_inc(s_nw, 1)
            dve.wait_ge(s_nw, 1)
            dve.reciprocal(norm_work[:, :, :], norm_work[:, :, :]).then_inc(s_nw, 1)
            dve.wait_ge(s_nw, 2)
            by_head = beta[:, :, :].rearrange("p g h -> p h g")
            dve.tensor_tensor(gamma_kappa[:, 0], norm_work[:, :, 0:GROUPS], by_head, ALU.mult).then_inc(s_nw, 1)
            dve.tensor_scalar(q_norm2[:, :, :], norm_work[:, :, GROUPS:2 * GROUPS], 1.0 / D, None,
                              ALU.mult).then_inc(s_nw, 1)
            dve.wait_ge(s_kn, 1)
            dve.tensor_tensor(gamma_kappa[:, 1], gamma_kappa[:, 1], by_head, ALU.mult).then_inc(s_nw, 1)

        @stage("scalar")
        def _(act):
            act.wait_ge(s_nw, 2)
            act.activation(gamma_kappa[:, 1], norm_work[:, :, 0:GROUPS], ACT.Sqrt).then_inc(s_kn, 1)
            for x in range(2):
                act.wait_ge(s_gkt, x + 1)
                act.activation(gk_rows[:, x, :], bank[x][:, 0:P], ACT.Copy).then_inc(s_gkc, 1)

        @stage("tensor")
        def _(pe):
            for x in range(2):
                pe.wait_ge(s_nw, 3 + 2 * x)
                pe.transpose(bank[x][:, 0:P], gamma_kappa[:, x].rearrange("p h g -> p (h g)"),
                             ident[:, :]).then_inc(s_gkt, 1)

        @stage("sync")
        def _(sp):
            for s in range(SEQ_TILES):
                if s == 0:
                    sp.wait_ge(s_nout, 64 * HEADS)
                    sp.wait_ge(s_prod, 14 * HEADS)
                src = scratch["systems"].rearrange("(s h) b m -> s (h b) m", s=SEQ_TILES)[s]
                sp.dma_start(system[:, s, 0:T * T], src).then_inc(s_sys[s], 16)
                if s == 0:
                    sp.wait_ge(s_gkc, 2)
                    for x in range(2):
                        sp.dma_start(scratch["row_scales"][x].rearrange("(m q) t -> m (q t)", q=4),
                                     gk_rows[:, x, :]).then_inc(s_rsd, 16)
                    sp.wait_ge(s_rsd, 32)
                    for x in range(2):
                        sp.dma_start(row_scale[:, x],
                                     scratch["row_scales"][x].rearrange("(s p) t -> p s t", p=P)).then_inc(s_rs, 16)

        @stage("gpsimd")
        def _(pool):
            pool.wait_ge(s_left, 5 * HEADS)
            pool.wait_ge(s_right, 4 * HEADS)
            pool.wait_ge(s_prod, 14 * HEADS)
            pool.memset(inverse[:, :, :], 0.0).then_inc(s_inv0, 1)
            pool.wait_ge(s_inv0, 1)
            pool.memset(inverse.rearrange("p s (k w) -> p s k w", w=T + 1)[:, :, :, 0:1], 1.0).then_inc(s_inv0, 1)

        @stage("vector")
        def _(dve):
            dve.wait_ge(s_rs, 32)
            dve.wait_ge(s_inv0, 2)

            def solve_tile(s, first):
                steps = 0
                a_t = system[:, ds(s, 1), :].squeeze(1)
                x_t = inverse[:, ds(s, 1), :].squeeze(1)

                def wait_steps():
                    if first is not None:
                        dve.wait_ge(s_solve, first + steps)
                        settled(dve)

                def block(array, half, rows, cols):
                    off = cols * half * T + rows * half
                    v = array.rearrange("p (k w) -> p k w", w=2 * half * (T + 1))[:, :, off:off + half * T]
                    return v.rearrange("p k (j x) -> p k j x", x=T)[:, :, :, 0:half]

                def emit(f):
                    nonlocal steps
                    if first is not None:
                        f().then_inc(s_solve, 1)
                    steps += 1

                full = a_t[:, 0:T * T].rearrange("p (j i) -> p j i", i=T)
                gamma = row_scale[:, 0, ds(s, 1), :].to_broadcast([P, T, T])
                emit(lambda: dve.tensor_tensor(full, full, gamma, ALU.mult))
                wait_steps()
                emit(lambda: dve.tensor_scalar(block(x_t, 1, 1, 0), block(a_t, 1, 1, 0), -1.0, None, ALU.mult))
                for half in (2, 4, 8, 16):
                    nb = T // (2 * half)
                    size = half * half
                    for second in range(2):
                        wait_steps()
                        if second:
                            left = half_out[:, 0:nb * size].rearrange("p (k j a) -> p k j a", k=nb, j=half)
                            right = block(x_t, half, 1, 1)
                            result, negate = block(x_t, half, 1, 0), True
                        else:
                            left = block(x_t, half, 0, 0)
                            right = block(a_t, half, 1, 0)
                            result = half_out[:, 0:nb * size].rearrange("p (k j a) -> p k j a", k=nb, j=half)
                            negate = False
                        if half <= 4:
                            for c in range(half):
                                dst = products[:, c * nb * size:(c + 1) * nb * size].rearrange(
                                    "p (k j i) -> p k j i", k=nb, j=half)
                                emit(lambda: dve.tensor_tensor(
                                    dst, left[:, :, :, c:c + 1].to_broadcast([P, nb, half, half]),
                                    right[:, :, c:c + 1, :].to_broadcast([P, nb, half, half]), ALU.mult))
                            summed = products[:, 0:half * nb * size].rearrange(
                                "p (c k j i) -> p k j i c", c=half, k=nb, j=half)
                        else:
                            for k in range(nb):
                                dst = products[:, k * half * size:(k + 1) * half * size].rearrange(
                                    "p (j i c) -> p j i c", j=half, i=half)
                                emit(lambda: dve.tensor_tensor(
                                    dst, left[:, k].unsqueeze(2).to_broadcast([P, half, half, half]),
                                    right[:, k].rearrange("p c i -> p i c").unsqueeze(1)
                                    .to_broadcast([P, half, half, half]), ALU.mult))
                            summed = products[:, 0:half * nb * size].rearrange(
                                "p (k j i c) -> p k j i c", c=half, k=nb, j=half)
                        wait_steps()
                        emit(lambda: dve.tensor_reduce(result, summed, AX.X, ALU.add, negate=negate))
                wait_steps()
                kappa = row_scale[:, 1, ds(s, 1), :].squeeze(1).unsqueeze(2).to_broadcast([P, T, T])
                x_full = x_t[:, 0:T * T].rearrange("p (j i) -> p j i", i=T)
                if first is not None:
                    dve.tensor_tensor(x_full, x_full, kappa, ALU.mult).then_inc(s_inv, 1)
                return steps

            STEPS = 2 + sum(2 * (half + 1 if half <= 4 else T // (2 * half) + 1) for half in (2, 4, 8, 16))
            with dve.Fori(0, SEQ_TILES) as s:
                for k in range(1):
                    settled(dve)
                    dve.wait_ge(s_sys[0], 16)
                    dve.wait_ge(s_sys[1], 16)
                    dve.wait_ge(s_sys[2], 16)
                    dve.wait_ge(s_sys[3], 16)
                    assert solve_tile(s, s * STEPS) == STEPS

        inv_diag = [tok(12), tok(13)]
        reads_in = [tok(14), tok(15)]
        values_in = [tok(1), tok(2)]
        outputs = arena[:, 16:24, :]
        delta = flat[:, 7 * N + SEQ_TILES * PAD:7 * N + SEQ_TILES * PAD + 3 * TILE].rearrange("p (r n) -> p r n", n=TILE)
        square_scrap = flat[:, 7 * N - P:7 * N]
        out_sq = sbuf("output_square_sums", [P, HEADS, GROUPS])
        s_ivz = sem("inverse_diagonals_cleared")
        s_ri = [sem(f"read_inputs_loaded{k}") for k in range(2)]
        s_dp = sem("deltas_ready")
        s_dc = sem("deltas_copied")
        s_op = sem("outputs_ready")
        s_oc = sem("outputs_copied")
        s_osq = sem("outputs_squared")

        @stage("gpsimd")
        def _(pool):
            pool.wait_ge(s_conv, 12 * HEADS)
            pool.wait_ge(s_gm, 24 * HEADS)
            pool.wait_ge(s_sq, 2 * HEADS)
            for k in range(2):
                pool.memset(inv_diag[k], 0.0).then_inc(s_ivz, 1)

        @stage("sync")
        def _(sp):
            def pair(i):
                for k in range(2):
                    if isinstance(i, int):
                        sp.wait_ge(s_ivz, 2)
                        sp.wait_ge(s_vout, 16 * HEADS)
                        sp.wait_ge(s_aout, 16 * HEADS)
                        sp.wait_ge(s_conv, 12 * HEADS)
                    else:
                        sp.wait_ge(s_oc, i * 8 + (4 * k - 4))
                    sp.dma_start(reads_in[k], at_head(scratch["reads"], i * 2 + k)).then_inc(s_ri[k], 16)
                    sp.dma_start(values_in[k], at_head(scratch["values"], i * 2 + k)).then_inc(s_ri[k], 16)
                sp.wait_ge(s_inv, i + 1)
                stored = at_head(scratch["inverses"].rearrange("(s h) b m -> s (h b) m", s=SEQ_TILES), i)
                sp.dma_start(stored, inverse[:, ds(i, 1), 0:T * T].squeeze(1)).then_inc(s_invd, 16)
                sp.wait_ge(s_invd, i * 16 + 16)
                for k in range(2):
                    for q in range(4):
                        rows = slice(T * q, T * q + T)
                        dst = inv_diag[k].rearrange("p (g i) -> p g i", i=P)[rows, :, rows]
                        src = at_head(scratch["inverses"], i * 2 + k).rearrange("(g q) (j i) -> q j g i", q=4, i=T)[q]
                        sp.dma_start(dst, src).then_inc(s_ri[k], 16)
            pair(0)
            with sp.Fori(1, SEQ_TILES) as i:
                pair(i)

        @stage("tensor")
        def _(pe):
            def body(h):
                for k in range(2):
                    pe.wait_ge(s_ri[k], h * 48 + 96)
                    if isinstance(h, int):
                        pe.wait_ge(s_gkc, 2)
                    at = h * 4 + 4 * k

                    def deltas(n):
                        wait(pe, s_dc, at + (n - 1))
                        for j in range(4):
                            cols = slice((4 * n + j) * P, (4 * n + j + 1) * P)
                            mm = pe.matmul(bank[n % 2][:, j * P:(j + 1) * P], inv_diag[k][:, cols],
                                           values_in[k][:, cols], start=True, stop=True, skip_group_check=True)
                        mm.then_inc(s_dp, 1)

                    deltas(0)
                    for n in range(TILES):
                        if n + 1 < TILES:
                            deltas(n + 1)
                        pe.wait_ge(s_dc, at + (n + 1))
                        wait(pe, s_oc, at + (n - 1))
                        for j in range(4):
                            cols = slice((4 * n + j) * P, (4 * n + j + 1) * P)
                            mm = pe.matmul(bank[2 + n % 2][:, j * P:(j + 1) * P], reads_in[k][:, cols],
                                           delta[:, n % 2, j * P:(j + 1) * P], start=True, stop=True,
                                           skip_group_check=True)
                        mm.then_inc(s_op, 1)
            body(0)
            with pe.Fori(1, HEADS // 2) as i:
                body(i * 2)

        @stage("scalar")
        def _(act):
            def body(h):
                for k in range(2):
                    at = h * 4 + 4 * k
                    for n in range(TILES):
                        act.wait_ge(s_dp, at + (n + 1))
                        wait(act, s_op, at + (n - 1))
                        act.activation(delta[:, n % 2, :], bank[n % 2][:, :], ACT.Copy).then_inc(s_dc, 1)
                        if n >= 1:
                            out_tile(h, k, n - 1)
                    out_tile(h, k, TILES - 1)

            def out_tile(h, k, n):
                at = h * 4 + 4 * k
                o_h = outputs[:, h + k, :] if isinstance(h, int) else outputs[:, ds(h + k, 1), :].squeeze(1)
                act.wait_ge(s_op, at + (n + 1))
                for j in range(4):
                    g = 4 * n + j
                    acc = out_sq[:, h + k, g:g + 1] if isinstance(h, int) else out_sq[:, ds(h + k, 1), g:g + 1].squeeze(1)
                    settled(act)
                    wait(act, s_osq, h * 16 + (16 * k + g))
                    settled(act)
                    act.activation(square_scrap, bank[2 + n % 2][:, j * P:(j + 1) * P], ACT.Square,
                                   accum_out=acc).then_inc(s_osq, 1)
                act.activation(dtile(o_h, n), bank[2 + n % 2][:, :], ACT.Copy).then_inc(s_oc, 1)
            body(0)
            with act.Fori(1, HEADS // 2) as i:
                body(i * 2)


        merge_w = [sbuf(f"merge_weights{k}", [P, 2 * P]) for k in range(2)]
        out_norm = sbuf("output_norm_weight", [P, 1])
        out_scale = sbuf("output_scales", [P, HEADS, GROUPS])
        gates = [tok(4), tok(5)]
        gated = [tok(8), tok(9)]
        heads_out = [tok(10), tok(11)]
        s_mw = [sem(f"merge_weights_loaded{k}") for k in range(2)]
        s_onw = sem("output_norm_weight_loaded")
        s_osc = sem("output_scale_steps")
        s_oroot = sem("output_scale_root")
        s_gt = sem("gate_logits_ready")
        s_gs = sem("gate_ready")
        s_gd = sem("gated_outputs_ready")
        s_ot = sem("gated_outputs_transposed")
        s_ots = sem("gated_outputs_scaled")
        s_wo = sem("merge_products_ready")
        s_merged = sem("residual_updated")
        EPS_OUT = 1e-5

        @stage("sync")
        def _(sp):
            sp.dma_start(out_norm[:, :], a["out_norm"]).then_inc(s_onw, 16)
            for k in range(2):
                sp.dma_start(merge_w[k][:, :], a["merge_w"][k]).then_inc(s_mw[k], 16)
            with sp.Fori(1, HEADS // 2) as i:
                h = i * 2
                for k in range(2):
                    sp.wait_ge(s_wo, h * 4 + (4 * k - 4))
                    sp.dma_start(merge_w[k][:, :], at_head(a["merge_w"], h + k)).then_inc(s_mw[k], 16)

        @stage("vector")
        def _(dve):
            dve.wait_ge(s_osq, 16 * HEADS)
            dve.wait_ge(s_nw, 5)
            dve.scalar_tensor_tensor(out=out_scale[:, :, :], in0=out_sq[:, :, :], scalar=1.0 / D,
                                     in1=q_norm2[:, :, :], op0=ALU.mult, op1=ALU.mult).then_inc(s_osc, 1)
            dve.wait_ge(s_osc, 1)
            dve.tensor_scalar(out_scale[:, :, :], out_scale[:, :, :], EPS_OUT, None, ALU.add).then_inc(s_osc, 1)
            dve.wait_ge(s_osc, 2)
            dve.reciprocal(out_scale[:, :, :], out_scale[:, :, :]).then_inc(s_osc, 1)
            dve.wait_ge(s_osc, 3)
            dve.tensor_tensor(out_scale[:, :, :], out_scale[:, :, :], q_norm2[:, :, :], ALU.mult).then_inc(s_osc, 1)
            dve.wait_ge(s_oroot, 1)

            def body(h):
                for k in range(2):
                    for n in range(TILES):
                        dve.wait_ge(s_gs, h * 4 + (4 * k + n + 1))
                        wait(dve, s_ot, h * 4 + (4 * k + n + 1 - 8))
                        for j in range(4):
                            g = 4 * n + j
                            cols = slice(g * P, (g + 1) * P)
                            o_h = outputs[:, h + k, cols] if isinstance(h, int) else outputs[:, ds(h + k, 1), cols].squeeze(1)
                            sc = out_scale[:, h + k, g:g + 1] if isinstance(h, int) else out_scale[:, ds(h + k, 1), g:g + 1].squeeze(1)
                            ins = dve.scalar_tensor_tensor(out=gated[k][:, cols], in0=o_h, scalar=sc,
                                                           in1=gates[k][:, cols], op0=ALU.mult, op1=ALU.mult)
                            ins.then_inc(s_gd, 1)
            body(0)
            with dve.Fori(1, HEADS // 2) as i:
                body(i * 2)
            dve.wait_ge(s_wo, 4 * HEADS)
            for n in range(TILES):
                dve.tensor_copy(dtile(residual, n), bank[4 + n][:, :]).then_inc(s_merged, 1)

        @stage("scalar")
        def _(act):
            act.wait_ge(s_osc, 4)
            act.activation(out_scale[:, :, :], out_scale[:, :, :], ACT.Sqrt).then_inc(s_oroot, 1)
            act.wait_ge(s_onw, 16)
            act.wait_ge(s_inv, SEQ_TILES)
            act.wait_ge(s_invd, 16 * SEQ_TILES)
            act.preload_act_table(ACT.Sigmoid)

            def body(h):
                for k in range(2):
                    for n in range(TILES):
                        act.wait_ge(s_gt, h * 4 + (4 * k + n + 1))
                        wait(act, s_gd, h * 16 + (16 * k + 4 * n + 4 - 32))
                        act.activation(dtile(gates[k], n), bank[n % 2][:, :], ACT.Sigmoid).then_inc(s_gs, 1)
                    for n in range(TILES):
                        act.wait_ge(s_ot, h * 4 + (4 * k + n + 1))
                        wait(act, s_wo, h * 4 + (4 * k + n + 1 - 8))
                        act.activation(dtile(heads_out[k], n), bank[2 + n % 2][:, :], ACT.Copy,
                                       scale=out_norm[:, 0:1]).then_inc(s_ots, 1)
            body(0)
            with act.Fori(1, HEADS // 2) as i:
                body(i * 2)

        @stage("tensor")
        def _(pe):
            for n in range(TILES):
                pe.matmul(bank[4 + n][:, :], ident[:, :], dtile(residual, n), start=True, stop=False,
                          skip_group_check=True)

            def body(h):
                for k in range(2):
                    pe.wait_ge(s_mw[k], h * 8 + 16)
                    if isinstance(h, int):
                        pe.wait_ge(s_oc, 4 * HEADS)
                    for n in range(TILES):
                        at = h * 4 + (4 * k + n + 1)
                        wait(pe, s_gs, h * 4 + (4 * k + n + 1 - 2))
                        for j in range(4):
                            g = 4 * n + j
                            mm = pe.matmul(bank[n % 2][:, j * P:(j + 1) * P], gate_low[:, g * P:(g + 1) * P],
                                           merge_w[k][:, 0:P], start=True, stop=True, skip_group_check=True)
                        mm.then_inc(s_gt, 1)
                    for n in range(TILES):
                        pe.wait_ge(s_gd, h * 16 + (16 * k + 4 * n + 4))
                        wait(pe, s_ots, h * 4 + (4 * k + n + 1 - 2))
                        for j in range(4):
                            g = 4 * n + j
                            mm = pe.transpose(bank[2 + n % 2][:, j * P:(j + 1) * P], gated[k][:, g * P:(g + 1) * P],
                                              ident[:, :])
                        mm.then_inc(s_ot, 1)
                    for n in range(TILES):
                        pe.wait_ge(s_ots, h * 4 + (4 * k + n + 1))
                        pe.matmul(bank[4 + n][:, :], merge_w[k][:, P:2 * P], dtile(heads_out[k], n), start=False,
                                  stop=False, skip_group_check=True).then_inc(s_wo, 1)
            body(0)
            with pe.Fori(1, HEADS // 2) as i:
                body(i * 2)

        def by_time(array):
            return array.rearrange("p (t b) -> p b t", b=B)

        def batch_first(array):
            return array.rearrange("p (b t) -> p b t", t=T)

        def step_tile(array, t):
            return array[:, t * B:(t + 1) * B] if isinstance(t, int) else array[:, ds(t * B, B)]

        def pairs_loop(engine, body, last_peeled=False):
            body(0, False)
            with engine.Fori(1, T // 2 - (1 if last_peeled else 0)) as i:
                body(i * 2, False)
            if last_peeled:
                body(T - 2, True)

        def gate_inputs(s_xp, q0, gates, w_cols, work, xw, bias, start, src, evacuated):
            @stage("tensor")
            def _(pe):
                for semaphore, value in start:
                    pe.wait_ge(semaphore, value)
                for q in range(4 * gates):
                    wait(pe, evacuated, q0 + q - 3)
                    pe.matmul(bank[q % 4][:, :], w_cols(q // 4), dtile(src, q % 4), start=True,
                              stop=True).then_inc(s_xp, 1)

            @stage("scalar")
            def _(act):
                act.preload_act_table(ACT.Sigmoid)
                for semaphore, value in start:
                    act.wait_ge(semaphore, value)
                for q in range(4 * gates):
                    act.wait_ge(s_xp, q0 + q + 1)
                    n = q % 4
                    dst = by_time(xw[:, q // 4, :])[:, n * 16:(n + 1) * 16, :]
                    act.activation(dst, batch_first(bank[n][:, :]), ACT.Identity,
                                   bias=bias(q // 4)).then_inc(evacuated, 1)

        lstm_semaphores = tuple(sem(f"lstm_{name}") for name in (
            "weights_loaded", "gate_inputs_stored", "cell_cleared", "g_ready", "ifo_ready", "g_tanh", "ifo_sigmoid",
            "cell_products", "cell_ready", "cell_tanh", "hidden_ready", "hidden_kept", "gate_inputs_ready"))

        def lstm(use, w_dram, hs, start):
            xw = arena[:, 4:8, :]
            work = tok(8)
            state = tok(9)
            w_x = work[:, 0:4 * P]
            w_h = work[:, 4 * P:8 * P]
            bias = work[:, 8 * P:8 * P + 4]
            h_ring = [state[:, k * B:(k + 1) * B] for k in range(2)]
            gc = [state[:, (2 + 2 * k) * B:(4 + 2 * k) * B] for k in range(2)]
            sig = [state[:, (6 + 3 * k) * B:(9 + 3 * k) * B] for k in range(2)]
            prod = [state[:, (12 + 2 * k) * B:(14 + 2 * k) * B] for k in range(2)]
            tanh_c = [state[:, (16 + k) * B:(17 + k) * B] for k in range(2)]
            (s_w, s_ev, s_c0, s_gg, s_gi, s_tg, s_sg, s_pr, s_c, s_tc, s_h, s_hs, s_xp) = lstm_semaphores
            T0 = use * T

            @stage("sync")
            def _(sp):
                for semaphore, value in start:
                    sp.wait_ge(semaphore, value)
                sp.dma_start(work[:, 0:8 * P + 4], w_dram).then_inc(s_w, 16)

            gate_inputs(s_xp, use * 16, 4, lambda g: w_x[:, g * P:(g + 1) * P], work, xw, lambda g: bias[:, g:g + 1],
                        start + [(s_w, use * 16 + 16)], residual, s_ev)

            @stage("vector")
            def _(dve):
                for semaphore, value in start:
                    dve.wait_ge(semaphore, value)
                dve.memset(gc[0][:, B:2 * B], 0.0).then_inc(s_c0, 1)
                dve.wait_ge(s_c0, use + 1)

                def body(t0, last):
                    for p in range(2):
                        t, u = t0 + p, t0 + (p + T0)
                        dve.wait_ge(s_tg, u + 1)
                        dve.wait_ge(s_sg, u + 1)
                        dve.tensor_tensor(prod[p], sig[p][:, 0:2 * B], gc[p], ALU.mult).then_inc(s_pr, 1)
                        dve.wait_ge(s_pr, u + 1)
                        wait(dve, s_tc, u - 1)
                        dve.tensor_tensor(gc[1 - p][:, B:2 * B], prod[p][:, 0:B], prod[p][:, B:2 * B],
                                          ALU.add).then_inc(s_c, 1)
                        dve.wait_ge(s_tc, u + 1)
                        wait(dve, s_hs, u - 1)
                        dve.tensor_tensor(h_ring[p], sig[p][:, 2 * B:3 * B], tanh_c[p], ALU.mult).then_inc(s_h, 1)
                pairs_loop(dve, body)

            @stage("scalar")
            def _(act):
                def body(t0, last):
                    for p in range(2):
                        t, u = t0 + p, t0 + (p + T0)
                        act.wait_ge(s_gg, u + 1)
                        wait(act, s_pr, u - 1)
                        act.activation(gc[p][:, 0:B], bank[4 + p][:, 0:B], ACT.Tanh).then_inc(s_tg, 1)
                        act.wait_ge(s_gi, u + 1)
                        wait(act, s_h, u - 1)
                        act.activation(sig[p], bank[6 + p][:, 0:3 * B], ACT.Sigmoid).then_inc(s_sg, 1)
                        act.wait_ge(s_c, u + 1)
                        act.activation(tanh_c[p], gc[1 - p][:, B:2 * B], ACT.Tanh).then_inc(s_tc, 1)
                pairs_loop(act, body)

            @stage("tensor")
            def _(pe):
                def inject(t, p):
                    u = t + T0
                    wait(pe, s_tg, u - 1)
                    pe.matmul(bank[4 + p][:, 0:B], ident[:, :], step_tile(xw[:, 3, :], t), start=True, stop=False,
                              skip_group_check=True)
                    wait(pe, s_sg, u - 1)
                    x = xw[:, 0:3, :]
                    x = x[:, :, t * B:(t + 1) * B] if isinstance(t, int) else x[:, :, ds(t * B, B)]
                    pe.matmul(bank[6 + p][:, 0:3 * B].rearrange("p (g b) -> p g b", g=3), ident[:, :], x, start=True,
                              stop=False, skip_group_check=True)

                def body(t0, last):
                    for p in range(2):
                        t, u = t0 + p, t0 + (p + T0)
                        wait(pe, s_h, u)
                        h = cond[:, :] if isinstance(t, int) and t == 0 else h_ring[1 - p]
                        pe.matmul(bank[4 + p][:, 0:B], w_h[:, 3 * P:4 * P], h, start=False, stop=True,
                                  skip_group_check=True).then_inc(s_gg, 1)
                        for g in range(3):
                            mm = pe.matmul(bank[6 + p][:, g * B:(g + 1) * B], w_h[:, g * P:(g + 1) * P], h,
                                           start=False, stop=(g == 2), skip_group_check=True)
                        mm.then_inc(s_gi, 1)
                        if not (last and p == 1):
                            inject(t + 1, 1 - p)
                pe.wait_ge(s_ev, use * 16 + 16)
                inject(0, 0)
                pairs_loop(pe, body, last_peeled=True)

            @stage("gpsimd")
            def _(pool):
                for semaphore, value in start:
                    pool.wait_ge(semaphore, value)

                def body(t0, last):
                    for p in range(2):
                        t, u = t0 + p, t0 + (p + T0)
                        pool.wait_ge(s_h, u + 1)
                        settled(pool)
                        dst = batch_first(hs)[:, :, t:t + 1] if isinstance(t, int) else batch_first(hs)[:, :, ds(t, 1)]
                        pool.tensor_copy(dst, h_ring[p].unsqueeze(2)).then_inc(s_hs, 1)
                pairs_loop(pool, body)

            return s_hs, T0 + T

        s_la, LA = lstm(0, a["lstm_a_w"], tok(1), [(s_merged, 4)])

        E8 = 8
        route = tok(21)[:, 0:7 * P].rearrange("p (k n) -> p k n", k=7)
        router_w = sbuf("router_weights", [P, 2 * E8 + 1])
        s_rw = sem("router_weights_loaded")

        @stage("sync")
        def _(sp):
            sp.dma_start(router_w[:, :], a["router_w"]).then_inc(s_rw, 16)

        TOP1_STEPS = 12
        s_lg = sem("gate_logits_ready_by_token")
        s_st = sem("token_gate_steps")
        s_ex = sem("token_gate_exp")
        s_tr = sem("token_gates_transposed")
        s_gc = sem("token_gates_copied")
        s_dr = sem("token_gates_stored")

        def token_gates(use, src, src_ready, w, softmax_first, top, dram):
            steps = 3 + (3 if softmax_first else 0) + 5 + (1 if softmax_first else 4)
            step0 = use * TOP1_STEPS
            wide_a = tok(18)[:, 0:GROUPS * 64].rearrange("p (g e j) -> p g e j", g=GROUPS, e=E8)
            wide_b = tok(19)[:, 0:GROUPS * 64].rearrange("p (g e j) -> p g e j", g=GROUPS, e=E8)
            small = tok(20)[:, 0:4 * GROUPS].rearrange("p (k g) -> p k g", k=4)

            @stage("tensor")
            def _(pe):
                pe.wait_ge(*src_ready)
                pe.wait_ge(s_rw, 16)
                for g in range(GROUPS):
                    mm = pe.matmul(bank[6][:, g * E8:(g + 1) * E8], src[:, g * P:(g + 1) * P], w, start=True,
                                   stop=True, skip_group_check=True)
                mm.then_inc(s_lg, 1)

            @stage("vector")
            def _(dve):
                logits, shifted, exps, scores, rank, kept, gate = (
                    route[:, k, :].rearrange("p (g e) -> p g e", e=E8) for k in range(7))
                top_v, total, inverse = (small[:, k, :] for k in range(3))
                n = step0

                def step(instruction):
                    nonlocal n
                    instruction.then_inc(s_st, 1)
                    n += 1
                    dve.wait_ge(s_st, n)

                def wide(x):
                    return x.unsqueeze(2).to_broadcast([P, GROUPS, E8])

                dve.wait_ge(s_lg, use + 1)
                step(dve.tensor_copy(route[:, 0, :], bank[6][:, 0:P]))
                step(dve.tensor_reduce(top_v, logits, AX.X, ALU.max))
                step(dve.tensor_tensor(shifted, logits, wide(top_v), ALU.subtract))
                dve.wait_ge(s_ex, use + 1)
                if softmax_first:
                    step(dve.tensor_reduce(total, exps, AX.X, ALU.add))
                    step(dve.reciprocal(inverse, total))
                    step(dve.tensor_tensor(scores, exps, wide(inverse), ALU.mult))
                    n = ranks(dve, s_st, n, scores, wide_a, wide_b, rank, GROUPS, E8)
                    dve.wait_ge(s_st, n)
                    step(dve.scalar_tensor_tensor(out=gate, in0=rank, scalar=top - 0.5, in1=scores, op0=ALU.is_lt,
                                                  op1=ALU.mult))
                else:
                    n = ranks(dve, s_st, n, logits, wide_a, wide_b, rank, GROUPS, E8)
                    dve.wait_ge(s_st, n)
                    step(dve.scalar_tensor_tensor(out=kept, in0=rank, scalar=top - 0.5, in1=exps, op0=ALU.is_lt,
                                                  op1=ALU.mult))
                    step(dve.tensor_reduce(total, kept, AX.X, ALU.add))
                    step(dve.reciprocal(inverse, total))
                    step(dve.tensor_tensor(gate, kept, wide(inverse), ALU.mult))
                assert n == step0 + steps
                dve.wait_ge(s_tr, use + 1)
                dve.tensor_copy(route[:, 5, :], bank[7][:, 0:P]).then_inc(s_gc, 1)

            @stage("scalar")
            def _(act):
                act.wait_ge(s_st, step0 + 3)
                act.activation(route[:, 2, :], route[:, 1, :], ACT.Exp).then_inc(s_ex, 1)

            @stage("tensor")
            def _(pe):
                pe.wait_ge(s_st, step0 + steps)
                pe.transpose(bank[7][:, 0:P], route[:, 6, :], ident[:, :]).then_inc(s_tr, 1)

            @stage("gpsimd")
            def _(pool):
                pool.wait_ge(s_gc, use + 1)
                pool.dma_start(dram.rearrange("g e p -> (g e) p"), route[:, 5, :]).then_inc(s_dr, 16)
                pool.wait_ge(s_dr, use * 16 + 16)
            return s_dr, use * 16 + 16

        
        low = tok(1)
        low_sq, low_root, low_norm = tok(2), tok(3), tok(10)
        s_ms = sem("moe_a_squares_ready")
        s_mb = sem("moe_a_square_sums_ready")
        s_mr = sem("moe_a_roots_ready")
        s_mi = sem("moe_a_inverse_roots_ready")
        s_mn = sem("moe_a_normed")
        s_me = sem("moe_a_sums_shifted")
        EPS_FFN = 1e-6

        @stage("scalar")
        def _(act):
            act.wait_ge(s_la, LA)
            act.activation(low_sq, low, ACT.Square).then_inc(s_ms, 1)
            for n in range(TILES):
                act.wait_ge(s_me, n + 1)
                act.activation(dtile(low_root, n), dtile(low_root, n), ACT.Sqrt).then_inc(s_mr, 1)

        @stage("tensor")
        def _(pe):
            pe.wait_ge(s_ms, 1)
            for n in range(TILES):
                pe.matmul(bank[n][:, :], ones[:, :], dtile(low_sq, n), start=True, stop=True).then_inc(s_mb, 1)

        @stage("vector")
        def _(dve):
            dve.wait_ge(s_rw, 16)
            for n in range(TILES):
                dve.wait_ge(s_mb, n + 1)
                dve.tensor_scalar(dtile(low_root, n), bank[n][:, :], 1.0 / D, EPS_FFN, ALU.mult,
                                  ALU.add).then_inc(s_me, 1)
            for n in range(TILES):
                dve.wait_ge(s_mr, n + 1)
                dve.reciprocal(dtile(low_root, n), dtile(low_root, n)).then_inc(s_mi, 1)
                dve.wait_ge(s_mi, n + 1)
                dve.scalar_tensor_tensor(out=dtile(low_norm, n), in0=dtile(low, n), scalar=router_w[:, 16:17],
                                         in1=dtile(low_root, n), op0=ALU.mult, op1=ALU.mult).then_inc(s_mn, 1)

        moe_a_gates = token_gates(0, low_norm, (s_mn, 4), router_w[:, 0:E8], True, 1,
                                  scratch["moe_a_gate"])
        s_ma, MA = moe(MOE_A, low_norm, residual, hidden=(11, 12), spread=(13, 14), weights=(15, 16), work=17,
                       hidden_act=ACT.Silu, w_dram=a["moe_a_w"],
                       spread_src=lambda e: scratch["moe_a_gate"][:, e, :].partition_broadcast(P),
                       src_ready=(s_mn, 4), gates_ready=moe_a_gates)

        def gru(w_dram, hs, y, start):
            xw = arena[:, 4:7, :]
            work, state = tok(8), tok(9)
            w_x, w_h, w_q = work[:, 0:3 * P], work[:, 3 * P:6 * P], work[:, 6 * P:7 * P]
            raw_bias = work[:, 7 * P:7 * P + 7]
            bias = work[:, 7 * P + 8:7 * P + 11]
            h_ring = [state[:, k * B:(k + 1) * B] for k in range(2)]
            r_s, z_s, rh, zh, oz, ht, ozht = ([state[:, (2 + 2 * j + k) * B:(3 + 2 * j + k) * B] for k in range(2)]
                                              for j in range(7))
            s_w = sem("gru_weights_loaded")
            s_b = sem("gru_biases_summed")
            s_ev = sem("gru_gate_inputs_stored")
            s_gr, s_gz_, s_gh = sem("gru_r_ready"), sem("gru_z_ready"), sem("gru_candidate_ready")
            s_sr, s_sz, s_th = sem("gru_r_sigmoid"), sem("gru_z_sigmoid"), sem("gru_candidate_tanh")
            s_rh, s_zh, s_oh = sem("gru_reset_hidden"), sem("gru_update_parts"), sem("gru_new_part")
            s_h, s_hs = sem("gru_hidden_ready"), sem("gru_hidden_kept")
            s_yp, s_y = sem("gru_outputs_projected"), sem("gru_outputs_ready")

            @stage("sync")
            def _(sp):
                for semaphore, value in start:
                    sp.wait_ge(semaphore, value)
                sp.dma_start(work[:, 0:7 * P + 7], w_dram).then_inc(s_w, 16)

            @stage("vector")
            def _(dve):
                dve.wait_ge(s_w, 16)
                dve.tensor_tensor(bias, raw_bias[:, 0:3], raw_bias[:, 3:6], ALU.add).then_inc(s_b, 1)

            gate_inputs(sem("gru_gate_inputs_ready"), 0, 3, lambda g: w_x[:, g * P:(g + 1) * P], work, xw, lambda g: bias[:, g:g + 1],
                        start + [(s_b, 1)], residual, s_ev)

            @stage("vector")
            def _(dve):
                def body(t0, last):
                    for p in range(2):
                        t = t0 + p
                        h = cond[:, :] if isinstance(t, int) and t == 0 else h_ring[1 - p]
                        wait(dve, s_h, t)
                        dve.wait_ge(s_sr, t + 1)
                        dve.tensor_tensor(rh[p], r_s[p], h, ALU.mult).then_inc(s_rh, 1)
                        dve.wait_ge(s_sz, t + 1)
                        dve.tensor_tensor(zh[p], z_s[p], h, ALU.mult).then_inc(s_zh, 1)
                        dve.tensor_scalar(oz[p], z_s[p], -1.0, 1.0, ALU.mult, ALU.add).then_inc(s_zh, 1)
                        dve.wait_ge(s_th, t + 1)
                        dve.wait_ge(s_zh, t * 2 + 2)
                        dve.tensor_tensor(ozht[p], oz[p], ht[p], ALU.mult).then_inc(s_oh, 1)
                        dve.wait_ge(s_oh, t + 1)
                        wait(dve, s_hs, t - 1)
                        dve.tensor_tensor(h_ring[p], ozht[p], zh[p], ALU.add).then_inc(s_h, 1)
                pairs_loop(dve, body)

            @stage("scalar")
            def _(act):
                def body(t0, last):
                    for p in range(2):
                        t = t0 + p
                        act.wait_ge(s_gr, t + 1)
                        act.activation(r_s[p], bank[p][:, 0:B], ACT.Sigmoid).then_inc(s_sr, 1)
                        act.wait_ge(s_gz_, t + 1)
                        act.activation(z_s[p], bank[2 + p][:, 0:B], ACT.Sigmoid).then_inc(s_sz, 1)
                        act.wait_ge(s_gh, t + 1)
                        act.activation(ht[p], bank[4 + p][:, 0:B], ACT.Tanh).then_inc(s_th, 1)
                pairs_loop(act, body)
                for n in range(TILES):
                    act.wait_ge(s_yp, n + 1)
                    act.activation(dtile(y, n), bank[n][:, :], ACT.Identity, bias=raw_bias[:, 6:7]).then_inc(s_y, 1)

            @stage("tensor")
            def _(pe):
                def inject(t, p, which):
                    gate, at, freed = [(1, p, s_sr), (0, 2 + p, s_sz), (2, 4 + p, s_th)][which]
                    wait(pe, freed, t - 1)
                    pe.matmul(bank[at][:, 0:B], ident[:, :], step_tile(xw[:, gate, :], t), start=True, stop=False,
                              skip_group_check=True)

                def body(t0, last):
                    for p in range(2):
                        t = t0 + p
                        more = not (last and p == 1)
                        wait(pe, s_h, t)
                        h = cond[:, :] if isinstance(t, int) and t == 0 else h_ring[1 - p]
                        pe.matmul(bank[p][:, 0:B], w_h[:, P:2 * P], h, start=False, stop=True,
                                  skip_group_check=True).then_inc(s_gr, 1)
                        pe.matmul(bank[2 + p][:, 0:B], w_h[:, 0:P], h, start=False, stop=True,
                                  skip_group_check=True).then_inc(s_gz_, 1)
                        if more:
                            inject(t + 1, 1 - p, 0)
                        pe.wait_ge(s_rh, t + 1)
                        pe.matmul(bank[4 + p][:, 0:B], w_h[:, 2 * P:3 * P], rh[p], start=False, stop=True,
                                  skip_group_check=True).then_inc(s_gh, 1)
                        if more:
                            inject(t + 1, 1 - p, 1)
                            inject(t + 1, 1 - p, 2)
                pe.wait_ge(s_ev, 12)
                for which in range(3):
                    inject(0, 0, which)
                pairs_loop(pe, body, last_peeled=True)
                pe.wait_ge(s_hs, T)
                pe.wait_ge(s_th, T)
                pe.wait_ge(s_sz, T)
                for n in range(TILES):
                    pe.matmul(bank[n][:, :], w_q, dtile(hs, n), start=True, stop=True).then_inc(s_yp, 1)

            @stage("gpsimd")
            def _(pool):
                for semaphore, value in start:
                    pool.wait_ge(semaphore, value)

                def body(t0, last):
                    for p in range(2):
                        t = t0 + p
                        pool.wait_ge(s_h, t + 1)
                        settled(pool)
                        dst = batch_first(hs)[:, :, t:t + 1] if isinstance(t, int) else batch_first(hs)[:, :, ds(t, 1)]
                        pool.tensor_copy(dst, h_ring[p].unsqueeze(2)).then_inc(s_hs, 1)
                pairs_loop(pool, body)

            return s_y, TILES

        s_gru, GRU = gru(a["gru_w"], tok(1), tok(2), [(s_ma, MA)])
        HEAD_PAIRS, HD = 8, 64
        att_in = tok(2)
        queries, keys = [tok(3), tok(4)], [tok(5), tok(6)]
        value_rows = [tok(7), tok(8)]
        soft = tok(10).rearrange("p (x h m) -> p x h m", x=2, h=2)
        probs_diag = arena[:, 11:13, :].rearrange("p a n -> p (a n)").rearrange("p (g h m) -> p g h m", g=GROUPS, h=2)
        att_out = [tok(13), tok(14)]
        qkv_slot = [tok(15)[:, k * 3 * P:(k + 1) * 3 * P] for k in range(2)]
        po_slot = [tok(15)[:, (6 + k) * P:(7 + k) * P] for k in range(2)]
        causal_wide = tok(16)[:, 0:4 * T].rearrange("p (q n) -> p q n", q=4)
        causal = tok(16)[:, 4 * T:5 * T]
        row_max, row_sum, row_inv = (tok(16)[:, (6 + j) * T:(7 + j) * T].rearrange("p (h g) -> p h g", h=2) for j in range(3))
        s_az = sem("attn_constants_made")
        s_aw = [sem(f"attn_qkv_weights_loaded{k}") for k in range(2)]
        s_ao = [sem(f"attn_out_weights_loaded{k}") for k in range(2)]
        s_at = sem("attn_ring_tile_ready")
        s_ae = sem("attn_ring_tile_copied")
        s_alg = sem("attn_logits_ready")
        s_asm = sem("attn_softmax_steps")
        s_aex = sem("attn_exp_done")
        s_awo = sem("attn_products_ready")
        s_att = sem("attn_residual_updated")
        SOFT = 20

        def ring(p, u):
            if isinstance(p, int) and p == HEAD_PAIRS - 1 and u >= 12:
                return p * 16 + u
            if u >= 12:
                return p * 16 + (12 + u)
            return u if isinstance(p, int) and p == 0 else p * 16 + (u - 4)

        def attn_loop(engine, body, drain=None):
            body(0, 0)
            with engine.Fori(1, HEAD_PAIRS // 2) as i:
                body(i * 2 + (-1), 1)
                body(i * 2, 0)
            body(HEAD_PAIRS - 1, 1)
            if drain:
                drain(HEAD_PAIRS - 1, 1)

        @stage("gpsimd")
        def _(pool):
            pool.wait_ge(s_gru, GRU)
            pool.memset(probs_diag[:, :, :, :], 0.0).then_inc(s_az, 1)
            pool.memset(causal_wide, 0.0).then_inc(s_az, 1)
            pool.wait_ge(s_az, 2)
            pool.affine_select(out=causal_wide, in_=causal_wide, compare_op=ALU.is_ge, fill=-1e30, base=0,
                               pattern=[[-T, 4], [-1, T]], channel_multiplier=1).then_inc(s_az, 1)
            pool.wait_ge(s_az, 3)
            for q in range(4):
                rows = slice(q * T, (q + 1) * T)
                pool.tensor_copy(causal[rows, :], causal_wide[rows, q, :]).then_inc(s_az, 1)

        @stage("sync")
        def _(sp):
            sp.wait_ge(s_ma, MA)

            def load(p, k, first):
                if not first:
                    sp.wait_ge(s_at, ring(p + (-2), 11) + 1)
                src = at_head(a["attn_w"], p)
                sp.dma_start(qkv_slot[k], src[:, 0:3 * P]).then_inc(s_aw[k], 16)
                if not first:
                    sp.wait_ge(s_awo, p * 4 + (-4))
                sp.dma_start(po_slot[k], src[:, 3 * P:4 * P]).then_inc(s_ao[k], 16)
            load(0, 0, True)
            load(1, 1, True)
            load(2, 0, False)
            load(3, 1, False)
            with sp.Fori(2, HEAD_PAIRS // 2) as i:
                load(i * 2, 0, False)
                load(i * 2 + 1, 1, False)

        @stage("tensor")
        def _(pe):
            def loads_of(p, k):
                return p * 8 + (16 if k == 0 else 8)

            def project(p, k):
                pe.wait_ge(s_aw[k], loads_of(p, k))
                for u in range(12):
                    wait(pe, s_ae, ring(p, u) + (-1))
                    out_bank = bank[u % 2]
                    if u < 8:
                        pe.matmul(out_bank[:, :], qkv_slot[k][:, (u // 4) * P:(u // 4 + 1) * P],
                                  dtile(att_in, u % 4), start=True, stop=True).then_inc(s_at, 1)
                        continue
                    for j in range(4):
                        g = 4 * (u - 8) + j
                        mm = pe.matmul(out_bank[:, j * P:(j + 1) * P], att_in[:, g * P:(g + 1) * P],
                                       qkv_slot[k][:, 2 * P:3 * P], start=True, stop=True, skip_group_check=True)
                    mm.then_inc(s_at, 1)

            def logits(p, k):
                pe.wait_ge(s_ae, ring(p, 7) + 1)
                settled(pe)
                for h in range(2):
                    half = slice(HD * h, HD * h + HD)
                    for g in range(GROUPS):
                        for q in range(4):
                            cols = slice((4 * g + q) * T, (4 * g + q + 1) * T)
                            mm = pe.matmul(bank[2 + h][q * T:(q + 1) * T, g * T:(g + 1) * T], queries[k][half, cols],
                                           keys[k][half, cols], start=True, stop=True, skip_group_check=True,
                                           tile_position=(HD * h, q * T))
                    mm.then_inc(s_alg, 1)

            def mix_values(p, k):
                pe.wait_ge(s_asm, p * SOFT + SOFT)
                pe.wait_ge(s_ae, ring(p, 11) + 1)
                for n in range(TILES):
                    pe.wait_ge(s_ae, ring(p, 12 + n) + (-1))
                    for h in range(2):
                        for j in range(4):
                            g = 4 * n + j
                            mm = pe.matmul(bank[n % 2][HD * h:HD * h + HD, j * P:(j + 1) * P],
                                           value_rows[k][:, g * P + HD * h:g * P + HD * h + HD],
                                           probs_diag[:, g, h, :], start=True, stop=True, skip_group_check=True)
                    mm.then_inc(s_at, 1)

            def project_out(p, k):
                pe.wait_ge(s_ao[k], loads_of(p, k))
                for n in range(TILES):
                    pe.wait_ge(s_ae, ring(p, 12 + n) + 1)
                    pe.matmul(bank[4 + n][:, :], po_slot[k], dtile(att_out[k], n), start=False, stop=False,
                              skip_group_check=True).then_inc(s_awo, 1)

            def body(p, k):
                project(p, k)
                if not (isinstance(p, int) and p == 0):
                    mix_values(p + (-1), 1 - k)
                logits(p, k)
                if not (isinstance(p, int) and p == 0):
                    project_out(p + (-1), 1 - k)

            def drain(p, k):
                mix_values(p, k)
                project_out(p, k)

            pe.wait_ge(s_gru, GRU)
            pe.wait_ge(s_az, 7)
            for n in range(TILES):
                pe.matmul(bank[4 + n][:, :], ident[:, :], dtile(residual, n), start=True, stop=False,
                          skip_group_check=True)
            attn_loop(pe, body, drain)

        @stage("scalar")
        def _(act):
            act.preload_act_table(ACT.Exp)

            def copy(dst, p, u):
                act.wait_ge(s_at, ring(p, u) + 1)
                act.activation(dst, bank[u % 2][:, :], ACT.Copy).then_inc(s_ae, 1)

            def exponentials(p):
                for h in range(2):
                    act.wait_ge(s_asm, p * SOFT + (5 + h))
                    act.activation(soft[:, 1, h, :], soft[:, 0, h, :], ACT.Exp).then_inc(s_aex, 1)

            def outputs_of(p, k):
                for n in range(TILES):
                    copy(dtile(att_out[k], n), p, 12 + n)

            def body(p, k):
                first = isinstance(p, int) and p == 0
                for u in range(4):
                    copy(dtile(queries[k], u), p, u)
                if not first:
                    exponentials(p + (-1))
                for u in range(4):
                    copy(dtile(keys[k], u), p, 4 + u)
                for u in range(4):
                    copy(dtile(value_rows[k], u), p, 8 + u)
                if not first:
                    outputs_of(p + (-1), 1 - k)

            def drain(p, k):
                exponentials(p)
                outputs_of(p, k)
            attn_loop(act, body, drain)

        @stage("vector")
        def _(dve):
            dve.wait_ge(s_az, 7)
            scale = 1.0 / HD ** 0.5
            grid = [[soft[:, x, h, :].rearrange("p (g n) -> p g n", g=GROUPS) for h in range(2)] for x in range(2)]
            mask = causal.unsqueeze(1).to_broadcast([P, GROUPS, T])

            def wide(x):
                return x.unsqueeze(2).to_broadcast([P, GROUPS, T])

            def body(p, k):
                at = p * SOFT
                for h in range(2):
                    dve.wait_ge(s_alg, p * 2 + (h + 1))
                    wait(dve, s_asm, at)
                    dve.scalar_tensor_tensor(out=grid[0][h], in0=bank[2 + h][:, :].rearrange("p (g n) -> p g n", g=GROUPS),
                                             scalar=scale, in1=mask, op0=ALU.mult, op1=ALU.add).then_inc(s_asm, 1)
                for h in range(2):
                    dve.wait_ge(s_asm, at + (1 + h))
                    dve.tensor_reduce(row_max[:, h, :], grid[0][h], AX.X, ALU.max).then_inc(s_asm, 1)
                for h in range(2):
                    dve.wait_ge(s_asm, at + (3 + h))
                    dve.tensor_tensor(grid[0][h], grid[0][h], wide(row_max[:, h, :]), ALU.subtract).then_inc(s_asm, 1)
                for h in range(2):
                    dve.wait_ge(s_aex, p * 2 + (h + 1))
                    dve.tensor_reduce(row_sum[:, h, :], grid[1][h], AX.X, ALU.add).then_inc(s_asm, 1)
                for h in range(2):
                    dve.wait_ge(s_asm, at + (7 + h))
                    dve.reciprocal(row_inv[:, h, :], row_sum[:, h, :]).then_inc(s_asm, 1)
                for h in range(2):
                    dve.wait_ge(s_asm, at + (9 + h))
                    dve.tensor_tensor(grid[1][h], grid[1][h], wide(row_inv[:, h, :]), ALU.mult).then_inc(s_asm, 1)
                for h in range(2):
                    dve.wait_ge(s_asm, at + (11 + h))
                    for q in range(4):
                        rows = slice(q * T, (q + 1) * T)
                        dve.transpose(probs_diag[rows, :, h, rows], grid[1][h][rows, :, :]).then_inc(s_asm, 1)
            attn_loop(dve, body)
            dve.wait_ge(s_awo, 4 * HEAD_PAIRS)
            for n in range(TILES):
                dve.tensor_copy(dtile(residual, n), bank[4 + n][:, :]).then_inc(s_att, 1)


        s_lb, LB = lstm(1, a["lstm_b_w"], tok(1), [(s_att, TILES)])
        moe_b_gates = token_gates(1, tok(1), (s_lb, LB), router_w[:, E8:2 * E8], False, 2,
                                  scratch["moe_b_gate"])
        s_mbx, MB = moe(MOE_B, tok(1), residual, hidden=(11, 12), spread=(13, 14), weights=(15, 16), work=17,
                        hidden_act="relu2", w_dram=a["moe_b_w"],
                        spread_src=lambda e: scratch["moe_b_gate"][:, e, :].partition_broadcast(P),
                        src_ready=(s_lb, LB), gates_ready=moe_b_gates)
        finish(residual, s_mbx, MB)

        @block.sync
        def _(sp):
            for f in programs["sync"]:
                f(sp)

        @block.tensor
        def _(pe):
            for f in programs["tensor"]:
                f(pe)

        @block.scalar
        def _(act):
            for f in programs["scalar"]:
                f(act)

        @block.vector
        def _(dve):
            for f in programs["vector"]:
                f(dve)

        @block.gpsimd
        def _(pool):
            for f in programs["gpsimd"]:
                f(pool)


def lay_out(i):
    def arr(name):
        return np.asarray(i[name])

    def chunked(w):
        lead, k, m = w.shape[:-2], w.shape[-2], w.shape[-1]
        return np.moveaxis(w.reshape(*lead, k // P, P, m), -3, -2).reshape(*lead, P, (k // P) * m)

    def columns(v):
        return np.swapaxes(v.reshape(*v.shape[:-1], v.shape[-1] // P, P), -1, -2)

    def stack(shared, experts):
        return np.concatenate([shared[None], experts], 0)

    d = {}
    d["x"] = arr("x").reshape(N, D).T
    d["cond"] = arr("cond_1024").T
    d["gate_in"] = np.concatenate([chunked(arr("L0_cond_gate_w")), arr("L0_cond_time_w")], 1)
    d["gate_rows"] = np.concatenate([arr("L0_cond_gate_b"), arr("L0_cond_time_b")])[None]
    d["mix_w"] = np.concatenate([
        stack(arr("L0_cond_sw1"), arr("L0_cond_ew1")),
        chunked(stack(arr("L0_cond_sw2"), arr("L0_cond_ew2"))),
        columns(stack(arr("L0_cond_sb1"), arr("L0_cond_eb1"))),
        columns(stack(arr("L0_cond_sb2"), arr("L0_cond_eb2")))], 2)
    d["low_w"] = np.concatenate([arr("L0_attn_Wfa").T, arr("L0_attn_Wga").T, arr("L0_attn_Wb").T], 1)
    d["head_cols"] = np.concatenate([arr("L0_attn_dt_bias").T,
                                     np.broadcast_to(arr("L0_attn_A_log")[None], (P, HEADS))], 1)
    heads = {n: arr(f"L0_attn_{n}").reshape(HEADS, P, P).swapaxes(1, 2) for n in ("Wq", "Wk", "Wv", "Wfb", "Wgb")}
    d["fb_w"] = heads["Wfb"]
    taps = [arr(f"L0_attn_w{n}_conv").reshape(HEADS, P, 4) for n in "qkv"]
    d["qkv_w"] = np.concatenate([heads["Wq"], heads["Wk"], heads["Wv"], *taps], 2)
    d["merge_w"] = np.concatenate([heads["Wgb"], arr("L0_attn_Wo").T.reshape(HEADS, P, P)], 2)
    d["out_norm"] = arr("L0_attn_o_norm_w")[:, None]
    for name, layer in (("lstm_a_w", "L0"), ("lstm_b_w", "L1")):
        d[name] = np.concatenate([arr(f"{layer}_cond2_Wx"), arr(f"{layer}_cond2_Wh"),
                                  columns(arr(f"{layer}_cond2_b"))], 1)
    d["router_w"] = np.concatenate([arr("L0_ffn_gate_w").T, arr("L1_ffn_w_router"), arr("L0_ffn_rms_w")[:, None]], 1)
    d["moe_a_w"] = np.concatenate([arr("L0_ffn_W1"), chunked(arr("L0_ffn_W2")), columns(arr("L0_ffn_b1")),
                                   columns(arr("L0_ffn_b2"))], 2)
    d["moe_b_w"] = np.concatenate([arr("L1_ffn_w1"), arr("L1_ffn_w2")], 2)
    d["gru_w"] = np.concatenate([arr(f"L1_cond_{n}").T for n in ("Wxz", "Wxr", "Wxh", "Whz", "Whr", "Whh", "Whq")] +
                                [arr(f"L1_cond_{n}")[:, None] for n in ("bxz", "bxr", "bxh", "bhz", "bhr", "bhh", "bhq")], 1)
    pairs = [arr(f"L1_attn_P_{n}").transpose(1, 0, 2).reshape(D, 8, P).transpose(1, 0, 2) for n in "qkv"]
    d["attn_w"] = np.concatenate([*pairs, arr("L1_attn_P_o").transpose(0, 2, 1).reshape(8, P, D)], 2)
    return {k: np.ascontiguousarray(v) for k, v in d.items()}


def kernel(**inputs):
    import concourse.bacc as bacc
    from concourse.bass_utils import run_bass_kernel_spmd

    arrays = lay_out(inputs)
    nc = bacc.Bacc("TRN2", target_bir_lowering=False, num_devices=1)
    a = {k: nc.dram_tensor(f"in_{k}", v.shape, F32, kind="ExternalInput").ap() for k, v in arrays.items()}
    out = nc.dram_tensor("out", [P, N], F32, kind="ExternalOutput").ap()
    build(nc, a, out)
    r = run_bass_kernel_spmd(nc, [{f"in_{k}": v for k, v in arrays.items()}], core_ids=[0])
    return np.ascontiguousarray(r.results[0]["out"].T).reshape(B, T, D)
```

```python
from contextlib import ExitStack

import numpy as np

import concourse.bass as bass
from concourse import mybir

F32 = mybir.dt.float32
U8 = mybir.dt.uint8
ALU = mybir.AluOpType
ACT = mybir.ActivationFunctionType
AX = mybir.AxisListType

B, T, D = 64, 32, 128
N = B * T
P = 128
TILE = 512
TILES = N // TILE
GROUPS = N // P
HEADS = 8
ds = bass.ds


class Moe:

    def __init__(self, name, experts, chunks, biases, plain_first, before=None):
        self.name, self.E, self.C = name, experts, chunks
        self.biases, self.plain_first = biases, plain_first
        self.w2 = chunks * P
        self.b1 = 2 * chunks * P
        self.b2 = self.b1 + chunks
        self.width = 2 * chunks * P + (chunks + 1 if biases else 0)
        self.peeled = 1 if plain_first else 0
        self.pairs = (experts - self.peeled) // 2
        self.units0 = 4 * before.E + before.units0 if before else 0
        self.chunks0 = 4 * before.E * before.C + before.chunks0 if before else 0
        self.loads0 = [before.loads0[k] + 16 * before.loads(k) if before else 0 for k in range(2)]
        self.gates0 = [before.gates0[k] + 16 * (before.loads(k) - (before.plain_first and k == 0)) if before else 0
                       for k in range(2)]

    def loads(self, slot):
        return len(range(slot, self.E, 2))


MIX = Moe("mix", 5, 4, True, True)
MOE_A = Moe("moe_a", 8, 4, True, False, MIX)
MOE_B = Moe("moe_b", 8, 1, False, False, MOE_A)


def wait(engine, semaphore, value):
    if not isinstance(value, int) or value > 0:
        engine.wait_ge(semaphore, value)


def build(nc, a, out):
    scratch = {
        "mix_gate": nc.dram_tensor("mix_gate", [4, N], F32, kind="Internal").ap(),
        "moe_a_gate": nc.dram_tensor("moe_a_gate", [GROUPS, 8, P], F32, kind="Internal").ap(),
        "moe_b_gate": nc.dram_tensor("moe_b_gate", [GROUPS, 8, P], F32, kind="Internal").ap(),
        "values": nc.dram_tensor("values", [HEADS, P, N], F32, kind="Internal").ap(),
        "reads": nc.dram_tensor("reads", [HEADS, P, N], F32, kind="Internal").ap(),
        "systems": nc.dram_tensor("systems", [HEADS, B, T * T], F32, kind="Internal").ap(),
        "inverses": nc.dram_tensor("inverses", [HEADS, B, T * T], F32, kind="Internal").ap(),
        "row_scales": nc.dram_tensor("row_scales", [2, HEADS * B, T], F32, kind="Internal").ap(),
    }
    with ExitStack() as ctx:
        def sbuf(name, shape, dtype=F32):
            return ctx.enter_context(nc.sbuf_tensor(name, shape, dtype))

        def sem(name):
            return ctx.enter_context(nc.semaphore(name))

        arena = sbuf("arena", [P, 24, N])
        banks = ctx.enter_context(nc.psum_tensor("banks", [P, 8 * TILE], F32))
        bank = [banks[:, i * TILE:(i + 1) * TILE] for i in range(8)]

        def tok(i):
            return arena[:, i, :]

        residual = tok(0)

        ident = sbuf("ident", [P, P])
        ones = sbuf("ones", [P, P])
        earlier = sbuf("earlier", [P, 8, 8])
        ident_mask = sbuf("ident_mask", [P, P], U8)
        level_mask = sbuf("level_mask", [P, 5, 64], U8)
        mask_work = tok(23)[:, 0:6 * P].rearrange("p (m n) -> p m n", n=P)
        epsilons = sbuf("epsilons", [P, 2])
        s_eps = sem("epsilons_made")
        s_carrier = sem("wait_carrier")
        s_const = sem("constants_made")
        s_const_copy = sem("constants_cast")
        CONST = 2 + 3 + 10

        cond = sbuf("cond", [P, B])
        gate_in = sbuf("gate_in", [P, 20])
        gate_rows = sbuf("gate_rows", [1, 12])
        s_x = sem("x_loaded")
        s_gate_in = sem("gate_inputs_loaded")

        block = ctx.enter_context(nc.Block())
        programs = {"sync": [], "tensor": [], "scalar": [], "vector": [], "gpsimd": []}

        def settled(engine):
            engine.sem_inc(s_carrier, 1)

        def stage(engine):
            def add(f):
                programs[engine].append(f)
                return f
            return add

        mixture_semaphores = (
            [sem(f"mixture_weights_loaded{k}") for k in range(2)],
            [sem(f"mixture_gate_spread{k}") for k in range(2)],
            sem("mixture_hidden_ready"),
            sem("mixture_relu_done"),
            sem("mixture_activated"),
            sem("mixture_expert_out_ready"),
            sem("mixture_gated"),
            sem("mixture_added"),
        )

        @stage("gpsimd")
        def _(pool):
            pool.memset(ones[:, :], 1.0).then_inc(s_const, 1)
            pool.memset(epsilons[:, 0:1], 1e-5).then_inc(s_eps, 1)
            pool.memset(epsilons[:, 1:2], 1e-6).then_inc(s_eps, 1)
            pool.memset(mask_work[:, :, :], 1.0).then_inc(s_const, 1)
            pool.wait_ge(s_const, 2)
            pool.affine_select(out=ident[:, :], in_=ones[:, :], compare_op=ALU.is_equal, fill=0.0,
                               base=0, pattern=[[-1, P]], channel_multiplier=1).then_inc(s_const, 1)
            pool.affine_select(out=earlier[:, :, :], in_=ones[:, 0:64].rearrange("p (e j) -> p e j", j=8),
                               compare_op=ALU.is_gt, fill=0.0, base=0, pattern=[[1, 8], [-1, 8]],
                               channel_multiplier=0).then_inc(s_const, 1)
            pool.affine_select(out=mask_work[:, 5, :], in_=ones[:, :], compare_op=ALU.is_equal, fill=0.0,
                               base=0, pattern=[[-1, P]], channel_multiplier=1).then_inc(s_const, 1)
            for level in range(5):
                half = 1 << level
                work = mask_work[:, level, 0:64].rearrange("p (c r) -> p c r", r=half)
                src = ones[:, 0:64].rearrange("p (c r) -> p c r", r=half)
                pool.affine_select(out=work, in_=src, compare_op=ALU.is_ge, fill=0.0, base=0,
                                   pattern=[[-2 * half, 64 // half], [0, half]],
                                   channel_multiplier=1).then_inc(s_const, 1)
                pool.wait_ge(s_const, 2 + 3 + 2 * level + 1)
                pool.affine_select(out=work, in_=work, compare_op=ALU.is_ge, fill=0.0, base=half - 1,
                                   pattern=[[2 * half, 64 // half], [0, half]],
                                   channel_multiplier=-1).then_inc(s_const, 1)

        @stage("vector")
        def _(dve):
            dve.wait_ge(s_const, CONST)
            dve.tensor_copy(ident_mask[:, :], mask_work[:, 5, :]).then_inc(s_const_copy, 1)
            dve.tensor_copy(level_mask[:, :, :], mask_work[:, 0:5, 0:64]).then_inc(s_const_copy, 1)

        @stage("sync")
        def _(sp):
            for e in range(2):
                sp.dma_start(tok(6 + e)[:, 0:MIX.width], a["mix_w"][e]).then_inc(mixture_semaphores[0][e], 16)
                if e == 0:
                    sp.dma_start(residual, a["x"]).then_inc(s_x, 16)
            sp.dma_start(cond[:, :], a["cond"]).then_inc(s_gate_in, 16)
            sp.dma_start(gate_in[:, :], a["gate_in"]).then_inc(s_gate_in, 16)
            sp.dma_start(gate_rows[:, :], a["gate_rows"]).then_inc(s_gate_in, 16)

        def moe(m, src, acc, hidden, spread, weights, work, hidden_act, w_dram, spread_src,
                src_ready, gates_ready, gate_hooks=None, prefetched=False, transpose_gates=None):
            C = m.C
            (s_w, s_g, s_h, s_r, s_a, s_y, s_c, s_acc) = mixture_semaphores
            U0, Q0 = m.units0, m.chunks0
            hid = [tok(i).rearrange("p (c n) -> p c n", n=TILE) for i in hidden]
            spr = [tok(i) for i in spread]
            wgt = [tok(i) for i in weights]
            tmp = [tok(work)[:, k * TILE:(k + 1) * TILE] for k in range(2)]
            squared = hidden_act == "relu2"
            rel = [tok(work)[:, (2 + k) * TILE:(3 + k) * TILE] for k in range(2)]
            loops = m.pairs

            def tile_of(array, n):
                return array[:, n * TILE:(n + 1) * TILE]

            @stage("sync")
            def _(sp):
                ready_waited = False
                for e in range(m.E):
                    if e >= 2:
                        sp.wait_ge(s_c, U0 + 4 * (e - 1))
                    if e == 0:
                        sp.wait_ge(*src_ready)
                    if e >= 2 or not prefetched:
                        sp.dma_start(wgt[e % 2][:, 0:m.width], w_dram[e]).then_inc(s_w[e % 2], 16)
                    if not (m.plain_first and e == 0):
                        if not ready_waited:
                            sp.wait_ge(*gates_ready)
                            ready_waited = True
                        rows = spread_src(e - m.peeled)
                        dst = spr[e % 2] if len(rows.shape) == 2 else spr[e % 2].rearrange("p (g n) -> p g n", n=P)
                        sp.dma_start(dst, rows).then_inc(s_g[e % 2], 16)

            def body_units(i, count):
                if count == 1:
                    return [(0, 0, 0, n) for n in range(4)]
                return [(i, i * 2 + m.peeled + k, m.peeled + k, n) for k in range(2) for n in range(4)]

            def run(engine, body, after_peeled=None):
                if m.peeled:
                    body(0, 1)
                    if after_peeled:
                        after_peeled(engine)
                    first = 0
                else:
                    body(0, 2)
                    first = 1
                with engine.Fori(first, loops) as i:
                    body(i, 2)

            @stage("tensor")
            def _(pe):
                pe.wait_ge(*src_ready)

                def up(i, e, k, n):
                    s, u = k % 2, e * 4 + (n + U0)
                    if n == 0:
                        pe.wait_ge(s_w[s], i * 16 + ((k // 2 + 1) * 16 + m.loads0[s]))
                    for c in range(C):
                        q = e * 4 * C + (n * C + c + Q0)
                        wait(pe, s_a, q - 3)
                        pe.matmul(bank[(k * 4 * C + n * C + c) % 4][:, :], wgt[s][:, c * P:(c + 1) * P],
                                  tile_of(src, n), start=True, stop=True).then_inc(s_h, 1)

                def down(i, e, k, n):
                    s, u = k % 2, e * 4 + (n + U0)
                    wait(pe, s_c, u - 1)
                    for c in range(C):
                        pe.wait_ge(s_a, e * 4 * C + (n * C + c + Q0 + 1))
                        mm = pe.matmul(bank[4 + n % 2][:, :], wgt[s][:, m.w2 + c * P:m.w2 + (c + 1) * P],
                                       hid[n % 2][:, c, :], start=(c == 0), stop=(c == C - 1))
                    mm.then_inc(s_y, 1)

                def body(i, count):
                    units = body_units(i, count)
                    up(*units[0])
                    for j, unit in enumerate(units):
                        if j + 1 < len(units):
                            up(*units[j + 1])
                        down(*unit)
                        if transpose_gates and j == 1 and isinstance(i, int):
                            transpose_gates(pe)

                run(pe, body, gate_hooks and gate_hooks["tensor"])

            @stage("scalar")
            def _(act):
                def body(i, count):
                    for i, e, k, n in body_units(i, count):
                        s, u = k % 2, e * 4 + (n + U0)
                        wait(act, s_y, u - 1)
                        for c in range(C):
                            q = e * 4 * C + (n * C + c + Q0)
                            act.wait_ge(s_h, q + 1)
                            src_bank = bank[(k * 4 * C + n * C + c) % 4][:, :]
                            dst = hid[n % 2][:, c, :]
                            if squared:
                                act.activation(rel[n % 2], src_bank, ACT.Relu).then_inc(s_r, 1)
                                act.wait_ge(s_r, q + (1 - Q0))
                                act.activation(dst, rel[n % 2], ACT.Square).then_inc(s_a, 1)
                            else:
                                act.activation(dst, src_bank, hidden_act,
                                               bias=wgt[s][:, m.b1 + c:m.b1 + c + 1]).then_inc(s_a, 1)

                run(act, body, gate_hooks and gate_hooks["scalar"])

            @stage("vector")
            def _(dve):
                def body(i, count):
                    for i, e, k, n in body_units(i, count):
                        s, u = k % 2, e * 4 + (n + U0)
                        b2 = wgt[s][:, m.b2:m.b2 + 1] if m.biases else 0.0
                        dve.wait_ge(s_y, u + 1)
                        if m.plain_first and count == 1:
                            dve.tensor_scalar(tile_of(acc, n), bank[4 + n % 2][:, :], b2, None,
                                              ALU.add).then_inc(s_c, 1)
                            dve.wait_ge(s_c, u + 1)
                            dve.sem_inc(s_acc, 1)
                            continue
                        if n == 0:
                            dve.wait_ge(s_g[s], i * 16 + (16 + m.gates0[s]))
                        wait(dve, s_acc, u - 1)
                        dve.scalar_tensor_tensor(out=tmp[n % 2], in0=bank[4 + n % 2][:, :], scalar=b2,
                                                 in1=tile_of(spr[s], n), op0=ALU.add,
                                                 op1=ALU.mult).then_inc(s_c, 1)
                        dve.wait_ge(s_c, u + 1)
                        dve.tensor_tensor(tile_of(acc, n), tile_of(acc, n), tmp[n % 2],
                                          ALU.add).then_inc(s_acc, 1)

                run(dve, body, gate_hooks and gate_hooks["vector"])

            return s_acc, U0 + 4 * m.E

        def load_first_experts(m, weights, w_dram, free):
            @stage("sync")
            def _(sp):
                if free:
                    sp.wait_ge(*free)
                for e in range(2):
                    sp.dma_start(tok(weights[e])[:, 0:m.width], w_dram[e]).then_inc(mixture_semaphores[0][e], 16)

        def ranks(dve, sem_steps, base, scores, wide_a, wide_b, rank, G, E):
            shape = [scores.shape[0], G, E, E]
            mine = scores.unsqueeze(3).to_broadcast(shape)
            other = scores.unsqueeze(2).to_broadcast(shape)
            tri = earlier[0:scores.shape[0], 0:E, 0:E].unsqueeze(1).to_broadcast(shape)
            dve.tensor_tensor(wide_a, other, mine, ALU.is_gt).then_inc(sem_steps, 1)
            dve.tensor_tensor(wide_b, other, mine, ALU.is_equal).then_inc(sem_steps, 1)
            dve.wait_ge(sem_steps, base + 2)
            dve.tensor_tensor(wide_b, wide_b, tri, ALU.mult).then_inc(sem_steps, 1)
            dve.wait_ge(sem_steps, base + 3)
            dve.tensor_tensor(wide_a, wide_a, wide_b, ALU.add).then_inc(sem_steps, 1)
            dve.wait_ge(sem_steps, base + 4)
            dve.tensor_reduce(rank, wide_a, AX.X, ALU.add).then_inc(sem_steps, 1)
            return base + 5

        E4 = 4
        seg = sbuf("segment_sums", [P, 3, B])
        agg = sbuf("aggregates", [P, 3, B])
        silu_cond = sbuf("silu_cond", [P, B])
        gsm = sbuf("gate_small", [B, 64])
        gwide = sbuf("gate_wide", [B, 2, 16])
        gmask = sbuf("gate_by_token", [B, E4, T])
        s_seg = sem("mix_segments_summed")
        s_agg = sem("mix_aggregates_ready")
        s_silu = sem("mix_condition_silu")
        s_glog = sem("mix_gate_logits")
        s_gst = sem("mix_gate_steps")
        s_gexp = sem("mix_gate_exp")
        s_gtok = sem("mix_gate_by_token")
        s_gdram = sem("mix_gate_stored")
        H3 = T // 3

        @stage("vector")
        def _(dve):
            dve.wait_ge(s_x, 16)
            x3 = residual.rearrange("p (b t) -> p b t", t=T)
            for k, (lo, hi) in enumerate([(0, H3), (H3, 2 * H3), (2 * H3, T)]):
                dve.tensor_reduce(seg[:, k, :], x3[:, :, lo:hi], AX.X, ALU.add).then_inc(s_seg, 1)
            dve.wait_ge(s_seg, 3)
            head, wrist, proprio = (seg[:, k, :] for k in range(3))
            dve.tensor_tensor(agg[:, 1, :], head, proprio, ALU.add).then_inc(s_seg, 1)
            dve.tensor_tensor(agg[:, 2, :], wrist, proprio, ALU.add).then_inc(s_seg, 1)
            dve.wait_ge(s_seg, 5)
            dve.tensor_tensor(agg[:, 0, :], agg[:, 1, :], wrist, ALU.add).then_inc(s_seg, 1)
            dve.wait_ge(s_seg, 6)
            for k, size in enumerate([T, T - H3, T - H3]):
                dve.tensor_scalar(agg[:, k, :], agg[:, k, :], 1.0 / size, None, ALU.mult).then_inc(s_agg, 1)

        @stage("scalar")
        def _(act):
            act.wait_ge(s_gate_in, 48)
            act.activation(silu_cond[:, :], cond[:, :], ACT.Silu).then_inc(s_silu, 1)

        def mix_gate_tensor(pe):
            pe.wait_ge(s_agg, 3)
            pe.wait_ge(s_silu, 1)
            pe.wait_ge(s_const, CONST)
            pe.wait_ge(s_gate_in, 48)
            for k in range(3):
                pe.matmul(bank[6][0:B, 0:4], agg[:, k, :], gate_in[:, 4 * k:4 * k + 4],
                          start=(k == 0), stop=False)
            pe.matmul(bank[6][0:B, 0:4], ones[0:1, 0:B], gate_rows[:, 0:4], start=False, stop=True)
            pe.matmul(bank[7][0:B, 0:8], silu_cond[:, :], gate_in[:, 12:20], start=True, stop=False)
            pe.matmul(bank[7][0:B, 0:8], ones[0:1, 0:B], gate_rows[:, 4:12], start=False,
                      stop=True).then_inc(s_glog, 1)

        def mix_gate_scalar(act):
            act.wait_ge(s_gst, 4)
            act.activation(gsm[:, 24:28], gsm[:, 16:20], ACT.Exp, bias=gsm[:, 20:21],
                           accum_out=gsm[:, 28:29]).then_inc(s_gexp, 1)

        def mix_gate_vector(dve):
            mod, scaled, logits, neg_max = gsm[:, 0:8], gsm[:, 8:12], gsm[:, 16:20], gsm[:, 20:21]
            exps, total, inverse = gsm[:, 24:28], gsm[:, 28:29], gsm[:, 29:30]
            scores, rank, kept = gsm[:, 32:36], gsm[:, 36:40], gsm[:, 40:44]
            kept_sum, kept_inverse, gate = gsm[:, 44:45], gsm[:, 45:46], gsm[:, 48:52]
            n = 0

            def step(instruction):
                nonlocal n
                instruction.then_inc(s_gst, 1)
                n += 1
                dve.wait_ge(s_gst, n)

            dve.wait_ge(s_glog, 1)
            step(dve.tensor_copy(mod, bank[7][0:B, 0:8]))
            step(dve.scalar_tensor_tensor(out=scaled, in0=mod[:, 0:4], scalar=1.0, in1=bank[6][0:B, 0:4],
                                          op0=ALU.add, op1=ALU.mult))
            step(dve.tensor_tensor(logits, scaled, mod[:, 4:8], ALU.add))
            step(dve.tensor_reduce(neg_max, logits, AX.X, ALU.max, negate=True))
            dve.wait_ge(s_gexp, 1)
            step(dve.reciprocal(inverse, total))
            step(dve.tensor_scalar(scores, exps, inverse, None, ALU.mult))
            n = ranks(dve, s_gst, n, scores.unsqueeze(1),
                      gwide[:, 0, :].rearrange("p (g e j) -> p g e j", g=1, e=4),
                      gwide[:, 1, :].rearrange("p (g e j) -> p g e j", g=1, e=4),
                      rank.unsqueeze(1), 1, E4)
            dve.wait_ge(s_gst, n)
            step(dve.scalar_tensor_tensor(out=kept, in0=rank, scalar=1.5, in1=scores, op0=ALU.is_lt, op1=ALU.mult))
            step(dve.tensor_reduce(kept_sum, kept, AX.X, ALU.add))
            step(dve.tensor_scalar(kept_sum, kept_sum, 1e-8, None, ALU.add))
            step(dve.reciprocal(kept_inverse, kept_sum))
            step(dve.tensor_scalar(gate, kept, kept_inverse, None, ALU.mult))
            step(dve.tensor_copy(gmask[:, :, :], gate.unsqueeze(2).to_broadcast([B, E4, T])))
            dve.memset(gmask[:, 1, H3:2 * H3], 0.0).then_inc(s_gtok, 1)
            dve.memset(gmask[:, 2, 0:H3], 0.0).then_inc(s_gtok, 1)

        mixed = tok(1)

        @stage("gpsimd")
        def _(pool):
            pool.wait_ge(s_gtok, 2)
            pool.dma_start(scratch["mix_gate"].rearrange("e (b t) -> b e t", t=T),
                           gmask[:, :, :]).then_inc(s_gdram, 16)
            pool.wait_ge(s_gdram, 16)

        s_mix, MIX_ADDS = moe(
            MIX, residual, mixed, hidden=(2, 3), spread=(4, 5), weights=(6, 7), work=8,
            hidden_act=ACT.Gelu_apprx_tanh, w_dram=a["mix_w"],
            spread_src=lambda e: scratch["mix_gate"][e, :].partition_broadcast(P),
            src_ready=(s_x, 16), gates_ready=(s_gdram, 16), prefetched=True,
            gate_hooks={"tensor": mix_gate_tensor, "scalar": mix_gate_scalar, "vector": mix_gate_vector})

        s_out = sem("result_stored")

        def finish(array, semaphore, value):
            @stage("sync")
            def _(sp):
                sp.wait_ge(semaphore, value)
                sp.dma_start(out, array).then_inc(s_out, 16)
                sp.wait_ge(s_out, 16)

        decay_low, gate_low = tok(2), tok(3)
        decay = arena[:, 4:12, :]
        low_w = tok(22)[:, 0:2 * P + HEADS]
        head_cols = sbuf("head_columns", [P, 2 * HEADS])
        neg_rate = sbuf("negative_rate", [P, HEADS])
        beta = sbuf("beta", [P, GROUPS, HEADS])
        small_marks = [tok(22)[:, (2 + k) * TILE:(3 + k) * TILE].bitcast(U8) for k in range(2)]
        fb_w = [tok(22)[:, (3 + k) * P:(4 + k) * P] for k in range(2)]
        s_low_w = sem("low_rank_weights_loaded")
        s_low = sem("low_rank_ready")
        s_low_copied = sem("low_rank_copied")
        s_rate = sem("rate_ready")
        s_fb = [sem(f"decay_weights_loaded{k}") for k in range(2)]
        s_dl = sem("decay_logits_ready")
        s_abs = sem("decay_abs_done")
        s_relu = sem("decay_relu_done")
        s_expu = sem("decay_exp_done")
        s_ln = sem("decay_log_done")
        s_poly = sem("decay_series_steps")
        s_small = sem("decay_small_marked")
        s_sp = sem("softplus_first_half_ready")
        s_sp2 = sem("softplus_second_half_ready")
        s_decay = sem("decay_ready")
        kk_gram, qk_gram = tok(20), tok(21)
        s_gz = sem("gram_arrays_cleared")
        POLY = 5

        def dtile(array, n):
            return array[:, n * TILE:(n + 1) * TILE]

        @stage("sync")
        def _(sp):
            sp.dma_start(low_w, a["low_w"]).then_inc(s_low_w, 16)
            sp.dma_start(head_cols[:, :], a["head_cols"]).then_inc(s_low_w, 16)
            for k in range(2):
                sp.dma_start(fb_w[k], a["fb_w"][k]).then_inc(s_fb[k], 16)
            with sp.Fori(1, HEADS // 2) as i:
                for k in range(2):
                    sp.wait_ge(s_dl, i * 8 + (4 * k - 4))
                    sp.dma_start(fb_w[k], a["fb_w"][ds(i * 2 + k, 1)].rearrange("a p n -> p (a n)")).then_inc(s_fb[k], 16)

        @stage("tensor")
        def _(pe):
            pe.wait_ge(s_mix, MIX_ADDS)
            pe.wait_ge(s_low_w, 32)
            for half in range(2):
                for n in range(TILES):
                    pe.matmul(bank[half * 4 + n][:, :], low_w[:, half * P:(half + 1) * P], dtile(mixed, n),
                              start=True, stop=True).then_inc(s_low, 1)
            pe.wait_ge(s_low_copied, 5)
            for g in range(GROUPS):
                mm = pe.matmul(bank[4][:, g * HEADS:(g + 1) * HEADS], mixed[:, g * P:(g + 1) * P],
                               low_w[:, 2 * P:2 * P + HEADS], start=(g == 0), stop=(g == GROUPS - 1), skip_group_check=True)
            mm.then_inc(s_low, 1)
            pe.wait_ge(s_low_copied, 9)

            def body(i):
                for k in range(2):
                    pe.wait_ge(s_fb[k], (i + 1) * 16)
                    for n in range(TILES):
                        wait(pe, s_relu, i * 8 + (4 * k + n + 1 - 8))
                        pe.matmul(bank[4 * k + n][:, :], fb_w[k], dtile(decay_low, n),
                                  start=True, stop=True).then_inc(s_dl, 1)
            body(0)
            with pe.Fori(1, HEADS // 2) as i:
                body(i)

        @stage("scalar")
        def _(act):
            for q in range(8):
                act.wait_ge(s_low, q + 1)
                act.activation(dtile(decay_low if q < 4 else gate_low, q % 4), bank[q][:, :],
                               ACT.Copy).then_inc(s_low_copied, 1)
            act.wait_ge(s_low, 9)
            act.activation(beta[:, :, :], bank[4][:, 0:GROUPS * HEADS].rearrange("p (g h) -> p g h", h=HEADS),
                           ACT.Sigmoid).then_inc(s_low_copied, 1)
            act.wait_ge(s_low_w, 32)
            act.activation(neg_rate[:, :], head_cols[:, HEADS:2 * HEADS], ACT.Exp).then_inc(s_rate, 1)

            def head_col(cols, h):
                return cols[:, h:h + 1] if isinstance(h, int) else cols[:, ds(h, 1)]

            def front(h, k):
                U, R, L = tok(12 + k), tok(14 + k), tok(16 + k)
                dt = head_col(head_cols, h)
                wait(act, s_decay, h - 1)
                for n in range(TILES):
                    act.wait_ge(s_dl, h * 4 + (n + 1))
                    settled(act)
                    act.activation(dtile(U, n), bank[4 * k + n][:, :], ACT.Abs, bias=dt).then_inc(s_abs, 1)
                    act.activation(dtile(R, n), bank[4 * k + n][:, :], ACT.Relu, bias=dt).then_inc(s_relu, 1)
                act.wait_ge(s_abs, h * 4 + 4)
                act.activation(U, U, ACT.Exp, scale=-1.0).then_inc(s_expu, 1)
                act.wait_ge(s_expu, h + 1)
                act.activation(L, U, ACT.Ln, bias=1.0).then_inc(s_ln, 1)

            def back(h, k):
                act.wait_ge(s_sp, h + 1)
                act.wait_ge(s_sp2, h + 1)
                dst = decay[:, h, :] if isinstance(h, int) else decay[:, ds(h, 1), :].rearrange("p a n -> p (a n)")
                settled(act)
                act.activation(dst, tok(14 + k), ACT.Exp, scale=head_col(neg_rate, h)).then_inc(s_decay, 1)

            act.preload_act_table_set("natural_log_exp_and_others")
            act.wait_ge(s_rate, 2)
            front(0, 0)
            with act.Fori(0, HEADS // 2 - 1) as i:
                front(i * 2 + 1, 1)
                back(i * 2, 0)
                front(i * 2 + 2, 0)
                back(i * 2 + 1, 1)
            front(HEADS - 1, 1)
            back(HEADS - 2, 0)
            back(HEADS - 1, 1)

        @stage("vector")
        def _(dve):
            dve.wait_ge(s_rate, 1)
            dve.tensor_scalar(neg_rate[:, :], neg_rate[:, :], -1.0, None, ALU.mult).then_inc(s_rate, 1)

            def body(i):
                for k in range(2):
                    U, R, L, Q = tok(12 + k), tok(14 + k), tok(16 + k), tok(18 + k)
                    small = small_marks[k]
                    at = i * (2 * POLY) + k * POLY
                    dve.wait_ge(s_expu, i * 2 + (k + 1))
                    dve.tensor_scalar(Q, U, -0.25, 1.0 / 3.0, ALU.mult, ALU.add).then_inc(s_poly, 1)
                    dve.wait_ge(s_poly, at + 1)
                    dve.tensor_tensor(Q, Q, U, ALU.mult).then_inc(s_poly, 1)
                    dve.wait_ge(s_poly, at + 2)
                    dve.scalar_tensor_tensor(out=Q, in0=Q, scalar=-0.5, in1=U, op0=ALU.add,
                                             op1=ALU.mult).then_inc(s_poly, 1)
                    dve.wait_ge(s_poly, at + 3)
                    dve.scalar_tensor_tensor(out=Q, in0=Q, scalar=1.0, in1=U, op0=ALU.add,
                                             op1=ALU.mult).then_inc(s_poly, 1)
                    dve.wait_ge(s_ln, i * 2 + (k + 1))
                    dve.wait_ge(s_poly, at + 4)
                    dve.wait_ge(s_small, i * 2 + (k + 1))
                    settled(dve)
                    dve.copy_predicated(L, small, Q).then_inc(s_poly, 1)
                    dve.wait_ge(s_poly, at + 5)
                    dve.wait_ge(s_relu, i * 8 + (4 * k + 4))
                    dve.tensor_tensor(R[:, 0:N // 2], R[:, 0:N // 2], L[:, 0:N // 2], ALU.add).then_inc(s_sp, 1)
            body(0)
            with dve.Fori(1, HEADS // 2) as i:
                body(i)

        @stage("gpsimd")
        def _(pool):
            pool.wait_ge(s_mix, MIX_ADDS)
            pool.memset(kk_gram, 0.0).then_inc(s_gz, 1)
            pool.memset(qk_gram, 0.0).then_inc(s_gz, 1)

            def body(h):
                for k in range(2):
                    pool.wait_ge(s_expu, h + (k + 1))
                    settled(pool)
                    pool.tensor_scalar(small_marks[k], tok(12 + k), 2.0 ** -5, None,
                                       ALU.is_lt).then_inc(s_small, 1)
                    R, L = tok(14 + k)[:, N // 2:N], tok(16 + k)[:, N // 2:N]
                    pool.wait_ge(s_poly, h * POLY + (k * POLY + 5))
                    pool.wait_ge(s_relu, h * 4 + (4 * k + 4))
                    settled(pool)
                    pool.tensor_tensor(R, R, L, ALU.add).then_inc(s_sp2, 1)
            body(0)
            with pool.Fori(1, HEADS // 2) as i:
                body(i * 2)

        q_tok, k_tok, v_tok = tok(12), tok(13), tok(14)
        in_left = tok(15)
        right_qk = [tok(16), tok(17)]
        left_k = [tok(18), tok(19)]
        v_rows = tok(22)
        squares = [tok(23), tok(2)]
        oldest = [tok(2)[:, n * TILE:(n + 1) * TILE] for n in range(TILES)]
        qkv_w = sbuf("qkv_weights", [P, 3 * P + 12])
        dots = sbuf("square_sums", [P, HEADS, 2 * GROUPS])
        s_qw = sem("qkv_weights_loaded")
        s_pj = sem("projection_ready")
        s_tap = sem("conv_current_tap_done")
        s_tap3 = sem("conv_oldest_tap_done")
        s_cstep = sem("conv_first_tap_added")
        s_cb = sem("conv_banks_read")
        s_conv = sem("conv_done")
        s_silu_h = sem("qkv_activated")
        s_vt = sem("value_rows_transposed")
        s_vev = sem("value_rows_copied")
        s_sq = sem("squares_ready")
        s_dot = sem("square_sums_ready")
        s_dotc = sem("square_sums_copied")
        s_prod = sem("decayed_operands_ready")
        s_left = sem("left_products_steps")
        s_right = sem("right_products_updated")
        s_gm = sem("gram_products_ready")
        s_pq = sem("qk_blocks_kept")
        s_pk = sem("gram_banks_kept")
        s_vout = sem("values_stored")
        s_aout = sem("reads_stored")
        s_nout = sem("systems_stored")
        HALVES = [1, 2, 4, 8, 16]

        def at_head(array, h):
            return array[h] if isinstance(h, int) else array[ds(h, 1)].squeeze(0)

        def decay_of(h):
            return decay[:, h, :] if isinstance(h, int) else decay[:, ds(h, 1), :].squeeze(1)

        def halves(array, half):
            v = array.rearrange("p (c w) -> p c w", w=2 * half)
            return v[:, :, 0:half], v[:, :, half:2 * half]

        def compact(array, part, half):
            v = array.rearrange("p (g x m) -> p g x m", g=GROUPS, x=2)[:, :, part, :]
            return v.rearrange("p g (c r) -> p g c r", r=half)

        def grouped(view):
            return view.rearrange("p (g c) r -> p g c r", g=GROUPS)

        def heads_loop(engine, body):
            body(0)
            with engine.Fori(1, HEADS) as h:
                body(h)

        @stage("sync")
        def _(sp):
            sp.dma_start(qkv_w[:, :], a["qkv_w"][0]).then_inc(s_qw, 16)

            def store(h, last):
                if not last:
                    sp.wait_ge(s_conv, h * 12 + 12)
                    nxt = a["qkv_w"][h + 1] if isinstance(h, int) else a["qkv_w"][ds(h + 1, 1)].squeeze(0)
                    sp.dma_start(qkv_w[:, :], nxt).then_inc(s_qw, 16)
                sp.wait_ge(s_vev, h * 4 + 4)
                sp.dma_start(at_head(scratch["values"], h), v_rows).then_inc(s_vout, 16)
                sp.wait_ge(s_pq, h * 10 + 10)
                sp.wait_ge(s_pk, h * 12 + 12)
                sp.dma_start(at_head(scratch["reads"], h), qk_gram).then_inc(s_aout, 16)
                for q in range(4):
                    rows = slice(T * q, T * q + T)
                    src = kk_gram.rearrange("p (g i) -> p g i", i=P)[rows, :, rows]
                    dst = at_head(scratch["systems"], h).rearrange("(g q) (j i) -> q j g i", q=4, i=T)[q]
                    sp.dma_start(dst, src).then_inc(s_nout, 16)
            with sp.Fori(0, HEADS - 1) as h:
                store(h, False)
            store(HEADS - 1, True)

        @stage("tensor")
        def _(pe):
            def project(h, units):
                for u in units:
                    m, n = u // 4, u % 4
                    if u == 0:
                        pe.wait_ge(s_qw, h * 16 + 16)
                    if u < 4:
                        wait(pe, s_vev, h * 4)
                        wait(pe, s_dotc, h * 2)
                    else:
                        pe.wait_ge(s_cb, h * 12 + (u - 3))
                    pe.matmul(bank[u % 4][:, :], qkv_w[:, m * P:(m + 1) * P], dtile(mixed, n), start=True,
                              stop=True).then_inc(s_pj, 1)

            def body(h, last=False):
                project(h, range(4, 12))

                def gram(level):
                    half = HALVES[level - 1] if level else 0
                    if level == 0:
                        pe.wait_ge(s_silu_h, h * 3 + 2)
                    else:
                        pe.wait_ge(s_prod, h * 14 + (3 * level - 1))
                    for b in range(4):
                        prior = h * 12 + (2 * (level - 1) + b // 2 + 1)
                        wait(pe, s_pk, prior)
                        for g in range(4 * b, 4 * b + 4):
                            cols = slice(g * P, (g + 1) * P)
                            left = (k_tok if level < 2 else left_k[level % 2])[:, cols]
                            moving = (q_tok if level == 0 else right_qk[level % 2])[:, cols]
                            mm = pe.matmul(bank[4 + b][:, (g % 4) * P:(g % 4 + 1) * P], left, moving,
                                           start=True, stop=True, skip_group_check=True)
                        mm.then_inc(s_gm, 1)

                def sums(which):
                    pe.wait_ge(s_vev, h * 4 + (which + 1))
                    pe.wait_ge(s_sq, h * 2 + (which + 1))
                    for g in range(GROUPS):
                        mm = pe.matmul(bank[which][:, g:g + 1], squares[which][:, g * P:(g + 1) * P], ones[:, 0:1],
                                       start=True, stop=True, skip_group_check=True)
                    mm.then_inc(s_dot, 1)

                gram(0)
                gram(1)
                pe.wait_ge(s_silu_h, h * 3 + 3)
                for n in range(TILES):
                    for j in range(4):
                        g = 4 * n + j
                        mm = pe.transpose(bank[n][:, j * P:(j + 1) * P], v_tok[:, g * P:(g + 1) * P], ident[:, :])
                    mm.then_inc(s_vt, 1)
                gram(2)
                sums(0)
                gram(3)
                sums(1)
                gram(4)
                if not last:
                    project(h + 1, range(4))
                gram(5)

            pe.wait_ge(s_decay, HEADS)
            project(0, range(4))
            body(0)
            with pe.Fori(1, HEADS - 1) as h:
                body(h)
            body(HEADS - 1, last=True)

        @stage("scalar")
        def _(act):
            act.preload_act_table(ACT.Silu)

            def body(h):
                def taps(m):
                    for n in range(TILES):
                        act.wait_ge(s_pj, h * 12 + (4 * m + n + 1))
                        if m == 0 and n == 0:
                            wait(act, s_prod, h * 14)
                        wait(act, s_conv, h * 12 + (4 * m + n - 3))
                        act.activation(oldest[n], bank[n][:, :], ACT.Copy,
                                       scale=qkv_w[:, 3 * P + 4 * m:3 * P + 4 * m + 1]).then_inc(s_tap3, 1)
                        act.activation(dtile((q_tok, k_tok, v_tok)[m], n), bank[n][:, :], ACT.Copy,
                                       scale=qkv_w[:, 3 * P + 4 * m + 3:3 * P + 4 * m + 4]).then_inc(s_tap, 1)

                def silu(m):
                    act.wait_ge(s_conv, h * 12 + (4 * m + 4))
                    x = (q_tok, k_tok, v_tok)[m]
                    act.activation(x, x, ACT.Silu).then_inc(s_silu_h, 1)

                taps(0)
                taps(1)
                silu(0)
                taps(2)
                silu(1)
                silu(2)
                act.wait_ge(s_silu_h, h * 3 + 3)
                wait(act, s_dot, h * 2)
                act.activation(squares[0], k_tok, ACT.Square).then_inc(s_sq, 1)
                act.activation(squares[1], q_tok, ACT.Square).then_inc(s_sq, 1)
                wait(act, s_vout, h * 16)
                for n in range(TILES):
                    act.wait_ge(s_vt, h * 4 + (n + 1))
                    act.activation(dtile(v_rows, n), bank[n][:, :], ACT.Copy).then_inc(s_vev, 1)
                for which in range(2):
                    act.wait_ge(s_dot, h * 2 + (which + 1))
                    dst = dots[:, h, which * 16:which * 16 + 16] if isinstance(h, int) \
                        else dots[:, ds(h, 1), which * 16:which * 16 + 16].squeeze(1)
                    settled(act)
                    act.activation(dst, bank[which][:, 0:GROUPS], ACT.Copy).then_inc(s_dotc, 1)
            heads_loop(act, body)

        @stage("gpsimd")
        def _(pool):
            pool.wait_ge(s_decay, HEADS)
            pool.memset(left_k[0], 0.0).then_inc(s_gz, 1)
            pool.memset(left_k[1], 0.0).then_inc(s_gz, 1)

            def body(h):
                right = decay_of(h)
                wait(pool, s_prod, h * 14)
                settled(pool)
                pool.memset(in_left, 1.0).then_inc(s_left, 1)
                pool.wait_ge(s_left, h * 5 + 1)
                settled(pool)
                pool.tensor_copy(halves(in_left, 1)[0], halves(right, 1)[1]).then_inc(s_left, 1)
                for u in range(12):
                    dst = dtile((q_tok, k_tok, v_tok)[u // 4], u % 4).rearrange("p (b t) -> p b t", t=T)
                    src = oldest[u % 4].rearrange("p (b t) -> p b t", t=T)
                    pool.wait_ge(s_tap3, h * 12 + (u + 1))
                    pool.wait_ge(s_cb, h * 12 + (u + 1))
                    pool.tensor_tensor(dst[:, :, 3:T], dst[:, :, 3:T], src[:, :, 0:T - 3],
                                       ALU.add).then_inc(s_conv, 1)
                for level in range(1, 5):
                    half = HALVES[level - 1]
                    left_end = halves(right, half)[0][:, :, half - 1:half]
                    right_end = halves(right, half)[1][:, :, half - 1:half]
                    shape = [P, N // (2 * half), half]
                    if level >= 2:
                        pool.wait_ge(s_prod, h * 14 + (3 * level - 3))
                        pool.wait_ge(s_left, h * 5 + level)
                        settled(pool)
                        lo = halves(in_left, half)[0]
                        pool.tensor_tensor(lo, lo, right_end.to_broadcast(shape), ALU.mult).then_inc(s_left, 1)
                    pool.wait_ge(s_prod, h * 14 + (3 * level - 1))
                    pool.wait_ge(s_left, h * 5 + level + 1)
                    settled(pool)
                    hi = halves(right, half)[1]
                    pool.tensor_tensor(hi, hi, left_end.to_broadcast(shape), ALU.mult).then_inc(s_right, 1)
                    pool.wait_ge(s_right, h * 4 + level)
            heads_loop(pool, body)

        def keep(dve, h, level):
            for b in range(2):
                gs = slice(8 * b, 8 * b + 8)
                grams = banks[:, (4 + 2 * b) * TILE:(6 + 2 * b) * TILE]
                dve.wait_ge(s_gm, h * 24 + (4 * level + 2 * b + 2))
                if b == 0 and level == 0:
                    wait(dve, s_aout, h * 16)
                    settled(dve)
                if b == 0 and level == 1:
                    wait(dve, s_nout, h * 64)
                settled(dve)
                if level == 0:
                    out_v = qk_gram.rearrange("p (g i) -> p g i", i=P)[:, gs, :]
                    data = grams.rearrange("p (g i) -> p g i", i=P)
                    mask = ident_mask[:, :].unsqueeze(1).to_broadcast([P, 8, P])
                    dve.copy_predicated(out_v, mask, data).then_inc(s_pk, 1)
                    continue
                half = HALVES[level - 1]
                c = 64 // half
                data = grams.rearrange("p (g x c r) -> p g x c r", g=8, x=2, r=half)
                mask = level_mask[:, level - 1, :].rearrange("p (c r) -> p c r", r=half).unsqueeze(1) \
                    .to_broadcast([P, 8, c, half])
                for part, dst in enumerate((qk_gram, kk_gram)):
                    out_v = dst.rearrange("p (g c w) -> p g c w", g=GROUPS, w=2 * half)[
                        :, gs, :, half:2 * half]
                    dve.copy_predicated(out_v, mask, data[:, :, part]).then_inc((s_pq, s_pk)[part], 1)

        @stage("vector")
        def _(dve):
            def body(h):
                right = decay_of(h)
                for u in range(12):
                    if u == 4 and not (isinstance(h, int) and h == 0):
                        keep(dve, h + (-1), 5)
                    m, n = u // 4, u % 4
                    dst = dtile((q_tok, k_tok, v_tok)[m], n).rearrange("p (b t) -> p b t", t=T)
                    src = bank[u % 4][:, :].rearrange("p (b t) -> p b t", t=T)
                    dve.wait_ge(s_tap, h * 12 + (u + 1))
                    for back in range(1, 3):
                        tap = qkv_w[:, 3 * P + 4 * m + 3 - back:3 * P + 4 * m + 4 - back]
                        if back > 1:
                            dve.wait_ge(s_cstep, h * 12 + (u + 1))
                        ins = dve.scalar_tensor_tensor(out=dst[:, :, back:T], in0=src[:, :, 0:T - back], scalar=tap,
                                                       in1=dst[:, :, back:T], op0=ALU.mult, op1=ALU.add)
                        ins.then_inc(s_cb if back == 2 else s_cstep, 1)

                def products(level):
                    half = HALVES[level - 1]
                    ring = level % 2
                    if level == 1:
                        if isinstance(h, int) and h == 0:
                            dve.wait_ge(s_gz, 4)
                        dve.wait_ge(s_silu_h, h * 3 + 2)
                        wait(dve, s_gm, h * 24)
                    else:
                        dve.wait_ge(s_gm, h * 24 + (4 * (level - 1)))
                        dve.wait_ge(s_left, h * 5 + level)
                        dve.tensor_tensor(halves(left_k[ring], half)[0], halves(k_tok, half)[0],
                                          halves(in_left, half)[0], ALU.mult).then_inc(s_prod, 1)
                        dve.wait_ge(s_right, h * 4 + (level - 1))
                    settled(dve)
                    factor = grouped(halves(right, half)[1])
                    for part, x in enumerate((q_tok, k_tok)):
                        dve.tensor_tensor(compact(right_qk[ring], part, half), grouped(halves(x, half)[1]), factor,
                                          ALU.mult).then_inc(s_prod, 1)

                products(1)
                keep(dve, h, 0)
                for level in range(2, 6):
                    products(level)
                    keep(dve, h, level - 1)
            heads_loop(dve, body)

        SEQ_TILES = HEADS * B // P
        PAD = T * (T + 1)
        flat = arena.rearrange("p a n -> p (a n)")
        system = flat[:, 4 * N:4 * N + SEQ_TILES * PAD].rearrange("p (s m) -> p s m", m=PAD)
        inverse = flat[:, 7 * N:7 * N + SEQ_TILES * PAD].rearrange("p (s m) -> p s m", m=PAD)
        products = flat[:, 10 * N:12 * N]
        half_out = flat[:, 4 * N + SEQ_TILES * PAD:4 * N + SEQ_TILES * PAD + 256]
        norm_work = sbuf("norm_work", [P, HEADS, 2 * GROUPS])
        gamma_kappa = sbuf("gamma_kappa", [P, 2, HEADS, GROUPS])
        q_root = norm_work[:, :, GROUPS:2 * GROUPS]
        q_norm2 = sbuf("q_norm_squared", [P, HEADS, GROUPS])
        gk_rows = sbuf("gamma_kappa_rows", [P, 2, P])
        row_scale = sbuf("row_scales_by_sequence", [P, 2, SEQ_TILES, T])
        s_nw = sem("norms_steps")
        s_kn = sem("k_norm_root")
        s_gkt = sem("gamma_kappa_transposed")
        s_gkc = sem("gamma_kappa_copied")
        s_rsd = sem("row_scales_stored")
        s_rs = sem("row_scales_loaded")
        s_sys = [sem(f"system_loaded{s}") for s in range(SEQ_TILES)]
        s_inv0 = sem("inverse_cleared")
        s_solve = sem("solve_steps")
        s_inv = sem("inverse_ready")
        s_invd = sem("inverses_stored")
        EPS_QK = 1e-6

        inv_diag = [tok(12), tok(13)]
        reads_in = [tok(14), tok(15)]
        values_in = [tok(1), tok(2)]
        outputs = arena[:, 16:24, :]
        delta = flat[:, 7 * N + SEQ_TILES * PAD:7 * N + SEQ_TILES * PAD + 2 * TILE].rearrange("p (r n) -> p r n", n=TILE)
        square_scrap = flat[:, 7 * N - P:7 * N]
        gap = 4 * N + SEQ_TILES * PAD + 256
        gates = [dtile(residual, n) for n in range(TILES)] + \
            [flat[:, gap + n * TILE:gap + (n + 1) * TILE] for n in range(3)] + \
            [flat[:, 7 * N + SEQ_TILES * PAD + 2 * TILE:7 * N + SEQ_TILES * PAD + 3 * TILE]]
        merge_w = [sbuf(f"merge_weights{k}", [P, 2 * P]) for k in range(2)]
        out_norm = sbuf("output_norm_weight", [P, 1])
        out_sq = sbuf("output_square_sums", [P, HEADS, GROUPS])
        out_scale = sbuf("output_scales", [P, HEADS, GROUPS])
        s_ivz = sem("inverse_diagonals_cleared")
        s_ri = [sem(f"read_inputs_loaded{k}") for k in range(2)]
        s_dp = sem("deltas_ready")
        s_dc = sem("deltas_copied")
        s_op = sem("outputs_ready")
        s_oc = sem("outputs_copied")
        s_osq = sem("outputs_squared")
        s_mw = [sem(f"merge_weights_loaded{k}") for k in range(2)]
        s_onw = sem("output_norm_weight_loaded")
        s_osc = sem("output_scale_steps")
        s_oroot = sem("output_scale_root")
        s_oinv = sem("output_scale_inverse_steps")
        s_gt = sem("gate_logits_ready")
        s_gs = sem("gate_ready")
        s_gd = sem("gated_outputs_ready")
        s_ot = sem("gated_outputs_transposed")
        s_ots = sem("gated_outputs_scaled")
        s_wo = sem("merge_products_ready")
        s_merged = sem("residual_updated")

        def of_pair(array, p, k, cols):
            return array[:, p * 2 + k, cols] if isinstance(p, int) else array[:, ds(p * 2 + k, 1), cols].squeeze(1)

        def both_heads(array, p):
            return array[:, p * 2:p * 2 + 2, :] if isinstance(p, int) else array[:, ds(p * 2, 2), :]

        def at_pair(array, p):
            return array[:, p, :] if isinstance(p, int) else array[:, ds(p, 1), :].squeeze(1)

        @stage("vector")
        def _(dve):
            dve.wait_ge(s_dotc, 2 * HEADS)
            dve.tensor_scalar(norm_work[:, :, :], dots[:, :, :], D * EPS_QK, None, ALU.add).then_inc(s_nw, 1)
            dve.wait_ge(s_nw, 1)
            dve.reciprocal(norm_work[:, :, :], norm_work[:, :, :]).then_inc(s_nw, 1)
            dve.wait_ge(s_nw, 2)
            by_head = beta[:, :, :].rearrange("p g h -> p h g")
            dve.tensor_tensor(gamma_kappa[:, 0], norm_work[:, :, 0:GROUPS], by_head, ALU.mult).then_inc(s_nw, 1)
            dve.tensor_scalar(q_norm2[:, :, :], norm_work[:, :, GROUPS:2 * GROUPS], 1.0 / D, None,
                              ALU.mult).then_inc(s_nw, 1)
            keep(dve, HEADS - 1, 5)
            dve.wait_ge(s_kn, 1)
            dve.tensor_tensor(gamma_kappa[:, 1], gamma_kappa[:, 1], by_head, ALU.mult).then_inc(s_nw, 1)

        @stage("scalar")
        def _(act):
            act.wait_ge(s_nw, 2)
            act.activation(gamma_kappa[:, 1], norm_work[:, :, 0:GROUPS], ACT.Sqrt).then_inc(s_kn, 1)
            act.wait_ge(s_nw, 4)
            act.activation(q_root, q_norm2[:, :, :], ACT.Sqrt).then_inc(s_kn, 1)
            for x in range(2):
                act.wait_ge(s_gkt, x + 1)
                act.activation(gk_rows[:, x, :], bank[x][:, 0:P], ACT.Copy).then_inc(s_gkc, 1)

        @stage("tensor")
        def _(pe):
            for x in range(2):
                pe.wait_ge(s_nw, 3 + 2 * x)
                pe.transpose(bank[x][:, 0:P], gamma_kappa[:, x].rearrange("p h g -> p (h g)"),
                             ident[:, :]).then_inc(s_gkt, 1)

        @stage("sync")
        def _(sp):
            for s in range(SEQ_TILES):
                if s == 0:
                    sp.wait_ge(s_nout, 64 * HEADS)
                    sp.wait_ge(s_prod, 14 * HEADS)
                src = scratch["systems"].rearrange("(s h) b m -> s (h b) m", s=SEQ_TILES)[s]
                sp.dma_start(system[:, s, 0:T * T], src).then_inc(s_sys[s], 16)
                if s == 0:
                    sp.wait_ge(s_gkc, 2)
                    for x in range(2):
                        sp.dma_start(scratch["row_scales"][x].rearrange("(m q) t -> m (q t)", q=4),
                                     gk_rows[:, x, :]).then_inc(s_rsd, 16)
                    sp.wait_ge(s_rsd, 32)
                    for x in range(2):
                        sp.dma_start(row_scale[:, x],
                                     scratch["row_scales"][x].rearrange("(s p) t -> p s t", p=P)).then_inc(s_rs, 16)

        @stage("gpsimd")
        def _(pool):
            pool.wait_ge(s_left, 5 * HEADS)
            pool.wait_ge(s_right, 4 * HEADS)
            pool.wait_ge(s_prod, 14 * HEADS)
            pool.memset(inverse[:, :, :], 0.0).then_inc(s_inv0, 1)
            pool.wait_ge(s_inv0, 1)
            pool.memset(inverse.rearrange("p s (k w) -> p s k w", w=T + 1)[:, :, :, 0:1], 1.0).then_inc(s_inv0, 1)

        @stage("vector")
        def _(dve):
            dve.wait_ge(s_rs, 32)
            dve.wait_ge(s_inv0, 2)
            dve.wait_ge(s_kn, 2)

            def solve_tile(s, first):
                steps = 0
                a_t = at_pair(system, s)
                x_t = at_pair(inverse, s)

                def wait_steps():
                    if first is not None:
                        dve.wait_ge(s_solve, first + steps)
                        settled(dve)

                def block(array, half, rows, cols):
                    off = cols * half * T + rows * half
                    v = array.rearrange("p (k w) -> p k w", w=2 * half * (T + 1))[:, :, off:off + half * T]
                    return v.rearrange("p k (j x) -> p k j x", x=T)[:, :, :, 0:half]

                def emit(f):
                    nonlocal steps
                    if first is not None:
                        f().then_inc(s_solve, 1)
                    steps += 1

                full = a_t[:, 0:T * T].rearrange("p (j i) -> p j i", i=T)
                gamma = (row_scale[:, 0, s:s + 1, :] if isinstance(s, int) else row_scale[:, 0, ds(s, 1), :]).to_broadcast([P, T, T])
                emit(lambda: dve.tensor_tensor(full, full, gamma, ALU.mult))
                wait_steps()
                emit(lambda: dve.tensor_scalar(block(x_t, 1, 1, 0), block(a_t, 1, 1, 0), -1.0, None, ALU.mult))
                for half in (2, 4, 8, 16):
                    nb = T // (2 * half)
                    size = half * half
                    for second in range(2):
                        wait_steps()
                        if second:
                            left = half_out[:, 0:nb * size].rearrange("p (k j a) -> p k j a", k=nb, j=half)
                            right = block(x_t, half, 1, 1)
                            result, negate = block(x_t, half, 1, 0), True
                        else:
                            left = block(x_t, half, 0, 0)
                            right = block(a_t, half, 1, 0)
                            result = half_out[:, 0:nb * size].rearrange("p (k j a) -> p k j a", k=nb, j=half)
                            negate = False
                        if half <= 4:
                            for c in range(half):
                                dst = products[:, c * nb * size:(c + 1) * nb * size].rearrange(
                                    "p (k j i) -> p k j i", k=nb, j=half)
                                emit(lambda: dve.tensor_tensor(
                                    dst, left[:, :, :, c:c + 1].to_broadcast([P, nb, half, half]),
                                    right[:, :, c:c + 1, :].to_broadcast([P, nb, half, half]), ALU.mult))
                            summed = products[:, 0:half * nb * size].rearrange(
                                "p (c k j i) -> p k j i c", c=half, k=nb, j=half)
                        elif half == 16:
                            low, high, every = slice(0, 8), slice(8, 16), slice(0, 16)
                            parts = [(every, low, low), (every, high, every)] if second else \
                                [(low, every, every), (high, every, high)]
                            summed = []
                            for at, (js, rows, inner) in zip((0, 2048), parts):
                                nj, ni, nc_ = js.stop - js.start, rows.stop - rows.start, inner.stop - inner.start
                                dst = products[:, at:at + nj * ni * nc_].rearrange("p (j i c) -> p j i c", j=nj, i=ni)
                                emit(lambda: dve.tensor_tensor(
                                    dst, left[:, 0][:, js, inner].unsqueeze(2).to_broadcast([P, nj, ni, nc_]),
                                    right[:, 0][:, inner, rows].rearrange("p c i -> p i c").unsqueeze(1)
                                    .to_broadcast([P, nj, ni, nc_]), ALU.mult))
                                summed.append((result[:, 0][:, js, rows], dst))
                            wait_steps()
                            for target, dst in summed:
                                emit(lambda: dve.tensor_reduce(target, dst, AX.X, ALU.add, negate=negate))
                            continue
                        else:
                            for k in range(nb):
                                dst = products[:, k * half * size:(k + 1) * half * size].rearrange(
                                    "p (j i c) -> p j i c", j=half, i=half)
                                emit(lambda: dve.tensor_tensor(
                                    dst, left[:, k].unsqueeze(2).to_broadcast([P, half, half, half]),
                                    right[:, k].rearrange("p c i -> p i c").unsqueeze(1)
                                    .to_broadcast([P, half, half, half]), ALU.mult))
                            summed = products[:, 0:half * nb * size].rearrange(
                                "p (k j i c) -> p k j i c", c=half, k=nb, j=half)
                        wait_steps()
                        emit(lambda: dve.tensor_reduce(result, summed, AX.X, ALU.add, negate=negate))
                wait_steps()
                kappa = at_pair(row_scale[:, 1], s).unsqueeze(2).to_broadcast([P, T, T])
                x_full = x_t[:, 0:T * T].rearrange("p (j i) -> p j i", i=T)
                if first is not None:
                    dve.tensor_tensor(x_full, x_full, kappa, ALU.mult).then_inc(s_inv, 1)
                return steps

            STEPS = 2 + sum(2 * (half + 1 if half <= 4 else T // (2 * half) + 1) for half in (2, 4, 8)) + 8

            def scale_and_gate(p):
                scales = both_heads(out_scale, p)
                dve.wait_ge(s_oroot, p + 1)
                settled(dve)
                dve.reciprocal(scales, scales).then_inc(s_oinv, 1)
                dve.wait_ge(s_oinv, p * 2 + 1)
                settled(dve)
                dve.tensor_tensor(scales, scales, both_heads(q_root, p), ALU.mult).then_inc(s_oinv, 1)
                dve.wait_ge(s_oinv, p * 2 + 2)
                for t in range(8):
                    k, n = t // 4, t % 4
                    dve.wait_ge(s_gs, p * 8 + (t + 1))
                    dve.wait_ge(s_oc, p * 8 + (t + 1))
                    settled(dve)
                    for j in range(4):
                        g = 4 * n + j
                        cols = slice(g * P, (g + 1) * P)
                        dve.scalar_tensor_tensor(out=gates[t][:, j * P:(j + 1) * P], in0=of_pair(outputs, p, k, cols),
                                                 scalar=of_pair(out_scale, p, k, slice(g, g + 1)),
                                                 in1=gates[t][:, j * P:(j + 1) * P], op0=ALU.mult,
                                                 op1=ALU.mult).then_inc(s_gd, 1)

            def tile_steps(s):
                settled(dve)
                for q in ([0] if isinstance(s, int) else range(SEQ_TILES)):
                    dve.wait_ge(s_sys[q], 16)
                assert solve_tile(s, s * STEPS) == STEPS

            tile_steps(0)
            with dve.Fori(1, SEQ_TILES) as s:
                tile_steps(s)
                scale_and_gate(s + (-1))
            scale_and_gate(SEQ_TILES - 1)
            dve.wait_ge(s_wo, 8 + 4 * HEADS)
            for n in range(TILES):
                dve.tensor_copy(dtile(residual, n), bank[4 + n][:, :]).then_inc(s_merged, 1)

        @stage("gpsimd")
        def _(pool):
            pool.wait_ge(s_conv, 12 * HEADS)
            pool.wait_ge(s_gm, 24 * HEADS)
            pool.wait_ge(s_sq, 2 * HEADS)
            for k in range(2):
                pool.memset(inv_diag[k], 0.0).then_inc(s_ivz, 1)

            def body(p):
                pool.wait_ge(s_osq, p * 32 + 32)
                settled(pool)
                pool.tensor_tensor(both_heads(out_scale, p), both_heads(out_sq, p), both_heads(q_norm2, p),
                                   ALU.mult).then_inc(s_osc, 1)
            pool.wait_ge(s_nw, 5)
            body(0)
            with pool.Fori(1, SEQ_TILES) as p:
                body(p)

        @stage("sync")
        def _(sp):
            sp.dma_start(out_norm[:, :], a["out_norm"]).then_inc(s_onw, 16)
            sp.wait_ge(s_ivz, 2)
            sp.wait_ge(s_vout, 16 * HEADS)
            sp.wait_ge(s_aout, 16 * HEADS)
            sp.wait_ge(s_conv, 12 * HEADS)

            def weights(p):
                for k in range(2):
                    sp.wait_ge(s_wo, p * 8 + (4 * k + 4))
                    sp.dma_start(merge_w[k][:, :], at_head(a["merge_w"], p * 2 + k)).then_inc(s_mw[k], 16)

            def pair(i):
                if not (isinstance(i, int) and i == 0):
                    weights(i + (-1))
                for k in range(2):
                    wait(sp, s_oc, i * 8 + (4 * k - 4))
                    sp.dma_start(reads_in[k], at_head(scratch["reads"], i * 2 + k)).then_inc(s_ri[k], 16)
                    sp.dma_start(values_in[k], at_head(scratch["values"], i * 2 + k)).then_inc(s_ri[k], 16)
                sp.wait_ge(s_inv, i + 1)
                stored = at_head(scratch["inverses"].rearrange("(s h) b m -> s (h b) m", s=SEQ_TILES), i)
                sp.dma_start(stored, at_pair(inverse, i)[:, 0:T * T]).then_inc(s_invd, 16)
                sp.wait_ge(s_invd, i * 16 + 16)
                for k in range(2):
                    for q in range(4):
                        rows = slice(T * q, T * q + T)
                        dst = inv_diag[k].rearrange("p (g i) -> p g i", i=P)[rows, :, rows]
                        src = at_head(scratch["inverses"], i * 2 + k).rearrange("(g q) (j i) -> q j g i", q=4, i=T)[q]
                        sp.dma_start(dst, src).then_inc(s_ri[k], 16)
            pair(0)
            with sp.Fori(1, SEQ_TILES) as i:
                pair(i)
            weights(SEQ_TILES - 1)

        @stage("tensor")
        def _(pe):
            pe.wait_ge(s_pk, 12 * HEADS)
            for n in range(TILES):
                pe.matmul(bank[4 + n][:, :], ident[:, :], dtile(residual, n), start=True, stop=False,
                          skip_group_check=True).then_inc(s_wo, 2)

            def merge(p):
                for t in range(8):
                    k, n = t // 4, t % 4
                    if n == 0:
                        pe.wait_ge(s_mw[k], p * 16 + 16)
                    if t >= 2:
                        pe.wait_ge(s_gs, p * 8 + (t - 1))
                    if t == 0:
                        pe.wait_ge(s_dc, p * 8 + 8)
                    for j in range(4):
                        g = 4 * n + j
                        mm = pe.matmul(bank[n % 2][:, j * P:(j + 1) * P], gate_low[:, g * P:(g + 1) * P],
                                       merge_w[k][:, 0:P], start=True, stop=True, skip_group_check=True)
                    mm.then_inc(s_gt, 1)
                for t in range(9):
                    if t < 8:
                        pe.wait_ge(s_gd, p * 32 + (4 * t + 4))
                        if t >= 2:
                            pe.wait_ge(s_ots, p * 8 + (t - 1))
                        if t == 0:
                            pe.wait_ge(s_oc, p * 8 + 8)
                        for j in range(4):
                            mm = pe.transpose(bank[2 + t % 2][:, j * P:(j + 1) * P],
                                              gates[t][:, j * P:(j + 1) * P], ident[:, :])
                        mm.then_inc(s_ot, 1)
                    if t > 0:
                        k, n = (t - 1) // 4, (t - 1) % 4
                        pe.wait_ge(s_ots, p * 8 + t)
                        settled(pe)
                        pe.matmul(bank[4 + n][:, :], merge_w[k][:, P:2 * P],
                                  of_pair(outputs, p, k, slice(n * TILE, (n + 1) * TILE)), start=False,
                                  stop=False, skip_group_check=True).then_inc(s_wo, 1)

            def read(p):
                for k in range(2):
                    pe.wait_ge(s_ri[k], p * 96 + 96)
                    if isinstance(p, int):
                        pe.wait_ge(s_gkc, 2)
                    else:
                        pe.wait_ge(s_gs, p * 8)
                        pe.wait_ge(s_ots, p * 8)
                    at = p * 8 + 4 * k

                    def deltas(n):
                        wait(pe, s_dc, at + (n - 1))
                        for j in range(4):
                            cols = slice((4 * n + j) * P, (4 * n + j + 1) * P)
                            mm = pe.matmul(bank[n % 2][:, j * P:(j + 1) * P], inv_diag[k][:, cols],
                                           values_in[k][:, cols], start=True, stop=True, skip_group_check=True)
                        mm.then_inc(s_dp, 1)

                    deltas(0)
                    for n in range(TILES):
                        if n + 1 < TILES:
                            deltas(n + 1)
                        pe.wait_ge(s_dc, at + (n + 1))
                        wait(pe, s_oc, at + (n - 1))
                        for j in range(4):
                            cols = slice((4 * n + j) * P, (4 * n + j + 1) * P)
                            mm = pe.matmul(bank[2 + n % 2][:, j * P:(j + 1) * P], reads_in[k][:, cols],
                                           delta[:, n % 2, j * P:(j + 1) * P], start=True, stop=True,
                                           skip_group_check=True)
                        mm.then_inc(s_op, 1)
            read(0)
            with pe.Fori(1, SEQ_TILES) as s:
                merge(s + (-1))
                read(s)
            merge(SEQ_TILES - 1)

        @stage("scalar")
        def _(act):
            def merge(p):
                act.preload_act_table(ACT.Sqrt)
                scales = both_heads(out_scale, p)
                act.wait_ge(s_osc, p + 1)
                settled(act)
                act.activation(scales, scales, ACT.Sqrt, scale=1.0 / D, bias=epsilons[:, 0:1]).then_inc(s_oroot, 1)
                act.preload_act_table(ACT.Sigmoid)
                for t in range(8):
                    act.wait_ge(s_gt, p * 8 + (t + 1))
                    act.activation(gates[t], bank[t % 2][:, :], ACT.Sigmoid).then_inc(s_gs, 1)
                for t in range(8):
                    act.wait_ge(s_ot, p * 8 + (t + 1))
                    settled(act)
                    act.activation(of_pair(outputs, p, t // 4, slice(t % 4 * TILE, (t % 4 + 1) * TILE)),
                                   bank[2 + t % 2][:, :], ACT.Copy, scale=out_norm[:, 0:1]).then_inc(s_ots, 1)

            def read(p):
                for k in range(2):
                    at = p * 8 + 4 * k
                    for n in range(TILES):
                        act.wait_ge(s_dp, at + (n + 1))
                        wait(act, s_op, at + (n - 1))
                        act.activation(delta[:, n % 2, :], bank[n % 2][:, :], ACT.Copy).then_inc(s_dc, 1)
                        if n >= 1:
                            out_tile(p, k, n - 1)
                    out_tile(p, k, TILES - 1)

            def out_tile(p, k, n):
                act.wait_ge(s_op, p * 8 + (4 * k + n + 1))
                for j in range(4):
                    g = 4 * n + j
                    settled(act)
                    wait(act, s_osq, p * 32 + (16 * k + g))
                    settled(act)
                    act.activation(square_scrap, bank[2 + n % 2][:, j * P:(j + 1) * P], ACT.Square,
                                   accum_out=of_pair(out_sq, p, k, slice(g, g + 1))).then_inc(s_osq, 1)
                act.activation(of_pair(outputs, p, k, slice(n * TILE, (n + 1) * TILE)), bank[2 + n % 2][:, :],
                               ACT.Copy).then_inc(s_oc, 1)

            act.wait_ge(s_onw, 16)
            act.wait_ge(s_eps, 2)
            read(0)
            with act.Fori(1, SEQ_TILES) as s:
                merge(s + (-1))
                read(s)
            merge(SEQ_TILES - 1)

        def by_time(array):
            return array.rearrange("p (t b) -> p b t", b=B)

        def batch_first(array):
            return array.rearrange("p (b t) -> p b t", t=T)

        def step_tile(array, t):
            return array[:, t * B:(t + 1) * B] if isinstance(t, int) else array[:, ds(t * B, B)]

        def pairs_loop(engine, body, last_peeled=False):
            body(0, False)
            with engine.Fori(1, T // 2 - (1 if last_peeled else 0)) as i:
                body(i * 2, False)
            if last_peeled:
                body(T - 2, True)

        def gate_inputs(s_xp, q0, gates, w_cols, work, xw, bias, start, src, evacuated):
            @stage("tensor")
            def _(pe):
                for semaphore, value in start:
                    pe.wait_ge(semaphore, value)
                for q in range(4 * gates):
                    wait(pe, evacuated, q0 + q - 3)
                    pe.matmul(bank[q % 4][:, :], w_cols(q // 4), dtile(src, q % 4), start=True,
                              stop=True).then_inc(s_xp, 1)

            @stage("scalar")
            def _(act):
                act.preload_act_table(ACT.Sigmoid)
                for semaphore, value in start:
                    act.wait_ge(semaphore, value)
                for q in range(4 * gates):
                    act.wait_ge(s_xp, q0 + q + 1)
                    n = q % 4
                    dst = by_time(xw[:, q // 4, :])[:, n * 16:(n + 1) * 16, :]
                    act.activation(dst, batch_first(bank[n][:, :]), ACT.Identity,
                                   bias=bias(q // 4)).then_inc(evacuated, 1)

        lstm_semaphores = tuple(sem(f"lstm_{name}") for name in (
            "weights_loaded", "gate_inputs_stored", "cell_cleared", "g_ready", "if_ready", "o_ready", "g_tanh", "if_sigmoid",
            "o_sigmoid", "cell_products", "cell_ready", "cell_tanh", "hidden_ready", "hidden_kept", "gate_inputs_ready"))

        def lstm(use, w_dram, hs, start, work_free):
            xw = arena[:, 4:8, :]
            work = tok(8)
            state = tok(9)
            w_x = work[:, 0:4 * P]
            w_h = work[:, 4 * P:8 * P]
            bias = work[:, 8 * P:8 * P + 4]
            h_ring = [state[:, k * B:(k + 1) * B] for k in range(2)]
            gc = [state[:, (2 + 2 * k) * B:(4 + 2 * k) * B] for k in range(2)]
            sig = [state[:, (6 + 3 * k) * B:(9 + 3 * k) * B] for k in range(2)]
            prod = [state[:, (12 + 2 * k) * B:(14 + 2 * k) * B] for k in range(2)]
            tanh_c = [state[:, (16 + k) * B:(17 + k) * B] for k in range(2)]
            (s_w, s_ev, s_c0, s_gg, s_gi, s_go, s_tg, s_sg, s_so, s_pr, s_c, s_tc, s_h, s_hs, s_xp) = lstm_semaphores
            tiles0 = use * 28
            T0 = use * T

            @stage("sync")
            def _(sp):
                sp.wait_ge(*work_free)
                sp.dma_start(work[:, 0:8 * P + 4], w_dram).then_inc(s_w, 16)

            gate_inputs(s_xp, tiles0, 4, lambda g: w_x[:, g * P:(g + 1) * P], work, xw, lambda g: bias[:, g:g + 1],
                        start + [(s_w, use * 16 + 16)], residual, s_ev)

            @stage("vector")
            def _(dve):
                for semaphore, value in start:
                    dve.wait_ge(semaphore, value)
                dve.memset(gc[0][:, B:2 * B], 0.0).then_inc(s_c0, 1)
                dve.wait_ge(s_c0, use + 1)

                def body(t0, last):
                    for p in range(2):
                        t, u = t0 + p, t0 + (p + T0)
                        dve.wait_ge(s_sg, u + 1)
                        dve.tensor_tensor(prod[p][:, B:2 * B], sig[p][:, B:2 * B], gc[p][:, B:2 * B],
                                          ALU.mult).then_inc(s_pr, 1)
                        dve.wait_ge(s_tg, u + 1)
                        dve.tensor_tensor(prod[p][:, 0:B], sig[p][:, 0:B], gc[p][:, 0:B], ALU.mult).then_inc(s_pr, 1)
                        dve.wait_ge(s_pr, u * 2 + 2)
                        wait(dve, s_tc, u - 1)
                        dve.tensor_tensor(gc[1 - p][:, B:2 * B], prod[p][:, 0:B], prod[p][:, B:2 * B],
                                          ALU.add).then_inc(s_c, 1)
                        dve.wait_ge(s_so, u + 1)
                        dve.wait_ge(s_tc, u + 1)
                        wait(dve, s_hs, u - 1)
                        dve.tensor_tensor(h_ring[p], sig[p][:, 2 * B:3 * B], tanh_c[p], ALU.mult).then_inc(s_h, 1)
                pairs_loop(dve, body)

            @stage("scalar")
            def _(act):
                def body(t0, last):
                    for p in range(2):
                        t, u = t0 + p, t0 + (p + T0)
                        act.wait_ge(s_gi, u + 1)
                        wait(act, s_pr, u * 2 + (-2))
                        act.activation(sig[p][:, 0:2 * B], bank[6 + p][:, 0:2 * B], ACT.Sigmoid).then_inc(s_sg, 1)
                        act.wait_ge(s_gg, u + 1)
                        act.activation(gc[p][:, 0:B], bank[4 + p][:, 0:B], ACT.Tanh).then_inc(s_tg, 1)
                        act.wait_ge(s_go, u + 1)
                        wait(act, s_h, u - 1)
                        act.activation(sig[p][:, 2 * B:3 * B], bank[p][:, 0:B], ACT.Sigmoid).then_inc(s_so, 1)
                        act.wait_ge(s_c, u + 1)
                        act.activation(tanh_c[p], gc[1 - p][:, B:2 * B], ACT.Tanh).then_inc(s_tc, 1)
                pairs_loop(act, body)

            @stage("tensor")
            def _(pe):
                def inject(t, p):
                    u = t + T0
                    wait(pe, s_tg, u - 1)
                    pe.matmul(bank[4 + p][:, 0:B], ident[:, :], step_tile(xw[:, 3, :], t), start=True, stop=False,
                              skip_group_check=True)
                    wait(pe, s_sg, u - 1)
                    x = xw[:, 0:2, :]
                    x = x[:, :, t * B:(t + 1) * B] if isinstance(t, int) else x[:, :, ds(t * B, B)]
                    pe.matmul(bank[6 + p][:, 0:2 * B].rearrange("p (g b) -> p g b", g=2), ident[:, :], x, start=True,
                              stop=False, skip_group_check=True)
                    wait(pe, s_so, u - 1)
                    pe.matmul(bank[p][:, 0:B], ident[:, :], step_tile(xw[:, 2, :], t), start=True, stop=False,
                              skip_group_check=True)

                def body(t0, last):
                    for p in range(2):
                        t, u = t0 + p, t0 + (p + T0)
                        wait(pe, s_h, u)
                        h = cond[:, :] if isinstance(t, int) and t == 0 else h_ring[1 - p]
                        for g in range(2):
                            mm = pe.matmul(bank[6 + p][:, g * B:(g + 1) * B], w_h[:, g * P:(g + 1) * P], h,
                                           start=False, stop=(g == 1), skip_group_check=True)
                        mm.then_inc(s_gi, 1)
                        pe.matmul(bank[4 + p][:, 0:B], w_h[:, 3 * P:4 * P], h, start=False, stop=True,
                                  skip_group_check=True).then_inc(s_gg, 1)
                        pe.matmul(bank[p][:, 0:B], w_h[:, 2 * P:3 * P], h, start=False, stop=True,
                                  skip_group_check=True).then_inc(s_go, 1)
                        if not (last and p == 1):
                            inject(t + 1, 1 - p)
                pe.wait_ge(s_ev, tiles0 + 16)
                inject(0, 0)
                pairs_loop(pe, body, last_peeled=True)

            @stage("gpsimd")
            def _(pool):
                for semaphore, value in start:
                    pool.wait_ge(semaphore, value)

                def body(t0, last):
                    for p in range(2):
                        t, u = t0 + p, t0 + (p + T0)
                        pool.wait_ge(s_h, u + 1)
                        settled(pool)
                        dst = batch_first(hs)[:, :, t:t + 1] if isinstance(t, int) else batch_first(hs)[:, :, ds(t, 1)]
                        pool.tensor_copy(dst, h_ring[p].unsqueeze(2)).then_inc(s_hs, 1)
                pairs_loop(pool, body)

            return s_hs, T0 + T

        s_la, LA = lstm(0, a["lstm_a_w"], tok(1), [(s_merged, 4)], (s_invd, 16 * SEQ_TILES))
        load_first_experts(MOE_A, (15, 16), a["moe_a_w"], (s_merged, 4))

        E8 = 8
        route = tok(21)[:, 0:7 * P].rearrange("p (k n) -> p k n", k=7)
        router_w = sbuf("router_weights", [P, 2 * E8 + 1])
        s_rw = sem("router_weights_loaded")

        @stage("sync")
        def _(sp):
            sp.dma_start(router_w[:, :], a["router_w"]).then_inc(s_rw, 16)

        TOP1_STEPS = 12
        s_lg = sem("gate_logits_ready_by_token")
        s_st = sem("token_gate_steps")
        s_ex = sem("token_gate_exp")
        s_tr = sem("token_gates_transposed")
        s_gc = sem("token_gates_copied")
        s_dr = sem("token_gates_stored")

        def token_gates(use, src, src_ready, w, softmax_first, top, dram):
            steps = 3 + (3 if softmax_first else 0) + 5 + (1 if softmax_first else 4)
            step0 = use * TOP1_STEPS
            wide_a = tok(18)[:, 0:GROUPS * 64].rearrange("p (g e j) -> p g e j", g=GROUPS, e=E8)
            wide_b = tok(19)[:, 0:GROUPS * 64].rearrange("p (g e j) -> p g e j", g=GROUPS, e=E8)
            small = tok(20)[:, 0:4 * GROUPS].rearrange("p (k g) -> p k g", k=4)

            @stage("tensor")
            def _(pe):
                pe.wait_ge(*src_ready)
                pe.wait_ge(s_rw, 16)
                for g in range(GROUPS):
                    mm = pe.matmul(bank[6][:, g * E8:(g + 1) * E8], src[:, g * P:(g + 1) * P], w, start=True,
                                   stop=True, skip_group_check=True)
                mm.then_inc(s_lg, 1)

            @stage("vector")
            def _(dve):
                logits, shifted, exps, scores, rank, kept, gate = (
                    route[:, k, :].rearrange("p (g e) -> p g e", e=E8) for k in range(7))
                top_v, total, inverse = (small[:, k, :] for k in range(3))
                n = step0

                def step(instruction):
                    nonlocal n
                    instruction.then_inc(s_st, 1)
                    n += 1
                    dve.wait_ge(s_st, n)

                def wide(x):
                    return x.unsqueeze(2).to_broadcast([P, GROUPS, E8])

                dve.wait_ge(s_lg, use + 1)
                step(dve.tensor_copy(route[:, 0, :], bank[6][:, 0:P]))
                step(dve.tensor_reduce(top_v, logits, AX.X, ALU.max))
                step(dve.tensor_tensor(shifted, logits, wide(top_v), ALU.subtract))
                dve.wait_ge(s_ex, use + 1)
                if softmax_first:
                    step(dve.tensor_reduce(total, exps, AX.X, ALU.add))
                    step(dve.reciprocal(inverse, total))
                    step(dve.tensor_tensor(scores, exps, wide(inverse), ALU.mult))
                    n = ranks(dve, s_st, n, scores, wide_a, wide_b, rank, GROUPS, E8)
                    dve.wait_ge(s_st, n)
                    step(dve.scalar_tensor_tensor(out=gate, in0=rank, scalar=top - 0.5, in1=scores, op0=ALU.is_lt,
                                                  op1=ALU.mult))
                else:
                    n = ranks(dve, s_st, n, logits, wide_a, wide_b, rank, GROUPS, E8)
                    dve.wait_ge(s_st, n)
                    step(dve.scalar_tensor_tensor(out=kept, in0=rank, scalar=top - 0.5, in1=exps, op0=ALU.is_lt,
                                                  op1=ALU.mult))
                    step(dve.tensor_reduce(total, kept, AX.X, ALU.add))
                    step(dve.reciprocal(inverse, total))
                    step(dve.tensor_tensor(gate, kept, wide(inverse), ALU.mult))
                assert n == step0 + steps
                dve.wait_ge(s_tr, use + 1)
                dve.tensor_copy(route[:, 5, :], bank[7][:, 0:P]).then_inc(s_gc, 1)

            @stage("scalar")
            def _(act):
                act.wait_ge(s_st, step0 + 3)
                act.activation(route[:, 2, :], route[:, 1, :], ACT.Exp).then_inc(s_ex, 1)

            def transpose_gates(pe):
                pe.wait_ge(s_st, step0 + steps)
                pe.transpose(bank[7][:, 0:P], route[:, 6, :], ident[:, :]).then_inc(s_tr, 1)

            @stage("gpsimd")
            def _(pool):
                pool.wait_ge(s_gc, use + 1)
                pool.dma_start(dram.rearrange("g e p -> (g e) p"), route[:, 5, :]).then_inc(s_dr, 16)
                pool.wait_ge(s_dr, use * 16 + 16)
            return (s_dr, use * 16 + 16), transpose_gates

        
        s_gru_w = sem("gru_weights_loaded")

        @stage("sync")
        def _(sp):
            sp.wait_ge(s_la, LA)
            sp.dma_start(tok(8)[:, 0:7 * P + 7], a["gru_w"]).then_inc(s_gru_w, 16)

        low = tok(1)
        low_sq, low_norm = tok(2), tok(10)
        token_scale = tok(3)[:, 0:GROUPS]
        scale_rows = tok(3)[0:GROUPS, P:2 * P]
        s_ms = sem("moe_a_squares_ready")
        s_mb = sem("moe_a_square_sums_ready")
        s_mr = sem("moe_a_roots_ready")
        s_mi = sem("moe_a_scales_ready")
        s_mt = sem("moe_a_scales_transposed")
        s_mc = sem("moe_a_scale_rows_copied")
        s_ml = sem("moe_a_scales_spread")
        s_mn = sem("moe_a_normed")

        @stage("scalar")
        def _(act):
            act.preload_act_table(ACT.Sqrt)
            act.wait_ge(s_la, LA)
            for n in range(TILES):
                act.activation(dtile(low_sq, n), dtile(low, n), ACT.Square).then_inc(s_ms, 1)
            act.wait_ge(s_eps, 2)
            act.wait_ge(s_mb, 1)
            act.activation(token_scale, bank[5][:, 0:GROUPS], ACT.Sqrt, scale=1.0 / D,
                           bias=epsilons[:, 1:2]).then_inc(s_mr, 1)
            act.wait_ge(s_mt, 1)
            act.activation(scale_rows, bank[4][0:GROUPS, 0:P], ACT.Copy).then_inc(s_mc, 1)

        @stage("tensor")
        def _(pe):
            for g in range(GROUPS):
                pe.wait_ge(s_ms, g // 4 + 1)
                mm = pe.matmul(bank[5][:, g:g + 1], low_sq[:, g * P:(g + 1) * P], ones[:, 0:1], start=True,
                               stop=True, skip_group_check=True)
            mm.then_inc(s_mb, 1)
            pe.wait_ge(s_mi, 1)
            pe.transpose(bank[4][0:GROUPS, 0:P], token_scale, ident[:, :]).then_inc(s_mt, 1)
            pe.wait_ge(s_mc, 1)
            for n in range(TILES):
                for j in range(4):
                    g = 4 * n + j
                    mm = pe.matmul(bank[n][:, j * P:(j + 1) * P], ident[0:GROUPS, g:g + 1].to_broadcast([GROUPS, P]),
                                   scale_rows, start=True, stop=True, skip_group_check=True)
                mm.then_inc(s_ml, 1)

        @stage("vector")
        def _(dve):
            dve.wait_ge(s_rw, 16)
            dve.wait_ge(s_mr, 1)
            dve.reciprocal(token_scale, token_scale).then_inc(s_mi, 1)
            for n in range(TILES):
                dve.wait_ge(s_ml, n + 1)
                dve.scalar_tensor_tensor(out=dtile(low_norm, n), in0=dtile(low, n), scalar=router_w[:, 16:17],
                                         in1=bank[n][:, :], op0=ALU.mult, op1=ALU.mult).then_inc(s_mn, 1)

        moe_a_gates, moe_a_transposes = token_gates(0, low_norm, (s_mn, 4), router_w[:, 0:E8], True, 1,
                                  scratch["moe_a_gate"])
        s_ma, MA = moe(MOE_A, low_norm, residual, hidden=(11, 12), spread=(13, 14), weights=(15, 16), work=17,
                       hidden_act=ACT.Silu, w_dram=a["moe_a_w"],
                       spread_src=lambda e: scratch["moe_a_gate"][:, e, :].partition_broadcast(P),
                       src_ready=(s_mn, 4), gates_ready=moe_a_gates, prefetched=True,
                       transpose_gates=moe_a_transposes)

        def gru(hs, y, start):
            xw = arena[:, 4:7, :]
            work, state = tok(8), tok(9)
            w_x, w_h, w_q = work[:, 0:3 * P], work[:, 3 * P:6 * P], work[:, 6 * P:7 * P]
            raw_bias = work[:, 7 * P:7 * P + 7]
            bias = work[:, 7 * P + 8:7 * P + 11]
            h_ring = [state[:, k * B:(k + 1) * B] for k in range(2)]
            r_s, z_s, rh, zh, oz, ht, ozht = ([state[:, (2 + 2 * j + k) * B:(3 + 2 * j + k) * B] for k in range(2)]
                                              for j in range(7))
            s_b = sem("gru_biases_summed")
            s_ev = lstm_semaphores[1]
            s_gr, s_gz_, s_gh = sem("gru_r_ready"), sem("gru_z_ready"), sem("gru_candidate_ready")
            s_sr, s_sz, s_th = sem("gru_r_sigmoid"), sem("gru_z_sigmoid"), sem("gru_candidate_tanh")
            s_rh, s_zh, s_oh = sem("gru_reset_hidden"), sem("gru_update_parts"), sem("gru_new_part")
            s_h, s_hs = sem("gru_hidden_ready"), sem("gru_hidden_kept")
            s_yp, s_y = sem("gru_outputs_projected"), sem("gru_outputs_ready")

            @stage("vector")
            def _(dve):
                dve.wait_ge(s_gru_w, 16)
                dve.tensor_tensor(bias, raw_bias[:, 0:3], raw_bias[:, 3:6], ALU.add).then_inc(s_b, 1)

            gate_inputs(lstm_semaphores[-1], 16, 3, lambda g: w_x[:, g * P:(g + 1) * P], work, xw, lambda g: bias[:, g:g + 1],
                        start + [(s_b, 1)], residual, s_ev)

            @stage("vector")
            def _(dve):
                def body(t0, last):
                    for p in range(2):
                        t = t0 + p
                        h = cond[:, :] if isinstance(t, int) and t == 0 else h_ring[1 - p]
                        wait(dve, s_h, t)
                        dve.wait_ge(s_sr, t + 1)
                        dve.tensor_tensor(rh[p], r_s[p], h, ALU.mult).then_inc(s_rh, 1)
                        dve.wait_ge(s_sz, t + 1)
                        dve.tensor_tensor(zh[p], z_s[p], h, ALU.mult).then_inc(s_zh, 1)
                        dve.tensor_scalar(oz[p], z_s[p], -1.0, 1.0, ALU.mult, ALU.add).then_inc(s_zh, 1)
                        dve.wait_ge(s_th, t + 1)
                        dve.wait_ge(s_zh, t * 2 + 2)
                        dve.tensor_tensor(ozht[p], oz[p], ht[p], ALU.mult).then_inc(s_oh, 1)
                        dve.wait_ge(s_oh, t + 1)
                        wait(dve, s_hs, t - 1)
                        dve.tensor_tensor(h_ring[p], ozht[p], zh[p], ALU.add).then_inc(s_h, 1)
                pairs_loop(dve, body)

            @stage("scalar")
            def _(act):
                def body(t0, last):
                    for p in range(2):
                        t = t0 + p
                        act.wait_ge(s_gr, t + 1)
                        act.activation(r_s[p], bank[p][:, 0:B], ACT.Sigmoid).then_inc(s_sr, 1)
                        act.wait_ge(s_gz_, t + 1)
                        act.activation(z_s[p], bank[2 + p][:, 0:B], ACT.Sigmoid).then_inc(s_sz, 1)
                        act.wait_ge(s_gh, t + 1)
                        act.activation(ht[p], bank[4 + p][:, 0:B], ACT.Tanh).then_inc(s_th, 1)
                pairs_loop(act, body)
                for n in range(TILES):
                    act.wait_ge(s_yp, n + 1)
                    act.activation(dtile(y, n), bank[n][:, :], ACT.Identity, bias=raw_bias[:, 6:7]).then_inc(s_y, 1)

            @stage("tensor")
            def _(pe):
                def inject(t, p, which):
                    gate, at, freed = [(1, p, s_sr), (0, 2 + p, s_sz), (2, 4 + p, s_th)][which]
                    wait(pe, freed, t - 1)
                    pe.matmul(bank[at][:, 0:B], ident[:, :], step_tile(xw[:, gate, :], t), start=True, stop=False,
                              skip_group_check=True)

                def body(t0, last):
                    for p in range(2):
                        t = t0 + p
                        more = not (last and p == 1)
                        wait(pe, s_h, t)
                        h = cond[:, :] if isinstance(t, int) and t == 0 else h_ring[1 - p]
                        pe.matmul(bank[p][:, 0:B], w_h[:, P:2 * P], h, start=False, stop=True,
                                  skip_group_check=True).then_inc(s_gr, 1)
                        pe.matmul(bank[2 + p][:, 0:B], w_h[:, 0:P], h, start=False, stop=True,
                                  skip_group_check=True).then_inc(s_gz_, 1)
                        if more:
                            inject(t + 1, 1 - p, 0)
                        pe.wait_ge(s_rh, t + 1)
                        pe.matmul(bank[4 + p][:, 0:B], w_h[:, 2 * P:3 * P], rh[p], start=False, stop=True,
                                  skip_group_check=True).then_inc(s_gh, 1)
                        if more:
                            inject(t + 1, 1 - p, 1)
                            inject(t + 1, 1 - p, 2)
                pe.wait_ge(s_ev, 28)
                for which in range(3):
                    inject(0, 0, which)
                pairs_loop(pe, body, last_peeled=True)
                pe.wait_ge(s_hs, T)
                pe.wait_ge(s_th, T)
                pe.wait_ge(s_sz, T)
                for n in range(TILES):
                    pe.matmul(bank[n][:, :], w_q, dtile(hs, n), start=True, stop=True).then_inc(s_yp, 1)

            @stage("gpsimd")
            def _(pool):
                for semaphore, value in start:
                    pool.wait_ge(semaphore, value)

                def body(t0, last):
                    for p in range(2):
                        t = t0 + p
                        pool.wait_ge(s_h, t + 1)
                        settled(pool)
                        dst = batch_first(hs)[:, :, t:t + 1] if isinstance(t, int) else batch_first(hs)[:, :, ds(t, 1)]
                        pool.tensor_copy(dst, h_ring[p].unsqueeze(2)).then_inc(s_hs, 1)
                pairs_loop(pool, body)

            return s_y, TILES

        s_gru, GRU = gru(tok(1), tok(2), [(s_ma, MA)])
        HEAD_PAIRS, HD = 8, 64
        att_in = tok(2)
        queries, keys = [tok(3), tok(4)], [tok(5), tok(6)]
        value_rows = [tok(7), tok(17)]
        soft = tok(10).rearrange("p (x h m) -> p x h m", x=2, h=2)
        probs_diag = arena[:, 11:13, :].rearrange("p a n -> p (a n)").rearrange("p (g h m) -> p g h m", g=GROUPS, h=2)
        att_out = [tok(13), tok(14)]
        qkv_slot = [tok(15)[:, k * 3 * P:(k + 1) * 3 * P] for k in range(2)]
        po_slot = [tok(15)[:, (6 + k) * P:(7 + k) * P] for k in range(2)]
        causal_wide = tok(16)[:, 0:4 * T].rearrange("p (q n) -> p q n", q=4)
        causal = tok(16)[:, 4 * T:5 * T]
        row_max, row_sum, row_inv = (tok(16)[:, (6 + j) * T:(7 + j) * T].rearrange("p (h g) -> p h g", h=2) for j in range(3))
        s_az = sem("attn_constants_made")
        s_aw = [sem(f"attn_qkv_weights_loaded{k}") for k in range(2)]
        s_ao = [sem(f"attn_out_weights_loaded{k}") for k in range(2)]
        s_at = sem("attn_ring_tile_ready")
        s_ae = sem("attn_ring_tile_copied")
        s_alg = sem("attn_logits_ready")
        s_asm = sem("attn_softmax_steps")
        s_aex = sem("attn_exp_done")
        s_awo = sem("attn_products_ready")
        s_att = sem("attn_residual_updated")
        SOFT = 20

        def ring(p, u):
            if isinstance(p, int) and p == HEAD_PAIRS - 1 and u >= 12:
                return p * 16 + u
            if u >= 12:
                return p * 16 + (12 + u)
            return u if isinstance(p, int) and p == 0 else p * 16 + (u - 4)

        def attn_loop(engine, body, drain=None):
            body(0, 0)
            with engine.Fori(1, HEAD_PAIRS // 2) as i:
                body(i * 2 + (-1), 1)
                body(i * 2, 0)
            body(HEAD_PAIRS - 1, 1)
            if drain:
                drain(HEAD_PAIRS - 1, 1)

        @stage("gpsimd")
        def _(pool):
            pool.wait_ge(s_gru, GRU)
            pool.memset(probs_diag[:, :, :, :], 0.0).then_inc(s_az, 1)
            pool.memset(causal_wide, 0.0).then_inc(s_az, 1)
            pool.wait_ge(s_az, 2)
            pool.affine_select(out=causal_wide, in_=causal_wide, compare_op=ALU.is_ge, fill=-1e30, base=0,
                               pattern=[[-T, 4], [-1, T]], channel_multiplier=1).then_inc(s_az, 1)
            pool.wait_ge(s_az, 3)
            for q in range(4):
                rows = slice(q * T, (q + 1) * T)
                pool.tensor_copy(causal[rows, :], causal_wide[rows, q, :]).then_inc(s_az, 1)

        @stage("sync")
        def _(sp):
            sp.wait_ge(s_ma, MA)

            def load(p, k, first):
                if not first:
                    sp.wait_ge(s_at, ring(p + (-2), 11) + 1)
                src = at_head(a["attn_w"], p)
                sp.dma_start(qkv_slot[k], src[:, 0:3 * P]).then_inc(s_aw[k], 16)
                if not first:
                    sp.wait_ge(s_awo, p * 4 + (-4))
                sp.dma_start(po_slot[k], src[:, 3 * P:4 * P]).then_inc(s_ao[k], 16)
            load(0, 0, True)
            load(1, 1, True)
            load(2, 0, False)
            load(3, 1, False)
            with sp.Fori(2, HEAD_PAIRS // 2) as i:
                load(i * 2, 0, False)
                load(i * 2 + 1, 1, False)

        @stage("tensor")
        def _(pe):
            def loads_of(p, k):
                return p * 8 + (16 if k == 0 else 8)

            def project(p, k):
                pe.wait_ge(s_aw[k], loads_of(p, k))
                for u in range(12):
                    wait(pe, s_ae, ring(p, u) + (-1))
                    out_bank = bank[u % 2]
                    if u < 8:
                        pe.matmul(out_bank[:, :], qkv_slot[k][:, (u // 4) * P:(u // 4 + 1) * P],
                                  dtile(att_in, u % 4), start=True, stop=True).then_inc(s_at, 1)
                        continue
                    for j in range(4):
                        g = 4 * (u - 8) + j
                        mm = pe.matmul(out_bank[:, j * P:(j + 1) * P], att_in[:, g * P:(g + 1) * P],
                                       qkv_slot[k][:, 2 * P:3 * P], start=True, stop=True, skip_group_check=True)
                    mm.then_inc(s_at, 1)

            def logits(p, k):
                pe.wait_ge(s_ae, ring(p, 7) + 1)
                settled(pe)
                for h in range(2):
                    half = slice(HD * h, HD * h + HD)
                    for g in range(GROUPS):
                        for q in range(4):
                            cols = slice((4 * g + q) * T, (4 * g + q + 1) * T)
                            mm = pe.matmul(bank[2 + h][q * T:(q + 1) * T, g * T:(g + 1) * T], queries[k][half, cols],
                                           keys[k][half, cols], start=True, stop=True, skip_group_check=True,
                                           tile_position=(HD * h, q * T))
                    mm.then_inc(s_alg, 1)

            def mix_values(p, k):
                pe.wait_ge(s_asm, p * SOFT + SOFT)
                pe.wait_ge(s_ae, ring(p, 11) + 1)
                for n in range(TILES):
                    pe.wait_ge(s_ae, ring(p, 12 + n) + (-1))
                    for h in range(2):
                        for j in range(4):
                            g = 4 * n + j
                            mm = pe.matmul(bank[n % 2][HD * h:HD * h + HD, j * P:(j + 1) * P],
                                           value_rows[k][:, g * P + HD * h:g * P + HD * h + HD],
                                           probs_diag[:, g, h, :], start=True, stop=True, skip_group_check=True)
                    mm.then_inc(s_at, 1)

            def project_out(p, k):
                pe.wait_ge(s_ao[k], loads_of(p, k))
                for n in range(TILES):
                    pe.wait_ge(s_ae, ring(p, 12 + n) + 1)
                    pe.matmul(bank[4 + n][:, :], po_slot[k], dtile(att_out[k], n), start=False, stop=False,
                              skip_group_check=True).then_inc(s_awo, 1)

            def body(p, k):
                project(p, k)
                if not (isinstance(p, int) and p == 0):
                    mix_values(p + (-1), 1 - k)
                logits(p, k)
                if not (isinstance(p, int) and p == 0):
                    project_out(p + (-1), 1 - k)

            def drain(p, k):
                mix_values(p, k)
                project_out(p, k)

            pe.wait_ge(s_gru, GRU)
            pe.wait_ge(s_az, 7)
            for n in range(TILES):
                pe.matmul(bank[4 + n][:, :], ident[:, :], dtile(residual, n), start=True, stop=False,
                          skip_group_check=True)
            attn_loop(pe, body, drain)

        @stage("scalar")
        def _(act):
            act.preload_act_table(ACT.Exp)

            def copy(dst, p, u):
                act.wait_ge(s_at, ring(p, u) + 1)
                act.activation(dst, bank[u % 2][:, :], ACT.Copy).then_inc(s_ae, 1)

            def exponentials(p):
                for h in range(2):
                    act.wait_ge(s_asm, p * SOFT + (5 + h))
                    act.activation(soft[:, 1, h, :], soft[:, 0, h, :], ACT.Exp).then_inc(s_aex, 1)

            def outputs_of(p, k):
                for n in range(TILES):
                    copy(dtile(att_out[k], n), p, 12 + n)

            def body(p, k):
                first = isinstance(p, int) and p == 0
                for u in range(4):
                    copy(dtile(queries[k], u), p, u)
                if not first:
                    exponentials(p + (-1))
                for u in range(4):
                    copy(dtile(keys[k], u), p, 4 + u)
                for u in range(4):
                    copy(dtile(value_rows[k], u), p, 8 + u)
                if not first:
                    outputs_of(p + (-1), 1 - k)

            def drain(p, k):
                exponentials(p)
                outputs_of(p, k)
            attn_loop(act, body, drain)

        @stage("vector")
        def _(dve):
            dve.wait_ge(s_az, 7)
            scale = 1.0 / HD ** 0.5
            grid = [[soft[:, x, h, :].rearrange("p (g n) -> p g n", g=GROUPS) for h in range(2)] for x in range(2)]
            mask = causal.unsqueeze(1).to_broadcast([P, GROUPS, T])

            def wide(x):
                return x.unsqueeze(2).to_broadcast([P, GROUPS, T])

            def body(p, k):
                at = p * SOFT
                for h in range(2):
                    dve.wait_ge(s_alg, p * 2 + (h + 1))
                    wait(dve, s_asm, at)
                    dve.scalar_tensor_tensor(out=grid[0][h], in0=bank[2 + h][:, :].rearrange("p (g n) -> p g n", g=GROUPS),
                                             scalar=scale, in1=mask, op0=ALU.mult, op1=ALU.add).then_inc(s_asm, 1)
                for h in range(2):
                    dve.wait_ge(s_asm, at + (1 + h))
                    dve.tensor_reduce(row_max[:, h, :], grid[0][h], AX.X, ALU.max).then_inc(s_asm, 1)
                for h in range(2):
                    dve.wait_ge(s_asm, at + (3 + h))
                    dve.tensor_tensor(grid[0][h], grid[0][h], wide(row_max[:, h, :]), ALU.subtract).then_inc(s_asm, 1)
                for h in range(2):
                    dve.wait_ge(s_aex, p * 2 + (h + 1))
                    dve.tensor_reduce(row_sum[:, h, :], grid[1][h], AX.X, ALU.add).then_inc(s_asm, 1)
                for h in range(2):
                    dve.wait_ge(s_asm, at + (7 + h))
                    dve.reciprocal(row_inv[:, h, :], row_sum[:, h, :]).then_inc(s_asm, 1)
                for h in range(2):
                    dve.wait_ge(s_asm, at + (9 + h))
                    dve.tensor_tensor(grid[1][h], grid[1][h], wide(row_inv[:, h, :]), ALU.mult).then_inc(s_asm, 1)
                for h in range(2):
                    dve.wait_ge(s_asm, at + (11 + h))
                    for q in range(4):
                        rows = slice(q * T, (q + 1) * T)
                        dve.transpose(probs_diag[rows, :, h, rows], grid[1][h][rows, :, :]).then_inc(s_asm, 1)
            attn_loop(dve, body)
            dve.wait_ge(s_awo, 4 * HEAD_PAIRS)
            for n in range(TILES):
                dve.tensor_copy(dtile(residual, n), bank[4 + n][:, :]).then_inc(s_att, 1)


        s_lb, LB = lstm(1, a["lstm_b_w"], tok(1), [(s_att, TILES)], (s_gru, GRU))
        load_first_experts(MOE_B, (15, 16), a["moe_b_w"], (s_att, TILES))
        moe_b_gates, moe_b_transposes = token_gates(1, tok(1), (s_lb, LB), router_w[:, E8:2 * E8], False, 2,
                                  scratch["moe_b_gate"])
        s_mbx, MB = moe(MOE_B, tok(1), residual, hidden=(11, 12), spread=(13, 14), weights=(15, 16), work=17,
                        hidden_act="relu2", w_dram=a["moe_b_w"],
                        spread_src=lambda e: scratch["moe_b_gate"][:, e, :].partition_broadcast(P),
                        src_ready=(s_lb, LB), gates_ready=moe_b_gates, prefetched=True,
                        transpose_gates=moe_b_transposes)
        finish(residual, s_mbx, MB)

        @block.sync
        def _(sp):
            for f in programs["sync"]:
                f(sp)

        @block.tensor
        def _(pe):
            for f in programs["tensor"]:
                f(pe)

        @block.scalar
        def _(act):
            for f in programs["scalar"]:
                f(act)

        @block.vector
        def _(dve):
            for f in programs["vector"]:
                f(dve)

        @block.gpsimd
        def _(pool):
            for f in programs["gpsimd"]:
                f(pool)


def lay_out(i):
    def arr(name):
        return np.asarray(i[name])

    def chunked(w):
        lead, k, m = w.shape[:-2], w.shape[-2], w.shape[-1]
        return np.moveaxis(w.reshape(*lead, k // P, P, m), -3, -2).reshape(*lead, P, (k // P) * m)

    def columns(v):
        return np.swapaxes(v.reshape(*v.shape[:-1], v.shape[-1] // P, P), -1, -2)

    def stack(shared, experts):
        return np.concatenate([shared[None], experts], 0)

    d = {}
    d["x"] = arr("x").reshape(N, D).T
    d["cond"] = arr("cond_1024").T
    d["gate_in"] = np.concatenate([chunked(arr("L0_cond_gate_w")), arr("L0_cond_time_w")], 1)
    d["gate_rows"] = np.concatenate([arr("L0_cond_gate_b"), arr("L0_cond_time_b")])[None]
    d["mix_w"] = np.concatenate([
        stack(arr("L0_cond_sw1"), arr("L0_cond_ew1")),
        chunked(stack(arr("L0_cond_sw2"), arr("L0_cond_ew2"))),
        columns(stack(arr("L0_cond_sb1"), arr("L0_cond_eb1"))),
        columns(stack(arr("L0_cond_sb2"), arr("L0_cond_eb2")))], 2)
    d["low_w"] = np.concatenate([arr("L0_attn_Wfa").T, arr("L0_attn_Wga").T, arr("L0_attn_Wb").T], 1)
    d["head_cols"] = np.concatenate([arr("L0_attn_dt_bias").T,
                                     np.broadcast_to(arr("L0_attn_A_log")[None], (P, HEADS))], 1)
    heads = {n: arr(f"L0_attn_{n}").reshape(HEADS, P, P).swapaxes(1, 2) for n in ("Wq", "Wk", "Wv", "Wfb", "Wgb")}
    d["fb_w"] = heads["Wfb"]
    taps = [arr(f"L0_attn_w{n}_conv").reshape(HEADS, P, 4) for n in "qkv"]
    d["qkv_w"] = np.concatenate([heads["Wq"], heads["Wk"], heads["Wv"], *taps], 2)
    d["merge_w"] = np.concatenate([heads["Wgb"], arr("L0_attn_Wo").T.reshape(HEADS, P, P)], 2)
    d["out_norm"] = arr("L0_attn_o_norm_w")[:, None]
    for name, layer in (("lstm_a_w", "L0"), ("lstm_b_w", "L1")):
        d[name] = np.concatenate([arr(f"{layer}_cond2_Wx"), arr(f"{layer}_cond2_Wh"),
                                  columns(arr(f"{layer}_cond2_b"))], 1)
    d["router_w"] = np.concatenate([arr("L0_ffn_gate_w").T, arr("L1_ffn_w_router"), arr("L0_ffn_rms_w")[:, None]], 1)
    d["moe_a_w"] = np.concatenate([arr("L0_ffn_W1"), chunked(arr("L0_ffn_W2")), columns(arr("L0_ffn_b1")),
                                   columns(arr("L0_ffn_b2"))], 2)
    d["moe_b_w"] = np.concatenate([arr("L1_ffn_w1"), arr("L1_ffn_w2")], 2)
    d["gru_w"] = np.concatenate([arr(f"L1_cond_{n}").T for n in ("Wxz", "Wxr", "Wxh", "Whz", "Whr", "Whh", "Whq")] +
                                [arr(f"L1_cond_{n}")[:, None] for n in ("bxz", "bxr", "bxh", "bhz", "bhr", "bhh", "bhq")], 1)
    pairs = [arr(f"L1_attn_P_{n}").transpose(1, 0, 2).reshape(D, 8, P).transpose(1, 0, 2) for n in "qkv"]
    d["attn_w"] = np.concatenate([*pairs, arr("L1_attn_P_o").transpose(0, 2, 1).reshape(8, P, D)], 2)
    return {k: np.ascontiguousarray(v) for k, v in d.items()}


def kernel(**inputs):
    import concourse.bacc as bacc
    from concourse.bass_utils import run_bass_kernel_spmd

    arrays = lay_out(inputs)
    nc = bacc.Bacc("TRN2", target_bir_lowering=False, num_devices=1)
    a = {k: nc.dram_tensor(f"in_{k}", v.shape, F32, kind="ExternalInput").ap() for k, v in arrays.items()}
    out = nc.dram_tensor("out", [P, N], F32, kind="ExternalOutput").ap()
    build(nc, a, out)
    r = run_bass_kernel_spmd(nc, [{f"in_{k}": v for k, v in arrays.items()}], core_ids=[0])
    return np.ascontiguousarray(r.results[0]["out"].T).reshape(B, T, D)
```
